# Optimizing a Trainium2 kernel written in Bass

```python
import numpy as np
import jax
import jax.numpy as jnp

def _softmax(x, axis=-1):
    return jax.nn.softmax(x, axis=axis)

def _gelu(x):
    return jax.nn.gelu(x, approximate=True)

def _silu(x):
    return jax.nn.silu(x)

def _sigmoid(x):
    return jax.nn.sigmoid(x)

def _layernorm(x, axis=-1, eps=1e-05):
    m = jnp.mean(x, axis=axis, keepdims=True)
    v = jnp.var(x, axis=axis, keepdims=True)
    return (x - m) / jnp.sqrt(v + eps)

def _scatter_add(tgt, idx, src, axis=0):
    return tgt.at[idx].add(src)

def _segment_sum(src, seg, n):
    return jax.ops.segment_sum(src, seg, n)
kernel_name = 'mk_flamingo_gated_d1_seqx_r2_1efce2'

def setup_inputs(seed: int=0):
    np.random.seed(seed)
    _w = jnp.asarray

    def _rec_inputs():
        import jax
        import jax.numpy as jnp
        _rk = jax.random.key(seed)
        x = 7.22e-05 + 1 * jax.random.normal(jax.random.fold_in(_rk, 1), (16, 100, 512), jnp.float32)
        _lenS = 100 - jax.random.randint(jax.random.fold_in(_rk, 7), (16,), 0, max(1, 100 // 4) + 1, jnp.int32)
        _lenS2 = 722 - jax.random.randint(jax.random.fold_in(_rk, 8), (16,), 0, max(1, 722 // 4) + 1, jnp.int32)
        _ctx_1024P = jax.random.normal(jax.random.fold_in(_rk, 11), (16, 16, 512), jnp.float32)
        _ctx_1024c = jax.random.dirichlet(jax.random.fold_in(_rk, 511), 0.3 * jnp.ones((16,), jnp.float32), (16, 722))
        _ctx_1024t = jnp.einsum('bsk,bkd->bsd', _ctx_1024c, _ctx_1024P)
        _ctx_1024t = _ctx_1024t * jax.lax.rsqrt(jnp.mean(jnp.square(_ctx_1024t)) + 1e-12) * 0.953939
        ctx_1024 = -0.000514642 + 1.00011 * (_ctx_1024t + 0.3 * jax.random.normal(jax.random.fold_in(_rk, 611), (16, 722, 512), jnp.float32))
        _g = jax.random.normal(jax.random.fold_in(_rk, 9001), (2, 1), jnp.float32)
        _g = jnp.sign(_g) * jnp.maximum(jnp.abs(_g), 1.0) + (_g == 0) * 1.0
        g_xattn = _g[0]
        g_ffn = _g[1]
        return (x, ctx_1024, g_xattn, g_ffn)
    x, ctx_1024, g_xattn, g_ffn = _rec_inputs()

    def _L0_xattn_setup():
        import jax, jax.numpy as jnp
        import numpy as np
        B, L_ENC, L_DEC, D = (16, 256, 128, 512)
        key = jax.random.key(seed)
        k1, k2, k3, k4, k5, k6 = jax.random.split(key, 6)
        encoder_hc = jax.random.normal(k1, (B, L_ENC, D), dtype=jnp.float32)
        decoder_hq = jax.random.normal(k2, (B, L_DEC, D), dtype=jnp.float32)
        w_sim = jax.random.normal(k3, (3 * D,), dtype=jnp.float32) * 0.02
        b_sim = jax.random.normal(k4, (1,), dtype=jnp.float32) * 0.02
        W_qv = jax.random.normal(k5, (4 * D, D), dtype=jnp.float32) * 0.02
        b_qv = jax.random.normal(k6, (D,), dtype=jnp.float32) * 0.02
        return {'encoder_hc': encoder_hc, 'decoder_hq': decoder_hq, 'w_sim': w_sim, 'b_sim': b_sim, 'W_qv': W_qv, 'b_qv': b_qv}
    _L0_xattn_all = _L0_xattn_setup()
    _L0_xattn_in = {k: v for k, v in _L0_xattn_all.items() if k in ('w_sim', 'b_sim', 'W_qv', 'b_qv')}
    del _L0_xattn_all

    def _L0_ffn_setup():
        import jax, jax.numpy as jnp
        import numpy as np
        import math
        D = 512
        H = 16
        E = 8
        TOPK = 2
        LAT = D // 2
        KPH = LAT // H
        HD = D // H

        def _forward(hs, q_w, q_b, k_w, k_b, v_w, v_b, o_w, o_b, router_w, router_b, w1, b1, w2, b2):
            B, S, _ = hs.shape
            Q = (hs @ q_w + q_b).reshape(B, S, H, HD).transpose(0, 2, 1, 3)
            K = (hs @ k_w + k_b).reshape(B, S, H, KPH).transpose(0, 2, 1, 3)
            V = (hs @ v_w + v_b).reshape(B, S, H, KPH).transpose(0, 2, 1, 3)
            scores = jnp.einsum('bhsk,bhtk->bhst', Q[..., :KPH], K) / math.sqrt(KPH)
            attn = jax.nn.softmax(scores, axis=-1)
            ao = jnp.einsum('bhst,bhtv->bhsv', attn, V)
            ao = ao.transpose(0, 2, 1, 3).reshape(B, S, H * KPH)
            ao = jnp.concatenate([ao, jnp.zeros((B, S, D - LAT), ao.dtype)], axis=-1)
            mla_out = ao @ o_w + o_b
            probs = jax.nn.softmax(mla_out @ router_w + router_b, axis=-1)
            topw, topi = jax.lax.top_k(probs, TOPK)
            topw = topw / (topw.sum(-1, keepdims=True) + 1e-08)
            combine = jnp.sum(jax.nn.one_hot(topi, E, dtype=probs.dtype) * topw[..., None], axis=-2)
            h1 = jnp.einsum('bsd,edf->ebsf', mla_out, w1) + b1[:, None, None, :]
            h1 = jax.nn.gelu(h1, approximate=False)
            h2 = jnp.einsum('ebsf,efd->ebsd', h1, w2) + b2[:, None, None, :]
            moe_out = jnp.einsum('bse,ebsd->bsd', combine, h2)
            return hs + 0.3 * moe_out
        key = jax.random.key(seed)
        ks = jax.random.split(key, 16)
        s = 0.02
        inp = {'hidden_states': jax.random.normal(ks[0], (2, 1024, D), jnp.float32), 'q_w': jax.random.normal(ks[1], (D, D), jnp.float32) * s, 'q_b': jnp.zeros((D,), jnp.float32), 'k_w': jax.random.normal(ks[2], (D, LAT), jnp.float32) * s, 'k_b': jnp.zeros((LAT,), jnp.float32), 'v_w': jax.random.normal(ks[3], (D, LAT), jnp.float32) * s, 'v_b': jnp.zeros((LAT,), jnp.float32), 'o_w': jax.random.normal(ks[4], (D, D), jnp.float32) * s, 'o_b': jnp.zeros((D,), jnp.float32), 'router_w': jax.random.normal(ks[5], (D, E), jnp.float32) * s, 'router_b': jnp.zeros((E,), jnp.float32), 'w1': jax.random.normal(ks[6], (E, D, 2 * D), jnp.float32) * s, 'b1': jnp.zeros((E, 2 * D), jnp.float32), 'w2': jax.random.normal(ks[7], (E, 2 * D, D), jnp.float32) * s, 'b2': jnp.zeros((E, D), jnp.float32)}
        return inp
    _L0_ffn_all = _L0_ffn_setup()
    _L0_ffn_in = {k: v for k, v in _L0_ffn_all.items() if k in ('q_w', 'q_b', 'k_w', 'k_b', 'v_w', 'v_b', 'o_w', 'o_b', 'router_w', 'router_b', 'w1', 'b1', 'w2', 'b2')}
    del _L0_ffn_all
    return {'x': x, 'ctx_1024': ctx_1024, 'g_xattn': g_xattn, 'g_ffn': g_ffn, 'L0_xattn_w_sim': _L0_xattn_in['w_sim'], 'L0_xattn_b_sim': _L0_xattn_in['b_sim'], 'L0_xattn_W_qv': _L0_xattn_in['W_qv'], 'L0_xattn_b_qv': _L0_xattn_in['b_qv'], 'L0_ffn_q_w': _L0_ffn_in['q_w'], 'L0_ffn_q_b': _L0_ffn_in['q_b'], 'L0_ffn_k_w': _L0_ffn_in['k_w'], 'L0_ffn_k_b': _L0_ffn_in['k_b'], 'L0_ffn_v_w': _L0_ffn_in['v_w'], 'L0_ffn_v_b': _L0_ffn_in['v_b'], 'L0_ffn_o_w': _L0_ffn_in['o_w'], 'L0_ffn_o_b': _L0_ffn_in['o_b'], 'L0_ffn_router_w': _L0_ffn_in['router_w'], 'L0_ffn_router_b': _L0_ffn_in['router_b'], 'L0_ffn_w1': _L0_ffn_in['w1'], 'L0_ffn_b1': _L0_ffn_in['b1'], 'L0_ffn_w2': _L0_ffn_in['w2'], 'L0_ffn_b2': _L0_ffn_in['b2']}

def reference(x, ctx_1024, g_xattn, g_ffn, L0_xattn_w_sim, L0_xattn_b_sim, L0_xattn_W_qv, L0_xattn_b_qv, L0_ffn_q_w, L0_ffn_q_b, L0_ffn_k_w, L0_ffn_k_b, L0_ffn_v_w, L0_ffn_v_b, L0_ffn_o_w, L0_ffn_o_b, L0_ffn_router_w, L0_ffn_router_b, L0_ffn_w1, L0_ffn_b1, L0_ffn_w2, L0_ffn_b2):
    import jax
    import jax.numpy as jnp

    def _L0_xattn_ref(encoder_hc, decoder_hq, w_sim, b_sim, W_qv, b_qv):
        import jax, jax.numpy as jnp
        import numpy as np
        B, L_ENC, L_DEC, D = (16, 256, 128, 512)
        d = encoder_hc.shape[-1]
        w1, w2, w3 = (w_sim[:d], w_sim[d:2 * d], w_sim[2 * d:])
        Sim = (encoder_hc @ w1)[:, :, None] + (decoder_hq @ w2)[:, None, :] + jnp.einsum('bid,bjd->bij', encoder_hc * w3, decoder_hq) + b_sim[0]
        A = jax.nn.softmax(Sim, axis=2)
        hq_hat = jnp.einsum('bij,bjd->bid', A, decoder_hq)
        Batt = jax.nn.softmax(jnp.max(Sim, axis=2), axis=1)
        hc_bar = jnp.einsum('bi,bid->bd', Batt, encoder_hc)[:, None, :]
        hc_hat = jnp.broadcast_to(hc_bar, encoder_hc.shape)
        feats = jnp.concatenate([encoder_hc, hq_hat, encoder_hc * hq_hat, encoder_hc * hc_hat], axis=-1)
        hcq = feats @ W_qv + b_qv
        return hcq

    def _L0_ffn_ref(hidden_states, q_w, q_b, k_w, k_b, v_w, v_b, o_w, o_b, router_w, router_b, w1, b1, w2, b2):
        import jax, jax.numpy as jnp
        import numpy as np
        import math
        D = 512
        H = 16
        E = 8
        TOPK = 2
        LAT = D // 2
        KPH = LAT // H
        HD = D // H

        def _forward(hs, q_w, q_b, k_w, k_b, v_w, v_b, o_w, o_b, router_w, router_b, w1, b1, w2, b2):
            B, S, _ = hs.shape
            Q = (hs @ q_w + q_b).reshape(B, S, H, HD).transpose(0, 2, 1, 3)
            K = (hs @ k_w + k_b).reshape(B, S, H, KPH).transpose(0, 2, 1, 3)
            V = (hs @ v_w + v_b).reshape(B, S, H, KPH).transpose(0, 2, 1, 3)
            scores = jnp.einsum('bhsk,bhtk->bhst', Q[..., :KPH], K) / math.sqrt(KPH)
            attn = jax.nn.softmax(scores, axis=-1)
            ao = jnp.einsum('bhst,bhtv->bhsv', attn, V)
            ao = ao.transpose(0, 2, 1, 3).reshape(B, S, H * KPH)
            ao = jnp.concatenate([ao, jnp.zeros((B, S, D - LAT), ao.dtype)], axis=-1)
            mla_out = ao @ o_w + o_b
            probs = jax.nn.softmax(mla_out @ router_w + router_b, axis=-1)
            topw, topi = jax.lax.top_k(probs, TOPK)
            topw = topw / (topw.sum(-1, keepdims=True) + 1e-08)
            combine = jnp.sum(jax.nn.one_hot(topi, E, dtype=probs.dtype) * topw[..., None], axis=-2)
            h1 = jnp.einsum('bsd,edf->ebsf', mla_out, w1) + b1[:, None, None, :]
            h1 = jax.nn.gelu(h1, approximate=False)
            h2 = jnp.einsum('ebsf,efd->ebsd', h1, w2) + b2[:, None, None, :]
            moe_out = jnp.einsum('bse,ebsd->bsd', combine, h2)
            return hs + 0.3 * moe_out
        return _forward(hidden_states, q_w, q_b, k_w, k_b, v_w, v_b, o_w, o_b, router_w, router_b, w1, b1, w2, b2)
    x = x + jnp.tanh(g_xattn[0]) * _L0_xattn_ref(_layernorm(x, axis=-1), ctx_1024, L0_xattn_w_sim, L0_xattn_b_sim, L0_xattn_W_qv, L0_xattn_b_qv)
    x = x + jnp.tanh(g_ffn[0]) * _L0_ffn_ref(_layernorm(x, axis=-1), L0_ffn_q_w, L0_ffn_q_b, L0_ffn_k_w, L0_ffn_k_b, L0_ffn_v_w, L0_ffn_v_b, L0_ffn_o_w, L0_ffn_o_b, L0_ffn_router_w, L0_ffn_router_b, L0_ffn_w1, L0_ffn_b1, L0_ffn_w2, L0_ffn_b2)
    return x

_drawn_inputs = setup_inputs


def setup_inputs(seed=0):
    import zlib

    import numpy as np

    out = dict(_drawn_inputs(seed))
    spreads = {'L0_ffn_q_b': (0.0, 0.8),
     'L0_ffn_k_b': (0.0, 0.8),
     'L0_ffn_v_b': (0.0, 0.1),
     'L0_ffn_o_b': (0.0, 0.1),
     'L0_ffn_router_b': (0.0, 0.1),
     'L0_ffn_b1': (0.0, 0.1),
     'L0_ffn_b2': (0.0, 0.1)}
    factors = {'L0_xattn_b_qv': 3.996, 'L0_ffn_q_w': 8.0, 'L0_ffn_k_w': 8.0, 'L0_ffn_w1': 2.874}
    for name, (base, spread) in spreads.items():
        noise = np.random.default_rng([zlib.crc32(name.encode()), seed]).standard_normal(out[name].shape)
        drawn = base * np.exp(spread * noise) if base else spread * noise
        out[name] = jnp.asarray(drawn.astype(out[name].dtype))
    for name, factor in factors.items():
        out[name] = (out[name] * factor).astype(out[name].dtype)
    return out
```

```python
from contextlib import ExitStack

import numpy as np

import concourse.bass as bass
from concourse import mybir

F32 = mybir.dt.float32
F32R = mybir.dt.float32r
U32 = mybir.dt.uint32
ALU = mybir.AluOpType
ACT = mybir.ActivationFunctionType
AX = mybir.AxisListType

P = 128
B, S, D = 16, 100, 512
C = 722
KC = D // P
JC = -(-C // P)
JREST = C - (JC - 1) * P
NF = 4 * KC
H, KPH = 16, 16
LAT = H * KPH
HB = P // KPH
NB = LAT // P
HD = D // H
E, FF = 8, 2 * D
FC = FF // P
EPS = 1e-5
QB = 2
QT = QB * S
NQ = B // QB


def chunk_rows(j):
    return P if j < JC - 1 else JREST


def apart(eng, done):
    eng.wait_ge(done, 1)


def over_batches(eng, step):
    step(0, 0)
    step(1, 1)
    with eng.Fori(1, B // 2 - 1) as i:
        step(2 * i, 0)
        step(2 * i + 1, 1)
    step(B - 2, 0)
    step(B - 1, 1)


def over_attend_steps(eng, step):
    step(0, True, False, True)
    step(1, True, True, True)
    with eng.Fori(1, B // 2 - 1) as i:
        step(2 * i, True, True, True)
        step(2 * i + 1, True, True, True)
    step(B - 2, True, True, True)
    step(B - 1, True, True, False)
    step(B, False, True, False)


def build(nc, x, ctx_1024, g_xattn, g_ffn, w_sim, b_sim, W_qv, b_qv, q_w, q_b, k_w, k_b, v_w, v_b, o_w, o_b,
          router_w, router_b, w1, b1, w2, b2, out):
    stack = ExitStack()
    with stack:
        base = -(-nc.sbuf_base // 32) * 32
        cursor = [base]

        def place(name, shape, dt=F32):
            size = int(np.prod(shape[1:])) * 4
            t = nc.alloc_sbuf_tensor_at(name, shape, dt, offset=cursor[0])
            cursor[0] += -(-size // 32) * 32
            return t

        def sem(name):
            return stack.enter_context(nc.semaphore(name))

        ident = place("ident", [P, P])
        ones = place("ones", [P, P])
        head_mask = place("head_mask", [P, HB])
        iota_e = place("iota_e", [P, E])
        w2T = place("w2T", [P, KC])
        w3T = place("w3T", [P, KC])
        b_sim_b = place("b_sim_b", [P, 1])
        g_b = place("g_b", [P, 2])
        tg = place("tg", [P, 2])
        tg_moe = place("tg_moe", [P, 1])
        minus_half = place("minus_half", [P, B])
        stats = place("stats", [S, B, 6])
        mv = place("mv", [S, B, 2])
        var_eps = place("var_eps", [S, B])
        rstd = place("rstd", [S, B])
        nmax_all = place("nmax_all", [S, B])
        rowsim_all = place("rowsim_all", [S, B])
        rmax = place("rmax", [S, B])
        pool_max = place("pool_max", [B, 1])
        pool_maxb = place("pool_maxb", [B, S])
        pool_e = place("pool_e", [S, B])
        pool_w = place("pool_w", [S, B])
        psum_row = place("psum_row", [S, 1])
        prob_inv = place("prob_inv", [S, 1])
        qbT = place("qbT", [P, NB])
        kbT = place("kbT", [P, NB])
        b1T = place("b1T", [P, FC, E])
        router_wT = place("router_wT", [P, KC, E])
        router_bb = place("router_bb", [S, E])
        logits = place("logits", [S, B, E])
        b1e = place("b1e", [P, FC])
        comb = place("comb", [S, B, E])
        rt_a = place("rt_a", [S, B, E])
        rt_m = place("rt_m", [S, B])
        top_p = place("top_p", [S, B, E])
        top_i = place("top_i", [S, B, E], U32)
        top_f = place("top_f", [S, B, E])
        hcb = place("hcb", [P, KC])
        x_all = place("x_all", [S, B, D])

        region_a = cursor[0]
        Wh = place("Wh", [P, NF, D], F32R)
        Wl = place("Wl", [P, NF, D], F32R)
        fT = place("fT", [P, B, 2 * KC, S])
        region_s = cursor[0]
        wstage = [place(f"wstage{i}", [P, D]) for i in range(2)]
        region_b = cursor[0]
        ctx = [place(f"ctx{i}", [P, JC, D]) for i in range(2)]
        ctxT = place("ctxT", [P, KC, C])
        hc = place("hc", [S, D])
        aT = place("aT", [P, KC, S])
        prob = place("prob", [S, C])
        probT = place("probT", [P, JC, S])
        w1_b = place("w1_b", [S, D])
        junk = place("junk", [S, D])
        end = cursor[0]
        cursor[0] = region_b
        wqk = place("wqk", [P, KC, 2 * LAT])
        wv = place("wv", [P, KC, LAT])
        fh = [place(f"fh{i}", [P, NF, S], F32R) for i in range(2)]
        fl = [place(f"fl{i}", [P, NF, S], F32R) for i in range(2)]
        prod = place("prod", [P, 2 * KC, S])
        diag = place("diag", [S, S])
        scaled = place("scaled", [P, KC, S])
        b_qv_b = place("b_qv_b", [S, D])
        y_b = place("y_b", [S, D])
        end = max(end, cursor[0])
        cursor[0] = region_s
        wo = place("wo", [P, NB, D])
        cursor[0] = region_a
        hs = place("hs", [S, D])
        hsT = place("hsT", [P, KC, S])
        qT = place("qT", [P, NB, S])
        KTm = place("KTm", [P, NB, HB, S])
        V = place("V", [S, H, KPH + 1])
        att = [place(f"att{i}", [S, HB, S]) for i in range(2)]
        attT = [place(f"attT{i}", [S, HB, S]) for i in range(2)]
        smax = [place(f"smax{i}", [S, HB]) for i in range(2)]
        den = place("den", [S, H])
        ao = place("ao", [S, H, KPH])
        aoT = place("aoT", [P, NB, S])
        mla = place("mla", [S, D])
        mT = place("mT", [P, KC, S])
        v_b_b = place("v_b_b", [S, LAT])
        o_b_b = place("o_b_b", [S, D])
        assert cursor[0] <= region_a + 2 * NF * D * 4
        cursor[0] = region_a + 2 * NF * D * 4
        mTh = place("mTh", [P, KC, B * S], F32R)
        mTl = place("mTl", [P, KC, B * S], F32R)
        assert cursor[0] <= region_s
        cursor[0] = region_a
        w1h = place("w1h", [P, KC, FF], F32R)
        w1l = place("w1l", [P, KC, FF], F32R)
        w2h = place("w2h", [P, FC, D], F32R)
        w2l = place("w2l", [P, FC, D], F32R)
        cursor[0] = region_s
        raw = place("raw", [P, KC * FF])
        h1f = [place(f"h1f{i}", [P, QT]) for i in range(2)]
        h1h = [place(f"h1h{i}", [P, FC, QT], F32R) for i in range(2)]
        h1l = [place(f"h1l{i}", [P, FC, QT], F32R) for i in range(2)]
        b2_b = place("b2_b", [S, D])
        tmp_o = [place(f"tmp_o{i}", [S, D]) for i in range(2)]
        end = max(end, cursor[0])
        assert end <= nc.sbuf_usable_end, (end, nc.sbuf_usable_end)

        bank = [stack.enter_context(nc.psum_tensor(f"bank{i}", [P, 512], F32)) for i in range(6)]
        pair = stack.enter_context(nc.psum_tensor("pair", [P, 2, 512], F32))

        x_loaded = [sem(f"x_loaded{g}") for g in range(4)]
        consts_loaded = sem("consts_loaded")
        ctx_loaded = [sem(f"ctx_loaded{i}") for i in range(2)]
        wstage_loaded = [sem(f"wstage_loaded{i}") for i in range(2)]
        attw_loaded = sem("attw_loaded")
        attb_loaded = sem("attb_loaded")
        bqv_loaded = sem("bqv_loaded")
        out_stored = sem("out_stored")
        pool_const = sem("pool_const")
        w_split = sem("w_split")
        gate_done = sem("gate_done")
        dve_step = sem("dve_step")
        mv_done = sem("mv_done")
        var_done = sem("var_done")
        rstd_done = sem("rstd_done")
        hc_ready = sem("hc_ready")
        rowsim_done = sem("rowsim_done")
        hcT_ps = sem("hcT_ps")
        hcT_sb = sem("hcT_sb")
        aT_ready = sem("aT_ready")
        ctxT_ps = sem("ctxT_ps")
        ctxT_even = sem("ctxT_even")
        ctxT_odd = sem("ctxT_odd")
        sim_done = sem("sim_done")
        max_done = sem("max_done")
        exp_done = sem("exp_done")
        inv_done = sem("inv_done")
        prob_done = sem("prob_done")
        probT_ps = sem("probT_ps")
        probT_sb = sem("probT_sb")
        hq_ps = sem("hq_ps")
        hq_sb = sem("hq_sb")
        pool_a = sem("pool_a")
        pool_b = sem("pool_b")
        pool_c = sem("pool_c")
        pool_exp = sem("pool_exp")
        pool_d = sem("pool_d")
        diag_done = sem("diag_done")
        eb_done = sem("eb_done")
        scaled_done = sem("scaled_done")
        hcb_done = sem("hcb_done")
        prod1_done = sem("prod1_done")
        prod_done = sem("prod_done")
        fh_lowhalf = sem("fh_lowhalf")
        fh_highhalf = sem("fh_highhalf")
        fl_lowhalf = sem("fl_lowhalf")
        fl_highhalf = sem("fl_highhalf")
        y_done = sem("y_done")
        y_biased = sem("y_biased")
        x1_done = sem("x1_done")
        stats2_done = sem("stats2_done")
        hs_ready = sem("hs_ready")
        hsT_ps = sem("hsT_ps")
        hsT_sb = sem("hsT_sb")
        qk_ps = sem("qk_ps")
        q_sb = sem("q_sb")
        k_sb = sem("k_sb")
        v_ps = sem("v_ps")
        v_sb = sem("v_sb")
        sc_ps = sem("sc_ps")
        smax_done = sem("smax_done")
        sub_done = sem("sub_done")
        att_exp = sem("att_exp")
        attT_ps = sem("attT_ps")
        attT_sb = sem("attT_sb")
        av_ps = sem("av_ps")
        den_done = sem("den_done")
        ao_sb = sem("ao_sb")
        aoT_ps = sem("aoT_ps")
        aoT_sb = sem("aoT_sb")
        mla_ps = sem("mla_ps")
        mla_sb = sem("mla_sb")
        mT_ps = sem("mT_ps")
        mT_sb = sem("mT_sb")
        mTh_sb = sem("mTh_sb")
        mTl_sb = sem("mTl_sb")
        lg_ps = sem("lg_ps")
        lg_sb = sem("lg_sb")
        base_done = sem("base_done")
        route_sub = sem("route_sub")
        route_exp = sem("route_exp")
        route_done = sem("route_done")
        raw1_loaded = sem("raw1_loaded")
        raw2_loaded = sem("raw2_loaded")
        b1e_done = sem("b1e_done")
        b2_loaded = sem("b2_loaded")
        w1h_done = sem("w1h_done")
        w1l_done = sem("w1l_done")
        w2h_done = sem("w2h_done")
        w2l_done = sem("w2l_done")
        h_ps = sem("h_ps")
        gelu_done = sem("gelu_done")
        h1h_done = sem("h1h_done")
        h1f_free = sem("h1f_free")
        pool_ps = sem("pool_ps")
        o_ps = sem("o_ps")
        o_free = sem("o_free")
        o_added = sem("o_added")

        block = stack.enter_context(nc.Block())

        x_v = x.rearrange("b s d -> s b d")
        out_v = out.rearrange("b s d -> s b d")
        W_v = W_qv.rearrange("(c p) n -> c p n", p=P)
        q_used = q_w.rearrange("(c p) (h t k) -> c t p h k", p=P, t=HD // KPH, k=KPH)
        N_CONSTS = 6 + 3 + E + H
        N_ATTW = 3 * KC + 1

        @block.sync
        def _(sp):
            with nc.allow_non_contiguous_dma(reason="short vectors laid over partitions"):
                for g in range(4):
                    sp.dma_start(x_all[:, 4 * g:4 * g + 4, :], x_v[:, 4 * g:4 * g + 4, :]).then_inc(x_loaded[g], 16)
                n = 0

                def const(dst, src):
                    nonlocal n
                    n += 1
                    sp.dma_start(dst, src).then_inc(consts_loaded, 16)

                const(w1_b[:, :], w_sim[0:D].partition_broadcast(S))
                const(w2T[:, :], w_sim[D:2 * D].rearrange("(c p) -> p c", p=P))
                const(w3T[:, :], w_sim[2 * D:3 * D].rearrange("(c p) -> p c", p=P))
                const(b_sim_b[:, :], b_sim.partition_broadcast(P))
                const(g_b[:, 0:1], g_xattn.partition_broadcast(P))
                const(g_b[:, 1:2], g_ffn.partition_broadcast(P))

                def load_ctx(b, p):
                    if not (isinstance(b, int) and b < 2):
                        sp.wait_ge(hq_ps, b - 1)
                    full = (JC - 1) * P
                    even = JREST - JREST % 16
                    sp.dma_start(ctx[p][:, 0:JC - 1, :], ctx_1024[b, 0:full, :].rearrange("(c p) n -> p c n", p=P)) \
                        .then_inc(ctx_loaded[p], 16)
                    sp.dma_start(ctx[p][0:even, JC - 1, :], ctx_1024[b, full:full + even, :]) \
                        .then_inc(ctx_loaded[p], 16)
                    sp.dma_start(ctx[p][even:JREST, JC - 1, :], ctx_1024[b, full + even:C, :]) \
                        .then_inc(ctx_loaded[p], 16)

                load_ctx(0, 0)
                load_ctx(1, 1)
                const(router_wT[:, :, :], router_w.rearrange("(c p) e -> p c e", p=P))
                const(router_bb[:, :], router_b.partition_broadcast(S))
                const(kbT[:, :], k_b.rearrange("(g p) -> p g", p=P))
                for e in range(E):
                    const(b1T[:, :, e], b1[e].rearrange("(f p) -> p f", p=P))
                for h in range(H):
                    r = (h % HB) * KPH
                    const(qbT[r:r + KPH, h // HB:h // HB + 1], q_b[h * HD:h * HD + KPH].rearrange("(k o) -> k o", o=1))
                assert n == N_CONSTS
                with sp.Fori(1, B // 2 - 1) as i:
                    load_ctx(2 * i, 0)
                    load_ctx(2 * i + 1, 1)
                load_ctx(B - 2, 0)
                load_ctx(B - 1, 1)
                sp.wait_ge(hq_ps, B)
                sp.wait_ge(probT_sb, 2 * B)
                sp.wait_ge(pool_d, 1)
                sp.dma_start(b_qv_b[:, :], b_qv.partition_broadcast(S)).then_inc(bqv_loaded, 16)
                for c in range(KC):
                    sp.dma_start(wqk[:, c, 0:LAT].rearrange("p (h k) -> p h k", k=KPH), q_used[c, 0]) \
                        .then_inc(attw_loaded, 16)
                    sp.dma_start(wqk[:, c, LAT:2 * LAT], k_w[c * P:(c + 1) * P, :]).then_inc(attw_loaded, 16)
                    sp.dma_start(wv[:, c, :], v_w[c * P:(c + 1) * P, :]).then_inc(attw_loaded, 16)
                sp.wait_ge(w_split, 2 * NF)
                sp.dma_start(wo[:, :, :], o_w[0:LAT, :].rearrange("(g p) n -> p g n", p=P)).then_inc(attw_loaded, 16)
                sp.wait_ge(y_done, B)
                sp.dma_start(v_b_b[:, :], v_b.partition_broadcast(S)).then_inc(attb_loaded, 16)
                sp.dma_start(o_b_b[:, :], o_b.partition_broadcast(S)).then_inc(attb_loaded, 16)
                sp.wait_ge(lg_sb, B)
                sp.wait_ge(mTl_sb, B)
                with sp.Fori(0, E) as e:
                    sp.wait_ge(w2l_done, e * KC + 1)
                    sp.dma_start(raw[:, :].rearrange("p (c n) -> p c n", c=KC),
                                 w1[e].rearrange("(c p) n -> p c n", p=P)).then_inc(raw1_loaded, 16)
                    sp.wait_ge(o_added, e * B + 1)
                    sp.dma_start(b2_b[:, :], b2[e].partition_broadcast(S)).then_inc(b2_loaded, 16)
                    sp.wait_ge(w1l_done, (e + 1) * KC)
                    sp.dma_start(raw[:, :].rearrange("p (c n) -> p c n", c=FC),
                                 w2[e].rearrange("(c p) n -> p c n", p=P)).then_inc(raw2_loaded, 16)
                for g in range(4):
                    sp.wait_ge(o_added, (E - 1) * B + 4 * (g + 1) + 1)
                    sp.dma_start(out_v[:, 4 * g:4 * g + 4, :], x_all[:, 4 * g:4 * g + 4, :]).then_inc(out_stored, 16)
                sp.wait_ge(out_stored, 64)


        @block.gpsimd
        def _(pool):
            n = 0

            def own(ins):
                nonlocal n
                n += 1
                ins.then_inc(pool_const, 1)
                pool.wait_ge(pool_const, n)

            own(pool.memset(ident[:, :], 0.0))
            own(pool.affine_select(out=ident[:, :], in_=ident[:, :], compare_op=ALU.not_equal, fill=1.0, base=0,
                                   pattern=[[-1, P]], channel_multiplier=1))
            own(pool.memset(ones[:, :], 1.0))
            own(pool.memset(minus_half[:, :], -0.5))
            own(pool.memset(head_mask[:, :], 1.0))
            own(pool.affine_select(out=head_mask[:, :], in_=head_mask[:, :], compare_op=ALU.is_ge, fill=0.0, base=0,
                                   pattern=[[-KPH, HB]], channel_multiplier=1))
            own(pool.affine_select(out=head_mask[:, :], in_=head_mask[:, :], compare_op=ALU.is_ge, fill=0.0,
                                   base=KPH - 1, pattern=[[KPH, HB]], channel_multiplier=-1))
            own(pool.iota(iota_e[:, :], pattern=[[1, E]], base=0, channel_multiplier=0,
                          allow_small_or_imprecise_dtypes=True))
            pool.wait_ge(var_done, 1)
            pool.tensor_tensor(rstd[:, :], var_eps[:, :], minus_half[0:S, :], ALU.pow).then_inc(rstd_done, 1)
            with pool.Fori(0, NF // 2) as m:
                k = 2 * m
                for i in range(2):
                    pool.dma_start(wstage[i][:, :], W_v[k + i]).then_inc(wstage_loaded[i], 16)
                for i in range(2):
                    pool.wait_ge(wstage_loaded[i], k * 8 + 16)
                    pool.tensor_copy(Wh[:, k + i, :], wstage[i][:, :]).then_inc(w_split, 1)
                    pool.wait_ge(w_split, k * 2 + 2 * i + 1)
                    pool.tensor_tensor(Wl[:, k + i, :], wstage[i][:, :], Wh[:, k + i, :].bitcast(F32), ALU.subtract) \
                        .then_inc(w_split, 1)
                pool.wait_ge(w_split, k * 2 + 4)
            pool.wait_ge(var_done, 2)
            pool.tensor_tensor(rstd[:, :], var_eps[:, :], minus_half[0:S, :], ALU.pow).then_inc(rstd_done, 1)

        NPOOL = 8

        @block.scalar
        def _(act):
            act.wait_ge(consts_loaded, N_CONSTS * 16)
            act.preload_act_table(ACT.Exp)
            act.activation(tg[:, :], g_b[:, :], ACT.Tanh).then_inc(gate_done, 1)

            def evac_ctxT(nb):
                for j in range(0, JC, 2):
                    act.wait_ge(ctxT_ps, nb * JC + j + 1)
                    r = chunk_rows(j)
                    act.activation(ctxT[:, :, j * P:j * P + r], bank[1][:, :].rearrange("p (c n) -> p c n", c=KC)[:, :, 0:r],
                                   ACT.Copy).then_inc(ctxT_even, 1)

            evac_ctxT(0)

            def cross(b, p):
                apart(act, pool_const)
                act.wait_ge(max_done, b + 1)
                act.wait_ge(probT_ps, 2 * b)
                act.activation(prob[:, :].rearrange("s (u n) -> s u n", u=2), pair[0:S, :, 0:C // 2], ACT.Exp,
                               bias=nmax_all[:, bass.ds(b, 1)],
                               accum_out=psum_row[:, :]).then_inc(exp_done, 1)
                if not (isinstance(b, int) and b == B - 1):
                    evac_ctxT(b + 1)
                for u in range(2):
                    act.wait_ge(probT_ps, 2 * b + u + 1)
                    act.wait_ge(hq_ps, b)
                    act.activation(probT[:, 3 * u:3 * u + 2, :],
                                   bank[3 + u][:, 0:2 * S].rearrange("p (c s) -> p c s", c=2), ACT.Copy)
                    r = chunk_rows(3 * u + 2)
                    act.activation(probT[0:r, 3 * u + 2, :], bank[3 + u][0:r, 2 * S:3 * S], ACT.Copy) \
                        .then_inc(probT_sb, 1)
                apart(act, pool_const)
                act.wait_ge(hq_ps, b + 1)
                act.activation(fT[:, b, KC:2 * KC, :], bank[5][:, 0:KC * S].rearrange("p (c s) -> p c s", c=KC),
                               ACT.Copy).then_inc(hq_sb, 1)

            over_batches(act, cross)

            act.wait_ge(pool_c, 1)
            act.activation(pool_e[:, :], pool_e[:, :], ACT.Exp).then_inc(pool_exp, 1)

            def round_features(nb, q):
                if not (isinstance(nb, int) and nb < 2):
                    act.wait_ge(y_done, nb - 1)
                apart(act, pool_const)
                act.wait_ge(hq_sb, nb + 1)
                act.activation(fh[q][:, 0:2 * KC, :], fT[:, nb, :, :], ACT.Copy).then_inc(fh_lowhalf, 1)
                act.wait_ge(prod_done, nb + 1)
                act.activation(fh[q][:, 2 * KC:NF, :], prod[:, :, :], ACT.Copy).then_inc(fh_highhalf, 1)

            act.wait_ge(pool_d, 1)
            round_features(0, 0)

            def project(b, p):
                if not (isinstance(b, int) and b == B - 1):
                    round_features(b + 1, 1 - p)

            over_batches(act, project)

            def attend(t, cur, prev, ahead):
                if cur:
                    act.wait_ge(hsT_ps, t + 1)
                    act.activation(hsT[:, :, :], bank[4][:, 0:KC * S].rearrange("p (c s) -> p c s", c=KC), ACT.Copy) \
                        .then_inc(hsT_sb, 1)
                if prev:
                    act.wait_ge(attT_ps, 2 * t)
                    act.activation(attT[1][:, :, :].rearrange("s (u h) n -> s u h n", u=2),
                                   pair[0:S, :, 0:4 * S].rearrange("s u (h n) -> s u h n", h=4), ACT.Copy) \
                        .then_inc(attT_sb, 1)
                    act.wait_ge(aoT_ps, t)
                    act.activation(aoT[:, :, :], bank[5][:, 0:NB * S].rearrange("p (g s) -> p g s", g=NB), ACT.Copy) \
                        .then_inc(aoT_sb, 1)
                if cur:
                    for u in range(2):
                        act.wait_ge(sub_done, 2 * t + u + 1)
                        act.activation(att[u][:, :, :], att[u][:, :, :], ACT.Exp, scale=float(KPH) ** -0.5) \
                            .then_inc(att_exp, 1)
                if prev:
                    act.wait_ge(mT_ps, t)
                    act.activation(mT[:, :, :], bank[4][:, 0:KC * S].rearrange("p (c s) -> p c s", c=KC), ACT.Copy) \
                        .then_inc(mT_sb, 1)
                    act.activation(mTh[:, :, bass.ds((t - 1) * S, S)],
                                   bank[4][:, 0:KC * S].rearrange("p (c s) -> p c s", c=KC), ACT.Copy) \
                        .then_inc(mTh_sb, 1)
                if cur:
                    act.wait_ge(attT_ps, 2 * t + 1)
                    act.activation(attT[0][:, :, :].rearrange("s (u h) n -> s u h n", u=2),
                                   pair[0:S, :, 0:4 * S].rearrange("s u (h n) -> s u h n", h=4), ACT.Copy) \
                        .then_inc(attT_sb, 1)

            over_attend_steps(act, attend)

            act.wait_ge(route_sub, 1)
            act.activation(rt_a[:, :, :], rt_a[:, :, :], ACT.Exp).then_inc(route_exp, 1)
            act.preload_act_table(ACT.Gelu)
            act.sem_inc(gelu_done, 2)

            with act.Fori(0, E) as e:
                act.wait_ge(raw1_loaded, e * 16 + 16)
                act.wait_ge(h_ps, e * NQ * FC + 1)
                for c in range(KC):
                    act.activation(w1h[:, c, :], raw[:, c * FF:(c + 1) * FF], ACT.Copy).then_inc(w1h_done, 1)
                act.wait_ge(raw2_loaded, e * 16 + 16)
                act.wait_ge(o_ps, e * B + 1)
                for c in range(KC):
                    act.activation(w2h[:, 2 * c:2 * c + 2, :],
                                   raw[:, c * FF:(c + 1) * FF].rearrange("p (u n) -> p u n", u=2), ACT.Copy) \
                        .then_inc(w2h_done, 1)
                act.wait_ge(gelu_done, e * NQ * FC + 2)
                act.activation(b1e[:, :], b1T[:, :, e], ACT.Copy).then_inc(b1e_done, 1)
                act.wait_ge(b1e_done, e + 1)
                for q in range(NQ):
                    act.wait_ge(o_ps, (e * NQ + max(q - 1, 0)) * QB + 1)
                    for f in range(FC):
                        n = (e * NQ + q) * FC + f
                        act.wait_ge(h_ps, n + 2)
                        act.wait_ge(h1f_free, n + 1)
                        act.activation(h1f[f % 2][:, :], bank[f % 2][:, 0:QT], ACT.Gelu,
                                       bias=b1e[:, f:f + 1]).then_inc(gelu_done, 1)
                        act.wait_ge(gelu_done, n + 3)
                        act.activation(h1h[q % 2][:, f, :], h1f[f % 2][:, :], ACT.Copy).then_inc(h1h_done, 1)

        @block.tensor
        def _(pe):
            pe.wait_ge(pool_const, NPOOL)

            def transpose_next(nb, p):
                pe.wait_ge(hc_ready, nb + 1)
                pe.wait_ge(aT_ready, nb)
                for c in range(KC):
                    t = nc.tensor.transpose(bank[0][:, c * S:(c + 1) * S], hc[:, c * P:(c + 1) * P], ident[0:S, 0:S])
                t.then_inc(hcT_ps, 1)
                pe.wait_ge(ctx_loaded[p], (nb - p) * 24 + 48)
                for j in range(JC):
                    r = chunk_rows(j)
                    pe.wait_ge(ctxT_odd if j % 2 else ctxT_even, nb * (JC // 2) + j // 2)
                    for c in range(KC):
                        t = nc.tensor.transpose(bank[1 + j % 2][:, c * P:c * P + r], ctx[p][0:r, j, c * P:(c + 1) * P],
                                                ident[0:r, 0:r])
                    t.then_inc(ctxT_ps, 1)

            transpose_next(0, 0)

            def cross(b, p):
                pe.wait_ge(aT_ready, b + 1)
                pe.wait_ge(ctxT_even, (b + 1) * (JC // 2))
                pe.wait_ge(ctxT_odd, (b + 1) * (JC // 2))
                pe.wait_ge(exp_done, b)
                for u in range(2):
                    for c in range(KC):
                        t = nc.tensor.matmul(pair[0:S, u, 0:C // 2], aT[:, c, :], ctxT[:, c, u * (C // 2):(u + 1) * (C // 2)],
                                             start=(c == 0), stop=(c == KC - 1))
                t.then_inc(sim_done, 1)
                if not (isinstance(b, int) and b == B - 1):
                    transpose_next(b + 1, 1 - p)
                pe.wait_ge(prob_done, b + 1)
                for u in range(2):
                    pe.wait_ge(probT_sb, 2 * b)
                    for i in range(3):
                        j = 3 * u + i
                        r = chunk_rows(j)
                        t = nc.tensor.transpose(bank[3 + u][0:r, i * S:(i + 1) * S], prob[:, j * P:j * P + r],
                                                ident[0:S, 0:S])
                    t.then_inc(probT_ps, 1)
                pe.wait_ge(probT_sb, 2 * b + 2)
                pe.wait_ge(hq_sb, b)
                for c in range(KC):
                    for j in range(JC):
                        r = chunk_rows(j)
                        t = nc.tensor.matmul(bank[5][:, c * S:(c + 1) * S], ctx[p][0:r, j, c * P:(c + 1) * P],
                                             probT[0:r, j, :], start=(j == 0), stop=(j == JC - 1))
                t.then_inc(hq_ps, 1)

            over_batches(pe, cross)

            pe.wait_ge(pool_a, 1)
            nc.tensor.transpose(bank[0][0:B, 0:S], rmax[:, :], ident[0:S, 0:S]).then_inc(pool_ps, 1)
            pe.wait_ge(pool_b, 1)
            nc.tensor.transpose(bank[0][0:S, 0:B], pool_maxb[:, :], ident[0:B, 0:B]).then_inc(pool_ps, 1)
            pe.wait_ge(pool_exp, 1)
            nc.tensor.matmul(bank[0][:, 0:B], ones[0:S, :], pool_e[:, :], start=True, stop=True).then_inc(pool_ps, 1)

            def weights_of(nb):
                pe.wait_ge(diag_done, nb + 1)
                nc.tensor.matmul(bank[2][:, 0:S], ones[0:S, :], diag[:, :], start=True, stop=True).then_inc(eb_done, 1)

            weights_of(0)

            def project(b, p):
                pe.wait_ge(w_split, 2 * NF)
                pe.wait_ge(fh_highhalf, b + 1)
                pe.wait_ge(fl_highhalf, b + 1)
                pe.wait_ge(y_biased, b)
                for k in range(NF):
                    if k == NF // 2 and not (isinstance(b, int) and b == B - 1):
                        weights_of(b + 1)
                    nc.tensor.matmul(bank[0][0:S, :], fl[p][:, k, :], Wh[:, k, :], start=(k == 0), stop=False)
                    nc.tensor.matmul(bank[0][0:S, :], fh[p][:, k, :], Wl[:, k, :], start=False, stop=False)
                    t = nc.tensor.matmul(bank[0][0:S, :], fh[p][:, k, :], Wh[:, k, :], start=False, stop=(k == NF - 1))
                t.then_inc(y_done, 1)

            over_batches(pe, project)

            X, Y = bank[4], bank[5]

            def att_transposes(u, count):
                for h in range(HB):
                    t = nc.tensor.transpose(pair[0:S, h // 4, (h % 4) * S:(h % 4 + 1) * S], att[u][:, h, :],
                                            ident[0:S, 0:S])
                t.then_inc(attT_ps, 1)

            def scores(t, u):
                pe.wait_ge(q_sb, t + 1)
                pe.wait_ge(k_sb, 2 * t + u + 1)
                pe.wait_ge(sub_done, 2 * t - 1 + u if not (isinstance(t, int) and t == 0) else 0)
                for i in range(2):
                    m = nc.tensor.matmul(bank[2 * u + i][0:S, 0:4 * S], qT[:, u, :],
                                         KTm[:, u, 4 * i:4 * i + 4, :].rearrange("p h s -> p (h s)"),
                                         start=True, stop=True)
                m.then_inc(sc_ps, 1)

            def attend(t, cur, prev, ahead):
                if cur:
                    pe.wait_ge(hs_ready, t + 1)
                    if prev:
                        pe.wait_ge(mTh_sb, t - 1)
                    for c in range(KC):
                        m = nc.tensor.transpose(X[:, c * S:(c + 1) * S], hs[:, c * P:(c + 1) * P], ident[0:S, 0:S])
                    m.then_inc(hsT_ps, 1)
                if prev:
                    pe.wait_ge(att_exp, 2 * t)
                    pe.wait_ge(attT_sb, 2 * t - 1)
                    att_transposes(1, t)
                    pe.wait_ge(attT_sb, 2 * t)
                    pe.wait_ge(v_sb, t)
                    pe.wait_ge(lg_sb, t - 1)
                    for h in range(H):
                        m = nc.tensor.matmul(Y[0:S, h * (KPH + 1):(h + 1) * (KPH + 1)], attT[h // HB][:, h % HB, :],
                                             V[:, h, :], start=True, stop=True)
                    m.then_inc(av_ps, 1)
                if cur:
                    pe.wait_ge(attw_loaded, N_ATTW * 16)
                    pe.wait_ge(hsT_sb, t + 1)
                    for g in range(2 * NB):
                        for c in range(KC):
                            m = nc.tensor.matmul(X[:, g * S:(g + 1) * S], wqk[:, c, g * P:(g + 1) * P], hsT[:, c, :],
                                                 start=(c == 0), stop=(c == KC - 1))
                    m.then_inc(qk_ps, 1)
                    pe.wait_ge(ao_sb, t)
                    for c in range(KC):
                        m = nc.tensor.matmul(Y[0:S, 0:LAT], hsT[:, c, :], wv[:, c, :], start=(c == 0), stop=(c == KC - 1))
                    m.then_inc(v_ps, 1)
                if prev:
                    pe.wait_ge(ao_sb, t)
                    if cur:
                        pe.wait_ge(v_sb, t + 1)
                    for g in range(NB):
                        m = nc.tensor.transpose(Y[:, g * S:(g + 1) * S],
                                                ao[:, g * HB:(g + 1) * HB, :].rearrange("s h k -> s (h k)"),
                                                ident[0:S, 0:S])
                    m.then_inc(aoT_ps, 1)
                if cur:
                    scores(t, 0)
                if prev:
                    pe.wait_ge(aoT_sb, t)
                    for g in range(NB):
                        m = nc.tensor.matmul(Y[0:S, :], aoT[:, g, :], wo[:, g, :], start=(g == 0), stop=(g == NB - 1))
                    m.then_inc(mla_ps, 1)
                if cur:
                    scores(t, 1)
                if prev:
                    pe.wait_ge(mla_sb, t)
                    for c in range(KC):
                        m = nc.tensor.transpose(X[:, c * S:(c + 1) * S], mla[:, c * P:(c + 1) * P], ident[0:S, 0:S])
                    m.then_inc(mT_ps, 1)
                if cur:
                    pe.wait_ge(att_exp, 2 * t + 1)
                    pe.wait_ge(attT_sb, 2 * t)
                    att_transposes(0, t)
                if prev:
                    pe.wait_ge(mT_sb, t)
                    for c in range(KC):
                        m = nc.tensor.matmul(Y[0:S, 0:E], mT[:, c, :], router_wT[:, c, :], start=(c == 0),
                                             stop=(c == KC - 1))
                    m.then_inc(lg_ps, 1)

            over_attend_steps(pe, attend)

            def inner(e, q):
                pe.wait_ge(mTl_sb, B)
                for f in range(FC):
                    pe.wait_ge(gelu_done, (e * NQ + q) * FC + f + 1)
                    tok = bass.ds(q * QT, QT) if not isinstance(q, int) else slice(q * QT, (q + 1) * QT)
                    for c in range(KC):
                        wh, wl = (w[:, c, f * P:(f + 1) * P] for w in (w1h, w1l))
                        nc.tensor.matmul(bank[f % 2][:, 0:QT], wl, mTh[:, c, tok], start=(c == 0), stop=False)
                        nc.tensor.matmul(bank[f % 2][:, 0:QT], wh, mTl[:, c, tok], start=False, stop=False)
                        m = nc.tensor.matmul(bank[f % 2][:, 0:QT], wh, mTh[:, c, tok], start=False, stop=(c == KC - 1))
                    m.then_inc(h_ps, 1)

            def outer(e, q):
                p = q % 2
                pe.wait_ge(h1h_done, (e * NQ + q + 1) * FC)
                pe.wait_ge(h1f_free, (e * NQ + q + 1) * FC + 2)
                for i in range(QB):
                    pe.wait_ge(o_free, (e * NQ + q) * QB + i + 1)
                    for f in range(FC):
                        hh, hl = (h[p][:, f, i * S:(i + 1) * S] for h in (h1h, h1l))
                        nc.tensor.matmul(bank[2 + i][0:S, :], hl, w2h[:, f, :], start=(f == 0), stop=False)
                        nc.tensor.matmul(bank[2 + i][0:S, :], hh, w2l[:, f, :], start=False, stop=False)
                        m = nc.tensor.matmul(bank[2 + i][0:S, :], hh, w2h[:, f, :], start=False, stop=(f == FC - 1))
                    m.then_inc(o_ps, 1)

            pe.sem_inc(h_ps, 1)
            pe.sem_inc(o_ps, 1)
            with pe.Fori(0, E) as e:
                pe.wait_ge(w1h_done, (e + 1) * KC)
                pe.wait_ge(w1l_done, (e + 1) * KC)
                inner(e, 0)
                for q in range(NQ):
                    if q + 1 < NQ:
                        inner(e, q + 1)
                    if q == 0:
                        pe.wait_ge(w2h_done, (e + 1) * KC)
                        pe.wait_ge(w2l_done, (e + 1) * KC + 1)
                    outer(e, q)

        @block.vector
        def _(dve):
            n = 0

            def own(ins):
                nonlocal n
                n += 1
                ins.then_inc(dve_step, 1)
                dve.wait_ge(dve_step, n)

            def row_stats():
                for b in range(B):
                    ins = dve.bn_aggr(mv[:, b, :], stats[:, b, :])
                own(ins)
                dve.tensor_scalar(var_eps[:, :], mv[:, :, 1], EPS, None, ALU.add).then_inc(var_done, 1)

            for b in range(B):
                if b % 4 == 0:
                    dve.wait_ge(x_loaded[b // 4], 16)
                ins = dve.bn_stats(stats[:, b, :], x_all[:, b, :])
            own(ins)
            row_stats()
            dve.wait_ge(consts_loaded, N_CONSTS * 16)
            dve.wait_ge(rstd_done, 1)

            def normalise(dst, b, done):
                dve.tensor_scalar(dst, x_all[:, b, :], mv[:, b, 0:1], rstd[:, bass.ds(b, 1)], ALU.subtract, ALU.mult) \
                    .then_inc(done, 1)

            def next_hc(nb):
                dve.wait_ge(hcT_ps, nb)
                normalise(hc[:, :], nb, hc_ready)
                dve.wait_ge(hc_ready, nb + 1)
                dve.scalar_tensor_tensor(junk[:, :], hc[:, :], 1.0, w1_b[:, :], ALU.mult, ALU.mult,
                                         accum_out=rowsim_all[:, bass.ds(nb, 1)]).then_inc(rowsim_done, 1)

            def next_aT(nb):
                src = bank[0][:, 0:KC * S].rearrange("p (c s) -> p c s", c=KC)
                apart(dve, pool_const)
                dve.wait_ge(hcT_ps, nb + 1)
                dve.tensor_copy(fT[:, nb, 0:KC, :], src).then_inc(hcT_sb, 1)
                dve.wait_ge(sim_done, nb)
                for c in range(KC):
                    ins = dve.tensor_scalar(aT[:, c, :], src[:, c, :], w3T[:, c:c + 1], w2T[:, c:c + 1], ALU.mult,
                                            ALU.add)
                ins.then_inc(aT_ready, 1)

            def odd_ctxT(nb):
                for j in range(1, JC, 2):
                    dve.wait_ge(ctxT_ps, nb * JC + j + 1)
                    r = chunk_rows(j)
                    dve.tensor_copy(ctxT[:, :, j * P:j * P + r],
                                    bank[2][:, :].rearrange("p (c n) -> p c n", c=KC)[:, :, 0:r]).then_inc(ctxT_odd, 1)

            next_hc(0)
            next_aT(0)
            odd_ctxT(0)

            def cross(b, p):
                last = isinstance(b, int) and b == B - 1
                if not last:
                    next_hc(b + 1)
                apart(dve, pool_const)
                dve.wait_ge(sim_done, b + 1)
                dve.tensor_reduce(nmax_all[:, bass.ds(b, 1)], pair[0:S, :, 0:C // 2], axis=AX.XY, op=ALU.max,
                                  negate=True).then_inc(max_done, 1)
                if not last:
                    next_aT(b + 1)
                dve.wait_ge(exp_done, b + 1)
                dve.reciprocal(prob_inv[:, :], psum_row[:, :]).then_inc(inv_done, 1)
                dve.wait_ge(inv_done, b + 1)
                dve.tensor_scalar(prob[:, :], prob[:, :], prob_inv[:, :], None, ALU.mult).then_inc(prob_done, 1)
                if not last:
                    odd_ctxT(b + 1)

            over_batches(dve, cross)

            own(dve.tensor_tensor(rmax[:, :], rowsim_all[:, :], nmax_all[:, :], ALU.subtract))
            dve.tensor_scalar(rmax[:, :], rmax[:, :], b_sim_b[0:S, :], None, ALU.add).then_inc(pool_a, 1)
            dve.wait_ge(pool_ps, 1)
            own(dve.tensor_reduce(pool_max[:, :], bank[0][0:B, 0:S], axis=AX.X, op=ALU.max))
            dve.tensor_copy(pool_maxb[:, :], pool_max[:, :].to_broadcast([B, S])).then_inc(pool_b, 1)
            dve.wait_ge(pool_ps, 2)
            dve.tensor_tensor(pool_e[:, :], rmax[:, :], bank[0][0:S, 0:B], ALU.subtract).then_inc(pool_c, 1)
            dve.wait_ge(pool_ps, 3)
            own(dve.reciprocal(pool_w[:, :], bank[0][0:S, 0:B]))
            dve.tensor_tensor(pool_w[:, :], pool_w[:, :], pool_e[:, :], ALU.mult).then_inc(pool_d, 1)
            dve.wait_ge(pool_d, 1)

            def diag_of(nb):
                dve.wait_ge(eb_done, nb)
                dve.tensor_scalar(diag[:, :], ident[0:S, 0:S], pool_w[:, bass.ds(nb, 1)], None, ALU.mult) \
                    .then_inc(diag_done, 1)

            def features(nb, q):
                hcT_b, hqT_b = fT[:, nb, 0:KC, :], fT[:, nb, KC:2 * KC, :]
                dve.wait_ge(fh_highhalf, nb)
                dve.wait_ge(fl_highhalf, nb)
                dve.tensor_tensor(prod[:, 0:KC, :], hcT_b, hqT_b, ALU.mult).then_inc(prod1_done, 1)
                dve.wait_ge(eb_done, nb + 1)
                dve.tensor_tensor(scaled[:, :, :], hcT_b, bank[2][:, 0:S].rearrange("p (o s) -> p o s", o=1)
                                  .to_broadcast([P, KC, S]), ALU.mult).then_inc(scaled_done, 1)
                dve.wait_ge(scaled_done, nb + 1)
                dve.tensor_reduce(hcb[:, :], scaled[:, :, :], axis=AX.X, op=ALU.add).then_inc(hcb_done, 1)
                dve.wait_ge(hcb_done, nb + 1)
                dve.tensor_tensor(prod[:, KC:2 * KC, :], hcT_b, hcb[:, :].rearrange("p (c o) -> p c o", o=1)
                                  .to_broadcast([P, KC, S]), ALU.mult).then_inc(prod_done, 1)
                dve.wait_ge(fh_lowhalf, nb + 1)
                dve.tensor_tensor(fl[q][:, 0:2 * KC, :], fT[:, nb, :, :], fh[q][:, 0:2 * KC, :].bitcast(F32),
                                  ALU.subtract).then_inc(fl_lowhalf, 1)
                dve.wait_ge(fh_highhalf, nb + 1)
                dve.tensor_tensor(fl[q][:, 2 * KC:NF, :], prod[:, :, :], fh[q][:, 2 * KC:NF, :].bitcast(F32),
                                  ALU.subtract).then_inc(fl_highhalf, 1)

            dve.wait_ge(hq_sb, B)
            diag_of(0)
            features(0, 0)
            dve.wait_ge(bqv_loaded, 16)
            dve.wait_ge(gate_done, 1)

            def project(b, p):
                if not (isinstance(b, int) and b == B - 1):
                    diag_of(b + 1)
                    features(b + 1, 1 - p)
                dve.wait_ge(y_done, b + 1)
                dve.tensor_tensor(y_b[:, :], bank[0][0:S, :], b_qv_b[:, :], ALU.add).then_inc(y_biased, 1)
                dve.wait_ge(y_biased, b + 1)
                dve.scalar_tensor_tensor(x_all[:, b, :], y_b[:, :], tg[0:S, 0:1], x_all[:, b, :], ALU.mult, ALU.add) \
                    .then_inc(x1_done, 1)
                apart(dve, pool_const)
                dve.wait_ge(x1_done, b + 1)
                dve.bn_stats(stats[:, b, :], x_all[:, b, :]).then_inc(stats2_done, 1)

            over_batches(dve, project)
            dve.wait_ge(stats2_done, B)
            row_stats()
            dve.memset(V[:, :, KPH:KPH + 1], 1.0).then_inc(dve_step, 1)
            n += 1
            dve.wait_ge(attb_loaded, 32)
            dve.wait_ge(rstd_done, 2)
            X, Y = bank[4], bank[5]

            def next_hs(t):
                dve.wait_ge(hsT_ps, t)
                normalise(hs[:, :], t, hs_ready)
                dve.wait_ge(hs_ready, t + 1)
                dve.scalar_tensor_tensor(x_all[:, t, :], hs[:, :], tg[0:S, 1:2], x_all[:, t, :], ALU.mult, ALU.add) \
                    .then_inc(base_done, 1)

            next_hs(0)

            def softmax_shift(t, u):
                view = [bank[2 * u + i][0:S, 0:4 * S].rearrange("s (h n) -> s h n", h=4) for i in range(2)]
                dve.wait_ge(sc_ps, 2 * t + u + 1)
                for i in range(2):
                    ins = dve.tensor_reduce(smax[u][:, 4 * i:4 * i + 4], view[i], axis=AX.X, op=ALU.max)
                ins.then_inc(smax_done, 1)
                dve.wait_ge(smax_done, 2 * t + u + 1)
                if not (isinstance(t, int) and t == 0):
                    dve.wait_ge(attT_ps, 2 * t - 1 + u)
                for i in range(2):
                    ins = dve.tensor_tensor(att[u][:, 4 * i:4 * i + 4, :], view[i],
                                            smax[u][:, 4 * i:4 * i + 4].rearrange("s (h o) -> s h o", o=1)
                                            .to_broadcast([S, 4, S]), ALU.subtract)
                ins.then_inc(sub_done, 1)

            def attend(t, cur, prev, ahead):
                if prev:
                    o = Y[0:S, 0:H * (KPH + 1)].rearrange("s (h k) -> s h k", h=H)
                    dve.wait_ge(av_ps, t)
                    dve.reciprocal(den[:, :], o[:, :, KPH]).then_inc(den_done, 1)
                    dve.wait_ge(den_done, t)
                    dve.tensor_tensor(ao[:, :, :], o[:, :, 0:KPH], den[:, :].rearrange("s (h o) -> s h o", o=1)
                                      .to_broadcast([S, H, KPH]), ALU.mult).then_inc(ao_sb, 1)
                if cur:
                    dve.wait_ge(qk_ps, t + 1)
                    for g in range(NB):
                        ins = dve.tensor_scalar(qT[:, g, :], X[:, g * S:(g + 1) * S], qbT[:, g:g + 1], None, ALU.add)
                    ins.then_inc(q_sb, 1)
                    for g in range(NB):
                        dve.scalar_tensor_tensor(KTm[:, g, :, :],
                                                 X[:, (NB + g) * S:(NB + g + 1) * S].rearrange("p (o s) -> p o s", o=1)
                                                 .to_broadcast([P, HB, S]), kbT[:, g:g + 1],
                                                 head_mask[:, :].rearrange("p (h o) -> p h o", o=1)
                                                 .to_broadcast([P, HB, S]), ALU.add, ALU.mult).then_inc(k_sb, 1)
                        if g == 0:
                            dve.wait_ge(v_ps, t + 1)
                            dve.tensor_tensor(V[:, :, 0:KPH], Y[0:S, 0:LAT].rearrange("s (h k) -> s h k", h=H),
                                              v_b_b[:, :].rearrange("s (h k) -> s h k", h=H), ALU.add) \
                                .then_inc(v_sb, 1)
                    softmax_shift(t, 0)
                if prev:
                    dve.wait_ge(mla_ps, t)
                    dve.tensor_tensor(mla[:, :], Y[0:S, :], o_b_b[:, :], ALU.add).then_inc(mla_sb, 1)
                if cur:
                    softmax_shift(t, 1)
                if prev:
                    dve.wait_ge(mT_sb, t)
                    dve.wait_ge(mTh_sb, t)
                    tok = bass.ds((t - 1) * S, S)
                    dve.tensor_tensor(mTl[:, :, tok], mT[:, :, :], mTh[:, :, tok].bitcast(F32), ALU.subtract) \
                        .then_inc(mTl_sb, 1)
                    dve.wait_ge(lg_ps, t)
                    dve.tensor_tensor(logits[:, bass.ds(t - 1, 1), :], Y[0:S, 0:E].rearrange("s (o e) -> s o e", o=1),
                                      router_bb[:, :].rearrange("s (o e) -> s o e", o=1), ALU.add).then_inc(lg_sb, 1)
                if ahead:
                    next_hs(t + 1)

            over_attend_steps(dve, attend)

            def wide(a):
                return a.rearrange("s (b o) -> s b o", o=1).to_broadcast([S, B, E])

            dve.wait_ge(lg_sb, B)
            own(dve.tensor_reduce(rt_m[:, :], logits[:, :, :], axis=AX.X, op=ALU.max))
            dve.tensor_tensor(rt_a[:, :, :], logits[:, :, :], wide(rt_m[:, :]), ALU.subtract).then_inc(route_sub, 1)
            dve.wait_ge(route_exp, 1)
            own(dve.tensor_reduce(rt_m[:, :], rt_a[:, :, :], axis=AX.X, op=ALU.add))
            own(dve.reciprocal(rt_m[:, :], rt_m[:, :]))
            own(dve.tensor_tensor(rt_a[:, :, :], rt_a[:, :, :], wide(rt_m[:, :]), ALU.mult))
            for b in range(B):
                ins = dve.max(top_p[:, b, :], rt_a[:, b, :])
            own(ins)
            for b in range(B):
                ins = dve.max_index(top_i[:, b, :], top_p[:, b, :], rt_a[:, b, :])
            own(ins)
            own(dve.tensor_copy(top_f[:, :, :], top_i[:, :, :]))
            own(dve.tensor_tensor(rt_m[:, :], top_p[:, :, 0], top_p[:, :, 1], ALU.add))
            own(dve.tensor_scalar(rt_m[:, :], rt_m[:, :], 1e-8, None, ALU.add))
            own(dve.reciprocal(rt_m[:, :], rt_m[:, :]))
            own(dve.tensor_scalar(tg_moe[:, :], tg[:, 1:2], 0.3, None, ALU.mult))
            own(dve.tensor_scalar(rt_m[:, :], rt_m[:, :], tg_moe[0:S, :], None, ALU.mult))
            experts = iota_e[0:S, :].rearrange("s (o e) -> s o e", o=1).to_broadcast([S, B, E])
            for k in range(2):
                dst = comb if k == 0 else rt_a
                own(dve.tensor_tensor(dst[:, :, :], experts, wide(top_f[:, :, k]), ALU.is_equal))
                own(dve.tensor_tensor(dst[:, :, :], dst[:, :, :], wide(top_p[:, :, k]), ALU.mult))
            own(dve.tensor_tensor(comb[:, :, :], comb[:, :, :], rt_a[:, :, :], ALU.add))
            own(dve.tensor_tensor(comb[:, :, :], comb[:, :, :], wide(rt_m[:, :]), ALU.mult))
            dve.sem_inc(h1f_free, 2)
            dve.sem_inc(o_free, 2)
            dve.sem_inc(w2l_done, 1)
            dve.sem_inc(o_added, 1)

            def add_outputs(e, q):
                for i in range(QB):
                    m = (e * NQ + q) * QB + i
                    b = q * QB + i
                    dve.wait_ge(o_ps, m + 2)
                    dve.wait_ge(b2_loaded, e * 16 + 16)
                    dve.tensor_tensor(tmp_o[i][:, :], bank[2 + i][0:S, :], b2_b[:, :], ALU.add).then_inc(o_free, 1)
                    dve.wait_ge(o_free, m + 3)
                    dve.scalar_tensor_tensor(x_all[:, b, :], tmp_o[i][:, :], comb[:, b, bass.ds(e, 1)], x_all[:, b, :],
                                             ALU.mult, ALU.add).then_inc(o_added, 1)

            with dve.Fori(0, E) as e:
                for c in range(KC):
                    dve.wait_ge(w1h_done, e * KC + c + 1)
                    dve.tensor_tensor(w1l[:, c, :], raw[:, c * FF:(c + 1) * FF], w1h[:, c, :].bitcast(F32),
                                      ALU.subtract).then_inc(w1l_done, 1)
                for c in range(KC):
                    dve.wait_ge(w2h_done, e * KC + c + 1)
                    dve.tensor_tensor(w2l[:, 2 * c:2 * c + 2, :],
                                      raw[:, c * FF:(c + 1) * FF].rearrange("p (u n) -> p u n", u=2),
                                      w2h[:, 2 * c:2 * c + 2, :].bitcast(F32), ALU.subtract).then_inc(w2l_done, 1)
                for q in range(NQ):
                    for f in range(FC):
                        n_f = (e * NQ + q) * FC + f
                        dve.wait_ge(h1h_done, n_f + 1)
                        dve.tensor_tensor(h1l[q % 2][:, f, :], h1f[f % 2][:, :], h1h[q % 2][:, f, :].bitcast(F32),
                                          ALU.subtract).then_inc(h1f_free, 1)
                    if q > 0:
                        add_outputs(e, q - 1)
                add_outputs(e, NQ - 1)


_FFN = ["q_w", "q_b", "k_w", "k_b", "v_w", "v_b", "o_w", "o_b", "router_w", "router_b", "w1", "b1", "w2", "b2"]
_INS = ["x", "ctx_1024", "g_xattn", "g_ffn"] + ["L0_xattn_" + n for n in ("w_sim", "b_sim", "W_qv", "b_qv")] \
    + ["L0_ffn_" + n for n in _FFN]
_OUTS = [((B, S, D), "float32")]


def kernel(**inputs):
    import numpy as _np
    import concourse.bacc as _bacc
    from concourse import mybir as _mybir
    from concourse.bass_utils import run_bass_kernel_spmd as _run

    nc = _bacc.Bacc("TRN2", target_bir_lowering=False, num_devices=1)
    arrays, args = {}, []
    for name in _INS:
        a = _np.ascontiguousarray(inputs[name])
        arrays[f"in_{name}_dram"] = a
        args.append(nc.dram_tensor(f"in_{name}_dram", a.shape, _mybir.dt.from_np(a.dtype), kind="ExternalInput").ap())
    for i, (shape, dtype) in enumerate(_OUTS):
        dt = _mybir.dt.from_np(_np.dtype(dtype))
        args.append(nc.dram_tensor(f"out_{i}_dram", shape, dt, kind="ExternalOutput").ap())
    build(nc, *args)
    r = _run(nc, [arrays], core_ids=[0])
    return r.results[0]["out_0_dram"]
```

```python
from contextlib import ExitStack

import numpy as np

import concourse.bass as bass
from concourse import mybir

F32 = mybir.dt.float32
F32R = mybir.dt.float32r
U32 = mybir.dt.uint32
ALU = mybir.AluOpType
ACT = mybir.ActivationFunctionType
AX = mybir.AxisListType

P = 128
B, S, D = 16, 100, 512
C = 722
KC = D // P
JC = -(-C // P)
JREST = C - (JC - 1) * P
NF = 4 * KC
H, KPH = 16, 16
LAT = H * KPH
HB = P // KPH
NB = LAT // P
HD = D // H
E, FF = 8, 2 * D
FC = FF // P
EPS = 1e-5
TOP = 2
TR = 256
TW = TR // P
NT = (TOP * B * S + E * (TR - 1)) // TR
NTE = -(-B * S // TR)
NG = 8
LIST = B * S + TR


def chunk_rows(j):
    return P if j < JC - 1 else JREST


def apart(eng, done):
    eng.wait_ge(done, 1)


def over_batches(eng, step):
    step(0, 0)
    step(1, 1)
    with eng.Fori(1, B // 2 - 1) as i:
        step(2 * i, 0)
        step(2 * i + 1, 1)
    step(B - 2, 0)
    step(B - 1, 1)


def over_tiles(eng, step):
    with eng.Fori(0, NT // 2 - 1) as i:
        step(2 * i, 0, True)
        step(2 * i + 1, 1, True)
    step(NT - 2, 0, True)
    step(NT - 1, 1, False)


def over_attend_steps(eng, step):
    step(0, 0, True, False, False, True)
    step(1, 1, True, True, False, True)
    with eng.Fori(1, B // 2 - 1) as i:
        step(2 * i, 0, True, True, True, True)
        step(2 * i + 1, 1, True, True, True, True)
    step(B - 2, 0, True, True, True, True)
    step(B - 1, 1, True, True, True, False)
    step(B, 0, False, True, True, False)
    step(B + 1, 1, False, False, True, False)


def build(nc, x, ctx_1024, g_xattn, g_ffn, w_sim, b_sim, W_qv, b_qv, q_w, q_b, k_w, k_b, v_w, v_b, o_w, o_b,
          router_w, router_b, w1, b1, w2, b2, out):
    stack = ExitStack()
    with stack:
        base = -(-nc.sbuf_base // 32) * 32
        cursor = [base]

        def place(name, shape, dt=F32):
            size = int(np.prod(shape[1:])) * 4
            t = nc.alloc_sbuf_tensor_at(name, shape, dt, offset=cursor[0])
            cursor[0] += -(-size // 32) * 32
            return t

        def sem(name):
            return stack.enter_context(nc.semaphore(name))

        ident = place("ident", [P, P])
        ones = place("ones", [P, P])
        head_mask = place("head_mask", [P, HB])
        iota_e = place("iota_e", [P, E])
        w2T = place("w2T", [P, KC])
        w3T = place("w3T", [P, KC])
        b_sim_b = place("b_sim_b", [P, 1])
        g_b = place("g_b", [P, 2])
        tg = place("tg", [P, 2])
        tg_moe = place("tg_moe", [P, 1])
        minus_half = place("minus_half", [P, B])
        stats = place("stats", [S, B, 6])
        mv = place("mv", [S, B, 2])
        var_eps = place("var_eps", [S, B])
        rstd = place("rstd", [S, B])
        nmax_all = place("nmax_all", [S, B])
        rowsim_all = place("rowsim_all", [S, B])
        rmax = place("rmax", [S, B])
        pool_max = place("pool_max", [B, 1])
        pool_maxb = place("pool_maxb", [B, S])
        pool_e = place("pool_e", [S, B])
        pool_w = place("pool_w", [S, B])
        psum_row = place("psum_row", [S, 1])
        prob_inv = place("prob_inv", [S, 1])
        qbT = place("qbT", [P, NB])
        kbT = place("kbT", [P, NB])
        b1T = place("b1T", [P, E, FC])
        router_wT = place("router_wT", [P, KC, E])
        router_bb = place("router_bb", [S, E])
        before = place("before", [P, P])
        before_e = place("before_e", [P, E, E])
        tile_row = place("tile_row", [P, NTE])
        list_row = place("list_row", [P, E])
        tile_no = place("tile_no", [P, NT])
        onehot = place("onehot", [S, B, TOP, E])
        weight = place("weight", [S, B, TOP])
        x_row = place("x_row", [S, B, TOP])
        run = place("run", [P, E])
        y_row = place("y_row", [S, B, TOP])
        y_row_i = place("y_row_i", [S, TOP * B, 1], U32)
        plan_i = place("plan_i", [1, E + 2 * NT], U32)
        hcb = place("hcb", [P, KC])
        zeros = place("zeros", [P, D])
        x_all = place("x_all", [S, B, D])

        region_a = cursor[0]
        Wh = place("Wh", [P, NF, D], F32R)
        Wl = place("Wl", [P, NF, D], F32R)
        fT = place("fT", [P, B, 2 * KC, S])
        region_s = cursor[0]
        wstage = [place(f"wstage{i}", [P, D]) for i in range(2)]
        region_b = cursor[0]
        ctx = [place(f"ctx{i}", [P, JC, D]) for i in range(2)]
        ctxT = place("ctxT", [P, KC, C])
        hc = place("hc", [S, D])
        aT = place("aT", [P, KC, S])
        prob = place("prob", [S, C])
        probT = place("probT", [P, JC, S])
        w1_b = place("w1_b", [S, D])
        junk = place("junk", [S, D])
        end = cursor[0]
        cursor[0] = region_b
        wqk = place("wqk", [P, KC, 2 * LAT])
        wv = place("wv", [P, KC, LAT])
        fh = [place(f"fh{i}", [P, NF, S], F32R) for i in range(2)]
        fl = [place(f"fl{i}", [P, NF, S], F32R) for i in range(2)]
        prod = place("prod", [P, 2 * KC, S])
        diag = place("diag", [S, S])
        scaled = place("scaled", [P, KC, S])
        b_qv_b = place("b_qv_b", [S, D])
        y_b = place("y_b", [S, D])
        end = max(end, cursor[0])
        cursor[0] = region_s
        wo = place("wo", [P, NB, D])
        cursor[0] = region_a
        hs = place("hs", [S, D])
        hsT = place("hsT", [P, KC, S])
        qT = place("qT", [P, NB, S])
        KTm = place("KTm", [P, NB, HB, S])
        V = place("V", [S, H, KPH + 1])
        att = [place(f"att{i}", [S, HB, S]) for i in range(2)]
        attT = [place(f"attT{i}", [S, HB, S]) for i in range(2)]
        smax = [place(f"smax{i}", [S, HB]) for i in range(2)]
        den = place("den", [S, H])
        ao = place("ao", [S, H, KPH])
        aoT = place("aoT", [P, NB, S])
        mla = [place(f"mla{i}", [S, D]) for i in range(2)]
        mT = place("mT", [P, KC, S])
        logit = place("logit", [S, E])
        neg_top = place("neg_top", [S, 1])
        esum = place("esum", [S, 1])
        einv = place("einv", [S, 1])
        rp = place("rp", [S, E])
        probs = place("probs", [S, E])
        top_p = place("top_p", [S, E])
        top_i = place("top_i", [S, E], U32)
        top_f = place("top_f", [S, E])
        wsum = place("wsum", [S, 1])
        wsum2 = place("wsum2", [S, 1])
        winv = place("winv", [S, 1])
        winv2 = place("winv2", [S, 1])
        chosen = place("chosen", [S, E])
        rank_sb = place("rank_sb", [S, 2 * E])
        row_of = place("row_of", [S, E])
        picked = place("picked", [S, TOP, E])
        x_row_i = [place(f"x_row_i{i}_{k}", [S, 1], U32) for i in range(2) for k in range(TOP)]
        v_b_b = place("v_b_b", [S, LAT])
        o_b_b = place("o_b_b", [S, D])
        assert cursor[0] <= region_s
        cursor[0] = region_a
        plan = [place(f"plan{i}", [P, E]) for i in range(6)]
        plan_c = place("plan_c", [P, E, NTE])
        plan_s = place("plan_s", [P, E, E])
        plan_t = place("plan_t", [P, NT, E])
        plan_n = [place(f"plan_n{i}", [P, NT]) for i in range(5)]
        plan_y = place("plan_y", [S, B * TOP, E])
        w1h = place("w1h", [P, KC, FF], F32R)
        w1l = place("w1l", [P, KC, FF], F32R)
        w2h = place("w2h", [P, FC, D], F32R)
        w2l = place("w2l", [P, FC, D], F32R)
        raw1 = place("raw1", [P, FC, D])
        raw2 = place("raw2", [P, FC, D])
        xs = place("xs", [P, TW, D])
        mTh = [place(f"mTh{i}", [P, KC, TR], F32R) for i in range(2)]
        mTl = [place(f"mTl{i}", [P, KC, TR], F32R) for i in range(2)]
        h1f = [place(f"h1f{i}", [P, TR]) for i in range(2)]
        h1h = place("h1h", [P, FC, TR], F32R)
        h1l = place("h1l", [P, FC, TR], F32R)
        b1_t = [place(f"b1_t{i}", [P, FC]) for i in range(2)]
        b2_t = [place(f"b2_t{i}", [P, D]) for i in range(2)]
        y_t = [place(f"y_t{i}", [P, D]) for i in range(TW)]
        end = max(end, cursor[0])
        cursor[0] = region_a + 16384
        got = [place(f"got{i}", [S, D]) for i in range(NG)]
        assert cursor[0] <= nc.sbuf_usable_end
        assert end <= nc.sbuf_usable_end, (end, nc.sbuf_usable_end)

        lists = nc.dram_tensor("lists", [E * LIST, D], F32).ap()
        tile_out = nc.dram_tensor("tile_out", [NT * TR, D], F32).ap()
        b1_rows = nc.dram_tensor("b1_rows", [E, P, FC], F32).ap()

        bank = [stack.enter_context(nc.psum_tensor(f"bank{i}", [P, 512], F32)) for i in range(6)]
        pair = stack.enter_context(nc.psum_tensor("pair", [P, 2, 512], F32))

        x_loaded = [sem(f"x_loaded{g}") for g in range(4)]
        consts_loaded = sem("consts_loaded")
        ctx_loaded = [sem(f"ctx_loaded{i}") for i in range(2)]
        wstage_loaded = [sem(f"wstage_loaded{i}") for i in range(2)]
        attw_loaded = sem("attw_loaded")
        attb_loaded = sem("attb_loaded")
        bqv_loaded = sem("bqv_loaded")
        out_stored = sem("out_stored")
        pool_const = sem("pool_const")
        w_split = sem("w_split")
        gate_done = sem("gate_done")
        dve_step = sem("dve_step")
        mv_done = sem("mv_done")
        var_done = sem("var_done")
        rstd_done = sem("rstd_done")
        hc_ready = sem("hc_ready")
        rowsim_done = sem("rowsim_done")
        hcT_ps = sem("hcT_ps")
        hcT_sb = sem("hcT_sb")
        aT_ready = sem("aT_ready")
        ctxT_ps = sem("ctxT_ps")
        ctxT_even = sem("ctxT_even")
        ctxT_odd = sem("ctxT_odd")
        sim_done = sem("sim_done")
        max_done = sem("max_done")
        exp_done = sem("exp_done")
        inv_done = sem("inv_done")
        prob_done = sem("prob_done")
        probT_ps = sem("probT_ps")
        probT_sb = sem("probT_sb")
        hq_ps = sem("hq_ps")
        hq_sb = sem("hq_sb")
        pool_a = sem("pool_a")
        pool_b = sem("pool_b")
        pool_c = sem("pool_c")
        pool_exp = sem("pool_exp")
        pool_d = sem("pool_d")
        pool_ps = sem("pool_ps")
        diag_done = sem("diag_done")
        eb_done = sem("eb_done")
        scaled_done = sem("scaled_done")
        hcb_done = sem("hcb_done")
        prod1_done = sem("prod1_done")
        prod_done = sem("prod_done")
        fh_lowhalf = sem("fh_lowhalf")
        fh_highhalf = sem("fh_highhalf")
        fl_lowhalf = sem("fl_lowhalf")
        fl_highhalf = sem("fl_highhalf")
        y_done = sem("y_done")
        y_biased = sem("y_biased")
        x1_done = sem("x1_done")
        stats2_done = sem("stats2_done")
        hs_ready = sem("hs_ready")
        hsT_ps = sem("hsT_ps")
        hsT_sb = sem("hsT_sb")
        qk_ps = sem("qk_ps")
        q_sb = sem("q_sb")
        k_sb = sem("k_sb")
        v_ps = sem("v_ps")
        v_sb = sem("v_sb")
        sc_ps = sem("sc_ps")
        smax_done = sem("smax_done")
        sub_done = sem("sub_done")
        att_exp = sem("att_exp")
        attT_ps = sem("attT_ps")
        attT_sb = sem("attT_sb")
        av_ps = sem("av_ps")
        den_done = sem("den_done")
        ao_sb = sem("ao_sb")
        aoT_ps = sem("aoT_ps")
        aoT_sb = sem("aoT_sb")
        mla_ps = sem("mla_ps")
        mla_sb = sem("mla_sb")
        mT_ps = sem("mT_ps")
        mT_sb = sem("mT_sb")
        lg_ps = sem("lg_ps")
        lg_sb = sem("lg_sb")
        base_done = sem("base_done")
        rank_read = sem("rank_read")
        neg_top_done = sem("neg_top_done")
        router_exp = sem("router_exp")
        einv_done = sem("einv_done")
        probs_done = sem("probs_done")
        top_done = sem("top_done")
        index_done = sem("index_done")
        index_f = sem("index_f")
        onehot_done = sem("onehot_done")
        chosen_done = sem("chosen_done")
        wsum_done = sem("wsum_done")
        wsum2_done = sem("wsum2_done")
        winv_done = sem("winv_done")
        winv2_done = sem("winv2_done")
        weight_done = sem("weight_done")
        row_done = sem("row_done")
        row2_done = sem("row2_done")
        run_done = sem("run_done")
        picked_done = sem("picked_done")
        x_row_done = sem("x_row_done")
        x_index_done = sem("x_index_done")
        scattered = [sem(f"scattered{i}") for i in range(2)]
        pads_written = sem("pads_written")
        b1_stored = sem("b1_stored")
        plan_done = sem("plan_done")
        xs_loaded = sem("xs_loaded")
        raw1_loaded = sem("raw1_loaded")
        raw2_loaded = sem("raw2_loaded")
        bias_loaded = [sem(f"bias_loaded{i}") for i in range(2)]
        out_tile_stored = [sem(f"out_tile_stored{i}") for i in range(TW)]
        xT_ps = sem("xT_ps")
        mTh_done = sem("mTh_done")
        mTl_done = sem("mTl_done")
        w1h_done = sem("w1h_done")
        w1l_done = sem("w1l_done")
        w2h_done = sem("w2h_done")
        w2l_done = sem("w2l_done")
        h_ps = sem("h_ps")
        gelu_done = sem("gelu_done")
        h1h_done = sem("h1h_done")
        h1l_done = sem("h1l_done")
        o_ps = sem("o_ps")
        y_sb = sem("y_sb")
        gathered = [sem(f"gathered{i}") for i in range(NG)]
        y_index_done = sem("y_index_done")
        combined = sem("combined")

        block = stack.enter_context(nc.Block())

        x_v = x.rearrange("b s d -> s b d")
        out_v = out.rearrange("b s d -> s b d")
        W_v = W_qv.rearrange("(c p) n -> c p n", p=P)
        q_used = q_w.rearrange("(c p) (h t k) -> c t p h k", p=P, t=HD // KPH, k=KPH)
        N_CONSTS = 6 + 3 + E + H
        N_ATTW = 3 * KC + 1

        @block.sync
        def _(sp):
            with nc.allow_non_contiguous_dma(reason="short vectors laid over partitions"):
                for g in range(4):
                    sp.dma_start(x_all[:, 4 * g:4 * g + 4, :], x_v[:, 4 * g:4 * g + 4, :]).then_inc(x_loaded[g], 16)
                n = 0

                def const(dst, src):
                    nonlocal n
                    n += 1
                    sp.dma_start(dst, src).then_inc(consts_loaded, 16)

                const(w1_b[:, :], w_sim[0:D].partition_broadcast(S))
                const(w2T[:, :], w_sim[D:2 * D].rearrange("(c p) -> p c", p=P))
                const(w3T[:, :], w_sim[2 * D:3 * D].rearrange("(c p) -> p c", p=P))
                const(b_sim_b[:, :], b_sim.partition_broadcast(P))
                const(g_b[:, 0:1], g_xattn.partition_broadcast(P))
                const(g_b[:, 1:2], g_ffn.partition_broadcast(P))

                def load_ctx(b, p):
                    if not (isinstance(b, int) and b < 2):
                        sp.wait_ge(hq_ps, b - 1)
                    full = (JC - 1) * P
                    even = JREST - JREST % 16
                    sp.dma_start(ctx[p][:, 0:JC - 1, :], ctx_1024[b, 0:full, :].rearrange("(c p) n -> p c n", p=P)) \
                        .then_inc(ctx_loaded[p], 16)
                    sp.dma_start(ctx[p][0:even, JC - 1, :], ctx_1024[b, full:full + even, :]) \
                        .then_inc(ctx_loaded[p], 16)
                    sp.dma_start(ctx[p][even:JREST, JC - 1, :], ctx_1024[b, full + even:C, :]) \
                        .then_inc(ctx_loaded[p], 16)

                load_ctx(0, 0)
                load_ctx(1, 1)
                const(router_wT[:, :, :], router_w.rearrange("(c p) e -> p c e", p=P))
                const(router_bb[:, :], router_b.partition_broadcast(S))
                const(kbT[:, :], k_b.rearrange("(g p) -> p g", p=P))
                for e in range(E):
                    const(b1T[:, e, :], b1[e].rearrange("(f p) -> p f", p=P))
                for h in range(H):
                    r = (h % HB) * KPH
                    const(qbT[r:r + KPH, h // HB:h // HB + 1], q_b[h * HD:h * HD + KPH].rearrange("(k o) -> k o", o=1))
                assert n == N_CONSTS
                with sp.Fori(1, B // 2 - 1) as i:
                    load_ctx(2 * i, 0)
                    load_ctx(2 * i + 1, 1)
                load_ctx(B - 2, 0)
                load_ctx(B - 1, 1)
                sp.wait_ge(hq_ps, B)
                sp.wait_ge(probT_sb, 2 * B)
                sp.wait_ge(pool_d, 1)
                sp.dma_start(b_qv_b[:, :], b_qv.partition_broadcast(S)).then_inc(bqv_loaded, 16)
                for c in range(KC):
                    sp.dma_start(wqk[:, c, 0:LAT].rearrange("p (h k) -> p h k", k=KPH), q_used[c, 0]) \
                        .then_inc(attw_loaded, 16)
                    sp.dma_start(wqk[:, c, LAT:2 * LAT], k_w[c * P:(c + 1) * P, :]).then_inc(attw_loaded, 16)
                    sp.dma_start(wv[:, c, :], v_w[c * P:(c + 1) * P, :]).then_inc(attw_loaded, 16)
                sp.wait_ge(w_split, 2 * NF)
                sp.dma_start(wo[:, :, :], o_w[0:LAT, :].rearrange("(g p) n -> p g n", p=P)).then_inc(attw_loaded, 16)
                sp.wait_ge(y_done, B)
                sp.dma_start(v_b_b[:, :], v_b.partition_broadcast(S)).then_inc(attb_loaded, 16)
                sp.dma_start(o_b_b[:, :], o_b.partition_broadcast(S)).then_inc(attb_loaded, 16)
                sp.wait_ge(consts_loaded, N_CONSTS * 16)
                sp.dma_start(b1_rows.rearrange("e p f -> p e f"), b1T[:, :, :]).then_inc(b1_stored, 16)
                sp.wait_ge(b1_stored, 16)
                sp.wait_ge(plan_done, 1)
                for e in range(E):
                    rows = sp.value_load(plan_i[0:1, e:e + 1], min_val=0, max_val=B * S)
                    for w in range(TW):
                        sp.dma_start(lists[bass.ds(rows + (e * LIST + w * P), P), :], zeros[:, :]) \
                            .then_inc(pads_written, 16)
                sp.wait_ge(pads_written, E * TW * 16)
                for i in range(2):
                    sp.wait_ge(scattered[i], TOP * (B // 2) * 16)

                def tile_expert(t):
                    return sp.value_load(plan_i[0:1, bass.ds(E + t, 1)], min_val=0, max_val=E - 1)

                def load_rows(t):
                    row = sp.value_load(plan_i[0:1, bass.ds(E + NT + t, 1)], min_val=0, max_val=E * LIST - TR)
                    sp.dma_start(xs[:, :, :], lists[bass.ds(row, TR), :].rearrange("(w p) n -> p w n", p=P)) \
                        .then_inc(xs_loaded, 16)

                def load_w1(e):
                    sp.dma_start(raw1[:, :, :].rearrange("p (c a) n -> p c (a n)", c=KC),
                                 w1[bass.ds(e, 1)].rearrange("o (c p) n -> p (o c) n", p=P)).then_inc(raw1_loaded, 16)

                def load_biases(e, p):
                    sp.dma_start(b1_t[p][:, :], b1_rows[bass.ds(e, 1)].rearrange("o p f -> (o p) f")) \
                        .then_inc(bias_loaded[p], 16)
                    sp.dma_start(b2_t[p][:, :], b2[bass.ds(e, 1)].partition_broadcast(P)
                                 if False else b2[bass.ds(e, 1), :].to_broadcast([P, D])).then_inc(bias_loaded[p], 16)

                def load_w2(e):
                    sp.dma_start(raw2[:, :, :], w2[bass.ds(e, 1)].rearrange("o (c p) n -> p (o c) n", p=P)) \
                        .then_inc(raw2_loaded, 16)

                e0 = tile_expert(0)
                load_w1(e0)
                load_rows(0)
                load_biases(e0, 0)
                load_w2(e0)

                def tile(t, p, more):
                    if more:
                        e = tile_expert(t + 1)
                        sp.wait_ge(xT_ps, TW * (t + 1))
                        load_rows(t + 1)
                        sp.wait_ge(w1l_done, (t + 1) * FC)
                        load_w1(e)
                        sp.wait_ge(y_sb, TW * t + 2)
                        load_biases(e, 1 - p)
                        sp.wait_ge(w2l_done, (t + 1) * FC + 1)
                        load_w2(e)
                    for w in range(TW):
                        sp.wait_ge(y_sb, TW * t + w + 3)
                        sp.dma_start(tile_out[bass.ds(t * TR + w * P, P), :], y_t[w][:, :]) \
                            .then_inc(out_tile_stored[w], 16)

                over_tiles(sp, tile)
                for g in range(4):
                    sp.wait_ge(combined, TOP * 4 * (g + 1))
                    sp.dma_start(out_v[:, 4 * g:4 * g + 4, :], x_all[:, 4 * g:4 * g + 4, :]).then_inc(out_stored, 16)
                sp.wait_ge(out_stored, 64)

        @block.gpsimd
        def _(pool):
            n = 0

            def own(ins):
                nonlocal n
                n += 1
                ins.then_inc(pool_const, 1)
                pool.wait_ge(pool_const, n)

            own(pool.memset(ident[:, :], 0.0))
            own(pool.affine_select(out=ident[:, :], in_=ident[:, :], compare_op=ALU.not_equal, fill=1.0, base=0,
                                   pattern=[[-1, P]], channel_multiplier=1))
            own(pool.memset(ones[:, :], 1.0))
            own(pool.memset(minus_half[:, :], -0.5))
            own(pool.memset(head_mask[:, :], 1.0))
            own(pool.affine_select(out=head_mask[:, :], in_=head_mask[:, :], compare_op=ALU.is_ge, fill=0.0, base=0,
                                   pattern=[[-KPH, HB]], channel_multiplier=1))
            own(pool.affine_select(out=head_mask[:, :], in_=head_mask[:, :], compare_op=ALU.is_ge, fill=0.0,
                                   base=KPH - 1, pattern=[[KPH, HB]], channel_multiplier=-1))
            own(pool.iota(iota_e[:, :], pattern=[[1, E]], base=0, channel_multiplier=0,
                          allow_small_or_imprecise_dtypes=True))
            own(pool.memset(before[:, :], 1.0))
            own(pool.affine_select(out=before[:, :], in_=before[:, :], compare_op=ALU.is_gt, fill=0.0, base=0,
                                   pattern=[[1, P]], channel_multiplier=-1))
            own(pool.memset(before_e[:, :, :], 1.0))
            own(pool.affine_select(out=before_e[:, :, :], in_=before_e[:, :, :], compare_op=ALU.is_gt, fill=0.0,
                                   base=0, pattern=[[1, E], [-1, E]], channel_multiplier=0))
            for dst, count, step in ((tile_row, NTE, TR), (list_row, E, LIST), (tile_no, NT, 1)):
                own(pool.iota(dst[:, :], pattern=[[step, count]], base=0, channel_multiplier=0,
                              allow_small_or_imprecise_dtypes=True))
            own(pool.memset(run[:, :], 0.0))
            own(pool.memset(zeros[:, :], 0.0))
            pool.wait_ge(var_done, 1)
            pool.tensor_tensor(rstd[:, :], var_eps[:, :], minus_half[0:S, :], ALU.pow).then_inc(rstd_done, 1)
            with pool.Fori(0, NF // 2) as m:
                k = 2 * m
                for i in range(2):
                    pool.dma_start(wstage[i][:, :], W_v[k + i]).then_inc(wstage_loaded[i], 16)
                for i in range(2):
                    pool.wait_ge(wstage_loaded[i], k * 8 + 16)
                    pool.tensor_copy(Wh[:, k + i, :], wstage[i][:, :]).then_inc(w_split, 1)
                    pool.wait_ge(w_split, k * 2 + 2 * i + 1)
                    pool.tensor_tensor(Wl[:, k + i, :], wstage[i][:, :], Wh[:, k + i, :].bitcast(F32), ALU.subtract) \
                        .then_inc(w_split, 1)
                pool.wait_ge(w_split, k * 2 + 4)
            pool.wait_ge(var_done, 2)
            pool.tensor_tensor(rstd[:, :], var_eps[:, :], minus_half[0:S, :], ALU.pow).then_inc(rstd_done, 1)
            for b in range(B):
                for k in range(TOP):
                    pool.wait_ge(x_index_done, TOP * b + k + 1)
                    pool.indirect_dma_start(lists[:, :], bass.IndirectOffsetOnAxis(ap=x_row_i[TOP * (b % 2) + k][:, :], axis=0),
                                            mla[b % 2][:, :], None).then_inc(scattered[b % 2], 16)
            pool.wait_ge(y_index_done, 1)
            for w in range(TW):
                pool.wait_ge(out_tile_stored[w], NT * 16)
            for n in range(TOP * B):
                if n >= NG:
                    pool.wait_ge(combined, n - NG + 1)
                pool.indirect_dma_start(got[n % NG][:, :], None, tile_out[:, :],
                                        bass.IndirectOffsetOnAxis(ap=y_row_i[:, n, :], axis=0)).then_inc(gathered[n % NG], 16)

        NPOOL = 17

        @block.scalar
        def _(act):
            act.wait_ge(consts_loaded, N_CONSTS * 16)
            act.preload_act_table(ACT.Exp)
            act.activation(tg[:, :], g_b[:, :], ACT.Tanh).then_inc(gate_done, 1)

            def evac_ctxT(nb):
                for j in range(0, JC, 2):
                    act.wait_ge(ctxT_ps, nb * JC + j + 1)
                    r = chunk_rows(j)
                    act.activation(ctxT[:, :, j * P:j * P + r], bank[1][:, :].rearrange("p (c n) -> p c n", c=KC)[:, :, 0:r],
                                   ACT.Copy).then_inc(ctxT_even, 1)

            evac_ctxT(0)

            def cross(b, p):
                apart(act, pool_const)
                act.wait_ge(max_done, b + 1)
                act.wait_ge(probT_ps, 2 * b)
                act.activation(prob[:, :].rearrange("s (u n) -> s u n", u=2), pair[0:S, :, 0:C // 2], ACT.Exp,
                               bias=nmax_all[:, bass.ds(b, 1)],
                               accum_out=psum_row[:, :]).then_inc(exp_done, 1)
                if not (isinstance(b, int) and b == B - 1):
                    evac_ctxT(b + 1)
                for u in range(2):
                    act.wait_ge(probT_ps, 2 * b + u + 1)
                    act.wait_ge(hq_ps, b)
                    act.activation(probT[:, 3 * u:3 * u + 2, :],
                                   bank[3 + u][:, 0:2 * S].rearrange("p (c s) -> p c s", c=2), ACT.Copy)
                    r = chunk_rows(3 * u + 2)
                    act.activation(probT[0:r, 3 * u + 2, :], bank[3 + u][0:r, 2 * S:3 * S], ACT.Copy) \
                        .then_inc(probT_sb, 1)
                apart(act, pool_const)
                act.wait_ge(hq_ps, b + 1)
                act.activation(fT[:, b, KC:2 * KC, :], bank[5][:, 0:KC * S].rearrange("p (c s) -> p c s", c=KC),
                               ACT.Copy).then_inc(hq_sb, 1)

            over_batches(act, cross)

            act.wait_ge(pool_c, 1)
            act.activation(pool_e[:, :], pool_e[:, :], ACT.Exp).then_inc(pool_exp, 1)

            def round_features(nb, q):
                if not (isinstance(nb, int) and nb < 2):
                    act.wait_ge(y_done, nb - 1)
                apart(act, pool_const)
                act.wait_ge(hq_sb, nb + 1)
                act.activation(fh[q][:, 0:2 * KC, :], fT[:, nb, :, :], ACT.Copy).then_inc(fh_lowhalf, 1)
                act.wait_ge(prod_done, nb + 1)
                act.activation(fh[q][:, 2 * KC:NF, :], prod[:, :, :], ACT.Copy).then_inc(fh_highhalf, 1)

            act.wait_ge(pool_d, 1)
            round_features(0, 0)

            def project(b, p):
                if not (isinstance(b, int) and b == B - 1):
                    round_features(b + 1, 1 - p)

            over_batches(act, project)

            def attend(t, p, cur, prev, rank, ahead):
                if cur:
                    act.wait_ge(hsT_ps, t + 1)
                    act.activation(hsT[:, :, :], bank[4][:, 0:KC * S].rearrange("p (c s) -> p c s", c=KC), ACT.Copy) \
                        .then_inc(hsT_sb, 1)
                if prev:
                    act.wait_ge(attT_ps, 2 * t)
                    act.activation(attT[1][:, :, :].rearrange("s (u h) n -> s u h n", u=2),
                                   pair[0:S, :, 0:4 * S].rearrange("s u (h n) -> s u h n", h=4), ACT.Copy) \
                        .then_inc(attT_sb, 1)
                    act.wait_ge(aoT_ps, t)
                    act.activation(aoT[:, :, :], bank[5][:, 0:NB * S].rearrange("p (g s) -> p g s", g=NB), ACT.Copy) \
                        .then_inc(aoT_sb, 1)
                if cur:
                    for u in range(2):
                        act.wait_ge(sub_done, 2 * t + u + 1)
                        act.activation(att[u][:, :, :], att[u][:, :, :], ACT.Exp, scale=float(KPH) ** -0.5) \
                            .then_inc(att_exp, 1)
                if prev:
                    act.wait_ge(mT_ps, t)
                    act.activation(mT[:, :, :], bank[4][:, 0:KC * S].rearrange("p (c s) -> p c s", c=KC), ACT.Copy) \
                        .then_inc(mT_sb, 1)
                if cur:
                    act.wait_ge(attT_ps, 2 * t + 1)
                    act.activation(attT[0][:, :, :].rearrange("s (u h) n -> s u h n", u=2),
                                   pair[0:S, :, 0:4 * S].rearrange("s u (h n) -> s u h n", h=4), ACT.Copy) \
                        .then_inc(attT_sb, 1)
                if prev:
                    act.wait_ge(neg_top_done, t)
                    act.activation(rp[:, :], logit[:, :], ACT.Exp, bias=neg_top[:, :], accum_out=esum[:, :]) \
                        .then_inc(router_exp, 1)

            over_attend_steps(act, attend)

            act.sem_inc(gelu_done, 2)
            act.preload_act_table(ACT.Gelu)

            def high_w1(t):
                act.wait_ge(raw1_loaded, (t + 1) * 16)
                act.wait_ge(h_ps, t * FC + 1)
                for i in range(FC):
                    act.activation(w1h[:, i // 2, (i % 2) * D:(i % 2 + 1) * D], raw1[:, i, :], ACT.Copy) \
                        .then_inc(w1h_done, 1)

            def high_rows(t, p):
                act.wait_ge(xT_ps, TW * (t + 1))
                for w in range(TW):
                    act.activation(mTh[p][:, :, w * P:(w + 1) * P], bank[2 + w][:, :].rearrange("p (c n) -> p c n", c=KC),
                                   ACT.Copy).then_inc(mTh_done, 1)

            high_w1(0)
            high_rows(0, 0)

            def tile(t, p, more):
                act.wait_ge(bias_loaded[p], (t - p) * 16 + 32)
                act.wait_ge(raw2_loaded, (t + 1) * 16)
                act.wait_ge(o_ps, TW * t + 1)
                for f in range(FC):
                    act.activation(w2h[:, f, :], raw2[:, f, :], ACT.Copy).then_inc(w2h_done, 1)
                    act.wait_ge(h_ps, t * FC + f + 2)
                    act.wait_ge(h1l_done, t * FC + f + 1)
                    act.activation(h1f[f % 2][:, :], bank[f % 2][:, 0:TR], ACT.Gelu, bias=b1_t[p][:, f:f + 1]) \
                        .then_inc(gelu_done, 1)
                if more:
                    high_rows(t + 1, 1 - p)
                    high_w1(t + 1)

            over_tiles(act, tile)

        @block.tensor
        def _(pe):
            pe.wait_ge(pool_const, NPOOL)

            def transpose_next(nb, p):
                pe.wait_ge(hc_ready, nb + 1)
                pe.wait_ge(aT_ready, nb)
                for c in range(KC):
                    t = nc.tensor.transpose(bank[0][:, c * S:(c + 1) * S], hc[:, c * P:(c + 1) * P], ident[0:S, 0:S])
                t.then_inc(hcT_ps, 1)
                pe.wait_ge(ctx_loaded[p], (nb - p) * 24 + 48)
                for j in range(JC):
                    r = chunk_rows(j)
                    pe.wait_ge(ctxT_odd if j % 2 else ctxT_even, nb * (JC // 2) + j // 2)
                    for c in range(KC):
                        t = nc.tensor.transpose(bank[1 + j % 2][:, c * P:c * P + r], ctx[p][0:r, j, c * P:(c + 1) * P],
                                                ident[0:r, 0:r])
                    t.then_inc(ctxT_ps, 1)

            transpose_next(0, 0)

            def cross(b, p):
                pe.wait_ge(aT_ready, b + 1)
                pe.wait_ge(ctxT_even, (b + 1) * (JC // 2))
                pe.wait_ge(ctxT_odd, (b + 1) * (JC // 2))
                pe.wait_ge(exp_done, b)
                for u in range(2):
                    for c in range(KC):
                        t = nc.tensor.matmul(pair[0:S, u, 0:C // 2], aT[:, c, :], ctxT[:, c, u * (C // 2):(u + 1) * (C // 2)],
                                             start=(c == 0), stop=(c == KC - 1))
                t.then_inc(sim_done, 1)
                if not (isinstance(b, int) and b == B - 1):
                    transpose_next(b + 1, 1 - p)
                pe.wait_ge(prob_done, b + 1)
                for u in range(2):
                    pe.wait_ge(probT_sb, 2 * b)
                    for i in range(3):
                        j = 3 * u + i
                        r = chunk_rows(j)
                        t = nc.tensor.transpose(bank[3 + u][0:r, i * S:(i + 1) * S], prob[:, j * P:j * P + r],
                                                ident[0:S, 0:S])
                    t.then_inc(probT_ps, 1)
                pe.wait_ge(probT_sb, 2 * b + 2)
                pe.wait_ge(hq_sb, b)
                for c in range(KC):
                    for j in range(JC):
                        r = chunk_rows(j)
                        t = nc.tensor.matmul(bank[5][:, c * S:(c + 1) * S], ctx[p][0:r, j, c * P:(c + 1) * P],
                                             probT[0:r, j, :], start=(j == 0), stop=(j == JC - 1))
                t.then_inc(hq_ps, 1)

            over_batches(pe, cross)

            pe.wait_ge(pool_a, 1)
            nc.tensor.transpose(bank[0][0:B, 0:S], rmax[:, :], ident[0:S, 0:S]).then_inc(pool_ps, 1)
            pe.wait_ge(pool_b, 1)
            nc.tensor.transpose(bank[0][0:S, 0:B], pool_maxb[:, :], ident[0:B, 0:B]).then_inc(pool_ps, 1)
            pe.wait_ge(pool_exp, 1)
            nc.tensor.matmul(bank[0][:, 0:B], ones[0:S, :], pool_e[:, :], start=True, stop=True).then_inc(pool_ps, 1)

            def weights_of(nb):
                pe.wait_ge(diag_done, nb + 1)
                nc.tensor.matmul(bank[2][:, 0:S], ones[0:S, :], diag[:, :], start=True, stop=True).then_inc(eb_done, 1)

            weights_of(0)

            def project(b, p):
                pe.wait_ge(w_split, 2 * NF)
                pe.wait_ge(fh_highhalf, b + 1)
                pe.wait_ge(fl_highhalf, b + 1)
                pe.wait_ge(y_biased, b)
                for k in range(NF):
                    if k == NF // 2 and not (isinstance(b, int) and b == B - 1):
                        weights_of(b + 1)
                    nc.tensor.matmul(bank[0][0:S, :], fl[p][:, k, :], Wh[:, k, :], start=(k == 0), stop=False)
                    nc.tensor.matmul(bank[0][0:S, :], fh[p][:, k, :], Wl[:, k, :], start=False, stop=False)
                    t = nc.tensor.matmul(bank[0][0:S, :], fh[p][:, k, :], Wh[:, k, :], start=False, stop=(k == NF - 1))
                t.then_inc(y_done, 1)

            over_batches(pe, project)

            X, Y = bank[4], bank[5]

            def att_transposes(u, count):
                for h in range(HB):
                    t = nc.tensor.transpose(pair[0:S, h // 4, (h % 4) * S:(h % 4 + 1) * S], att[u][:, h, :],
                                            ident[0:S, 0:S])
                t.then_inc(attT_ps, 1)

            def scores(t, u):
                pe.wait_ge(q_sb, t + 1)
                pe.wait_ge(k_sb, 2 * t + u + 1)
                if not (isinstance(t, int) and t == 0):
                    pe.wait_ge(sub_done, 2 * t - 1 + u)
                for i in range(2):
                    m = nc.tensor.matmul(bank[2 * u + i][0:S, 0:4 * S], qT[:, u, :],
                                         KTm[:, u, 4 * i:4 * i + 4, :].rearrange("p h s -> p (h s)"),
                                         start=True, stop=True)
                m.then_inc(sc_ps, 1)

            def attend(t, p, cur, prev, rank, ahead):
                if cur:
                    pe.wait_ge(hs_ready, t + 1)
                    if rank:
                        pe.wait_ge(mT_sb, t - 1)
                    for c in range(KC):
                        m = nc.tensor.transpose(X[:, c * S:(c + 1) * S], hs[:, c * P:(c + 1) * P], ident[0:S, 0:S])
                    m.then_inc(hsT_ps, 1)
                if prev:
                    pe.wait_ge(att_exp, 2 * t)
                    pe.wait_ge(attT_sb, 2 * t - 1)
                    att_transposes(1, t)
                    pe.wait_ge(attT_sb, 2 * t)
                    pe.wait_ge(v_sb, t)
                    if rank:
                        pe.wait_ge(lg_sb, t - 1)
                    for h in range(H):
                        m = nc.tensor.matmul(Y[0:S, h * (KPH + 1):(h + 1) * (KPH + 1)], attT[h // HB][:, h % HB, :],
                                             V[:, h, :], start=True, stop=True)
                    m.then_inc(av_ps, 1)
                if cur:
                    pe.wait_ge(attw_loaded, N_ATTW * 16)
                    pe.wait_ge(hsT_sb, t + 1)
                    for g in range(2 * NB):
                        for c in range(KC):
                            m = nc.tensor.matmul(X[:, g * S:(g + 1) * S], wqk[:, c, g * P:(g + 1) * P], hsT[:, c, :],
                                                 start=(c == 0), stop=(c == KC - 1))
                    m.then_inc(qk_ps, 1)
                    if prev:
                        pe.wait_ge(ao_sb, t)
                    for c in range(KC):
                        m = nc.tensor.matmul(Y[0:S, 0:LAT], hsT[:, c, :], wv[:, c, :], start=(c == 0), stop=(c == KC - 1))
                    m.then_inc(v_ps, 1)
                if prev:
                    pe.wait_ge(ao_sb, t)
                    if cur:
                        pe.wait_ge(v_sb, t + 1)
                    for g in range(NB):
                        m = nc.tensor.transpose(Y[:, g * S:(g + 1) * S],
                                                ao[:, g * HB:(g + 1) * HB, :].rearrange("s h k -> s (h k)"),
                                                ident[0:S, 0:S])
                    m.then_inc(aoT_ps, 1)
                if cur:
                    scores(t, 0)
                if prev:
                    pe.wait_ge(aoT_sb, t)
                    for g in range(NB):
                        m = nc.tensor.matmul(Y[0:S, :], aoT[:, g, :], wo[:, g, :], start=(g == 0), stop=(g == NB - 1))
                    m.then_inc(mla_ps, 1)
                if cur:
                    scores(t, 1)
                if prev:
                    pe.wait_ge(mla_sb, t)
                    for c in range(KC):
                        m = nc.tensor.transpose(X[:, c * S:(c + 1) * S], mla[1 - p][:, c * P:(c + 1) * P],
                                                ident[0:S, 0:S])
                    m.then_inc(mT_ps, 1)
                if cur:
                    pe.wait_ge(att_exp, 2 * t + 1)
                    if prev:
                        pe.wait_ge(attT_sb, 2 * t)
                    att_transposes(0, t)
                if prev:
                    pe.wait_ge(mT_sb, t)
                    for c in range(KC):
                        m = nc.tensor.matmul(Y[0:S, 0:E], mT[:, c, :], router_wT[:, c, :], start=(c == 0),
                                             stop=(c == KC - 1))
                if rank:
                    pe.wait_ge(chosen_done, t - 1)
                    if not prev:
                        pe.wait_ge(lg_sb, t - 1)
                    nc.tensor.matmul(Y[0:S, E:2 * E], before[0:S, 0:S], chosen[:, :], start=True, stop=True)
                    m = nc.tensor.matmul(Y[0:S, 2 * E:3 * E], ones[0:S, 0:S], chosen[:, :], start=True, stop=True)
                if prev or rank:
                    m.then_inc(lg_ps, 1)

            over_attend_steps(pe, attend)

            pe.sem_inc(h_ps, 1)
            pe.sem_inc(o_ps, 1)

            def rows_of(t):
                pe.wait_ge(xs_loaded, (t + 1) * 16)
                for w in range(TW):
                    for c in range(KC):
                        m = nc.tensor.transpose(bank[2 + w][:, c * P:(c + 1) * P], xs[:, w, c * P:(c + 1) * P],
                                                ident[:, :])
                    m.then_inc(xT_ps, 1)

            rows_of(0)

            def tile(t, p, more):
                pe.wait_ge(mTh_done, TW * (t + 1))
                pe.wait_ge(mTl_done, TW * (t + 1))
                pe.wait_ge(w1h_done, FC * (t + 1))
                pe.wait_ge(w1l_done, FC * (t + 1))
                for f in range(FC):
                    pe.wait_ge(gelu_done, t * FC + f + 1)
                    for c in range(KC):
                        wh, wl = (w[:, c, f * P:(f + 1) * P] for w in (w1h, w1l))
                        nc.tensor.matmul(bank[f % 2][:, 0:TR], wl, mTh[p][:, c, :], start=(c == 0), stop=False)
                        nc.tensor.matmul(bank[f % 2][:, 0:TR], wh, mTl[p][:, c, :], start=False, stop=False)
                        m = nc.tensor.matmul(bank[f % 2][:, 0:TR], wh, mTh[p][:, c, :], start=False,
                                             stop=(c == KC - 1))
                    m.then_inc(h_ps, 1)
                if more:
                    rows_of(t + 1)
                for w in range(TW):
                    pe.wait_ge(y_sb, TW * t + w + 1)
                    for f in range(FC):
                        if w == 0:
                            pe.wait_ge(h1l_done, t * FC + f + 3)
                            pe.wait_ge(w2l_done, t * FC + f + 2)
                        hh, hl = (h[:, f, w * P:(w + 1) * P] for h in (h1h, h1l))
                        nc.tensor.matmul(bank[4 + w][:, :], hl, w2h[:, f, :], start=(f == 0), stop=False)
                        nc.tensor.matmul(bank[4 + w][:, :], hh, w2l[:, f, :], start=False, stop=False)
                        m = nc.tensor.matmul(bank[4 + w][:, :], hh, w2h[:, f, :], start=False, stop=(f == FC - 1))
                    m.then_inc(o_ps, 1)

            over_tiles(pe, tile)

        @block.vector
        def _(dve):
            n = 0

            def own(ins):
                nonlocal n
                n += 1
                ins.then_inc(dve_step, 1)
                dve.wait_ge(dve_step, n)

            def row_stats():
                for b in range(B):
                    ins = dve.bn_aggr(mv[:, b, :], stats[:, b, :])
                own(ins)
                dve.tensor_scalar(var_eps[:, :], mv[:, :, 1], EPS, None, ALU.add).then_inc(var_done, 1)

            for b in range(B):
                if b % 4 == 0:
                    dve.wait_ge(x_loaded[b // 4], 16)
                ins = dve.bn_stats(stats[:, b, :], x_all[:, b, :])
            own(ins)
            row_stats()
            dve.wait_ge(consts_loaded, N_CONSTS * 16)
            dve.wait_ge(rstd_done, 1)

            def normalise(dst, b, done):
                dve.tensor_scalar(dst, x_all[:, b, :], mv[:, b, 0:1], rstd[:, bass.ds(b, 1)], ALU.subtract, ALU.mult) \
                    .then_inc(done, 1)

            def next_hc(nb):
                dve.wait_ge(hcT_ps, nb)
                normalise(hc[:, :], nb, hc_ready)
                dve.wait_ge(hc_ready, nb + 1)
                dve.scalar_tensor_tensor(junk[:, :], hc[:, :], 1.0, w1_b[:, :], ALU.mult, ALU.mult,
                                         accum_out=rowsim_all[:, bass.ds(nb, 1)]).then_inc(rowsim_done, 1)

            def next_aT(nb):
                src = bank[0][:, 0:KC * S].rearrange("p (c s) -> p c s", c=KC)
                apart(dve, pool_const)
                dve.wait_ge(hcT_ps, nb + 1)
                dve.tensor_copy(fT[:, nb, 0:KC, :], src).then_inc(hcT_sb, 1)
                dve.wait_ge(sim_done, nb)
                for c in range(KC):
                    ins = dve.tensor_scalar(aT[:, c, :], src[:, c, :], w3T[:, c:c + 1], w2T[:, c:c + 1], ALU.mult,
                                            ALU.add)
                ins.then_inc(aT_ready, 1)

            def odd_ctxT(nb):
                for j in range(1, JC, 2):
                    dve.wait_ge(ctxT_ps, nb * JC + j + 1)
                    r = chunk_rows(j)
                    dve.tensor_copy(ctxT[:, :, j * P:j * P + r],
                                    bank[2][:, :].rearrange("p (c n) -> p c n", c=KC)[:, :, 0:r]).then_inc(ctxT_odd, 1)

            next_hc(0)
            next_aT(0)
            odd_ctxT(0)

            def cross(b, p):
                last = isinstance(b, int) and b == B - 1
                if not last:
                    next_hc(b + 1)
                apart(dve, pool_const)
                dve.wait_ge(sim_done, b + 1)
                dve.tensor_reduce(nmax_all[:, bass.ds(b, 1)], pair[0:S, :, 0:C // 2], axis=AX.XY, op=ALU.max,
                                  negate=True).then_inc(max_done, 1)
                if not last:
                    next_aT(b + 1)
                dve.wait_ge(exp_done, b + 1)
                dve.reciprocal(prob_inv[:, :], psum_row[:, :]).then_inc(inv_done, 1)
                dve.wait_ge(inv_done, b + 1)
                dve.tensor_scalar(prob[:, :], prob[:, :], prob_inv[:, :], None, ALU.mult).then_inc(prob_done, 1)
                if not last:
                    odd_ctxT(b + 1)

            over_batches(dve, cross)

            own(dve.tensor_tensor(rmax[:, :], rowsim_all[:, :], nmax_all[:, :], ALU.subtract))
            dve.tensor_scalar(rmax[:, :], rmax[:, :], b_sim_b[0:S, :], None, ALU.add).then_inc(pool_a, 1)
            dve.wait_ge(pool_ps, 1)
            own(dve.tensor_reduce(pool_max[:, :], bank[0][0:B, 0:S], axis=AX.X, op=ALU.max))
            dve.tensor_copy(pool_maxb[:, :], pool_max[:, :].to_broadcast([B, S])).then_inc(pool_b, 1)
            dve.wait_ge(pool_ps, 2)
            dve.tensor_tensor(pool_e[:, :], rmax[:, :], bank[0][0:S, 0:B], ALU.subtract).then_inc(pool_c, 1)
            dve.wait_ge(pool_ps, 3)
            own(dve.reciprocal(pool_w[:, :], bank[0][0:S, 0:B]))
            dve.tensor_tensor(pool_w[:, :], pool_w[:, :], pool_e[:, :], ALU.mult).then_inc(pool_d, 1)
            dve.wait_ge(pool_d, 1)

            def diag_of(nb):
                dve.wait_ge(eb_done, nb)
                dve.tensor_scalar(diag[:, :], ident[0:S, 0:S], pool_w[:, bass.ds(nb, 1)], None, ALU.mult) \
                    .then_inc(diag_done, 1)

            def features(nb, q):
                hcT_b, hqT_b = fT[:, nb, 0:KC, :], fT[:, nb, KC:2 * KC, :]
                dve.wait_ge(fh_highhalf, nb)
                dve.wait_ge(fl_highhalf, nb)
                dve.tensor_tensor(prod[:, 0:KC, :], hcT_b, hqT_b, ALU.mult).then_inc(prod1_done, 1)
                dve.wait_ge(eb_done, nb + 1)
                dve.tensor_tensor(scaled[:, :, :], hcT_b, bank[2][:, 0:S].rearrange("p (o s) -> p o s", o=1)
                                  .to_broadcast([P, KC, S]), ALU.mult).then_inc(scaled_done, 1)
                dve.wait_ge(scaled_done, nb + 1)
                dve.tensor_reduce(hcb[:, :], scaled[:, :, :], axis=AX.X, op=ALU.add).then_inc(hcb_done, 1)
                dve.wait_ge(hcb_done, nb + 1)
                dve.tensor_tensor(prod[:, KC:2 * KC, :], hcT_b, hcb[:, :].rearrange("p (c o) -> p c o", o=1)
                                  .to_broadcast([P, KC, S]), ALU.mult).then_inc(prod_done, 1)
                dve.wait_ge(fh_lowhalf, nb + 1)
                dve.tensor_tensor(fl[q][:, 0:2 * KC, :], fT[:, nb, :, :], fh[q][:, 0:2 * KC, :].bitcast(F32),
                                  ALU.subtract).then_inc(fl_lowhalf, 1)
                dve.wait_ge(fh_highhalf, nb + 1)
                dve.tensor_tensor(fl[q][:, 2 * KC:NF, :], prod[:, :, :], fh[q][:, 2 * KC:NF, :].bitcast(F32),
                                  ALU.subtract).then_inc(fl_highhalf, 1)

            dve.wait_ge(hq_sb, B)
            diag_of(0)
            features(0, 0)
            dve.wait_ge(bqv_loaded, 16)
            dve.wait_ge(gate_done, 1)

            def project(b, p):
                if not (isinstance(b, int) and b == B - 1):
                    diag_of(b + 1)
                    features(b + 1, 1 - p)
                dve.wait_ge(y_done, b + 1)
                dve.tensor_tensor(y_b[:, :], bank[0][0:S, :], b_qv_b[:, :], ALU.add).then_inc(y_biased, 1)
                dve.wait_ge(y_biased, b + 1)
                dve.scalar_tensor_tensor(x_all[:, b, :], y_b[:, :], tg[0:S, 0:1], x_all[:, b, :], ALU.mult, ALU.add) \
                    .then_inc(x1_done, 1)
                apart(dve, pool_const)
                dve.wait_ge(x1_done, b + 1)
                dve.bn_stats(stats[:, b, :], x_all[:, b, :]).then_inc(stats2_done, 1)

            over_batches(dve, project)
            dve.wait_ge(stats2_done, B)
            row_stats()
            dve.memset(V[:, :, KPH:KPH + 1], 1.0).then_inc(dve_step, 1)
            n += 1
            dve.wait_ge(attb_loaded, 32)
            dve.wait_ge(rstd_done, 2)
            X, Y = bank[4], bank[5]

            def next_hs(t):
                dve.wait_ge(hsT_ps, t)
                normalise(hs[:, :], t, hs_ready)
                dve.wait_ge(hs_ready, t + 1)
                dve.scalar_tensor_tensor(x_all[:, t, :], hs[:, :], tg[0:S, 1:2], x_all[:, t, :], ALU.mult, ALU.add) \
                    .then_inc(base_done, 1)

            next_hs(0)

            def softmax_shift(t, u):
                view = [bank[2 * u + i][0:S, 0:4 * S].rearrange("s (h n) -> s h n", h=4) for i in range(2)]
                dve.wait_ge(sc_ps, 2 * t + u + 1)
                for i in range(2):
                    ins = dve.tensor_reduce(smax[u][:, 4 * i:4 * i + 4], view[i], axis=AX.X, op=ALU.max)
                ins.then_inc(smax_done, 1)
                dve.wait_ge(smax_done, 2 * t + u + 1)
                if not (isinstance(t, int) and t == 0):
                    dve.wait_ge(attT_ps, 2 * t - 1 + u)
                for i in range(2):
                    ins = dve.tensor_tensor(att[u][:, 4 * i:4 * i + 4, :], view[i],
                                            smax[u][:, 4 * i:4 * i + 4].rearrange("s (h o) -> s h o", o=1)
                                            .to_broadcast([S, 4, S]), ALU.subtract)
                ins.then_inc(sub_done, 1)

            def attend(t, p, cur, prev, rank, ahead):
                if prev:
                    o = Y[0:S, 0:H * (KPH + 1)].rearrange("s (h k) -> s h k", h=H)
                    dve.wait_ge(av_ps, t)
                    dve.reciprocal(den[:, :], o[:, :, KPH]).then_inc(den_done, 1)
                    dve.wait_ge(den_done, t)
                    dve.tensor_tensor(ao[:, :, :], o[:, :, 0:KPH], den[:, :].rearrange("s (h o) -> s h o", o=1)
                                      .to_broadcast([S, H, KPH]), ALU.mult).then_inc(ao_sb, 1)
                if cur:
                    dve.wait_ge(qk_ps, t + 1)
                    for g in range(NB):
                        ins = dve.tensor_scalar(qT[:, g, :], X[:, g * S:(g + 1) * S], qbT[:, g:g + 1], None, ALU.add)
                    ins.then_inc(q_sb, 1)
                    for g in range(NB):
                        dve.scalar_tensor_tensor(KTm[:, g, :, :],
                                                 X[:, (NB + g) * S:(NB + g + 1) * S].rearrange("p (o s) -> p o s", o=1)
                                                 .to_broadcast([P, HB, S]), kbT[:, g:g + 1],
                                                 head_mask[:, :].rearrange("p (h o) -> p h o", o=1)
                                                 .to_broadcast([P, HB, S]), ALU.add, ALU.mult).then_inc(k_sb, 1)
                        if g == 0:
                            dve.wait_ge(v_ps, t + 1)
                            dve.tensor_tensor(V[:, :, 0:KPH], Y[0:S, 0:LAT].rearrange("s (h k) -> s h k", h=H),
                                              v_b_b[:, :].rearrange("s (h k) -> s h k", h=H), ALU.add) \
                                .then_inc(v_sb, 1)
                    softmax_shift(t, 0)
                if prev:
                    dve.wait_ge(mla_ps, t)
                    if not (isinstance(t, int) and t < 3):
                        dve.wait_ge(scattered[1 - p], TOP * 8 * (t - 1 - (1 - p)))
                    dve.tensor_tensor(mla[1 - p][:, :], Y[0:S, :], o_b_b[:, :], ALU.add).then_inc(mla_sb, 1)
                if cur:
                    softmax_shift(t, 1)
                if prev or rank:
                    dve.wait_ge(lg_ps, t)
                if rank:
                    dve.tensor_copy(rank_sb[:, :], Y[0:S, E:3 * E]).then_inc(rank_read, 1)
                if prev:
                    dve.tensor_tensor(logit[:, :], Y[0:S, 0:E], router_bb[:, :], ALU.add).then_inc(lg_sb, 1)
                if rank:
                    places(t - 2, p)
                if prev:
                    route(t - 1)
                if ahead:
                    next_hs(t + 1)

            def route(b):
                dve.wait_ge(lg_sb, b + 1)
                dve.tensor_reduce(neg_top[:, :], logit[:, :], axis=AX.X, op=ALU.max, negate=True) \
                    .then_inc(neg_top_done, 1)
                dve.wait_ge(router_exp, b + 1)
                dve.reciprocal(einv[:, :], esum[:, :]).then_inc(einv_done, 1)
                dve.wait_ge(einv_done, b + 1)
                dve.tensor_scalar(probs[:, :], rp[:, :], einv[:, :], None, ALU.mult).then_inc(probs_done, 1)
                apart(dve, pool_const)
                dve.wait_ge(probs_done, b + 1)
                dve.max(top_p[:, :], probs[:, :]).then_inc(top_done, 1)
                apart(dve, pool_const)
                dve.wait_ge(top_done, b + 1)
                dve.max_index(top_i[:, :], top_p[:, :], probs[:, :]).then_inc(index_done, 1)
                dve.tensor_tensor(wsum[:, :], top_p[:, 0:1], top_p[:, 1:2], ALU.add).then_inc(wsum_done, 1)
                dve.wait_ge(index_done, b + 1)
                dve.tensor_copy(top_f[:, :], top_i[:, :]).then_inc(index_f, 1)
                dve.wait_ge(wsum_done, b + 1)
                dve.tensor_scalar(wsum2[:, :], wsum[:, :], 1e-8, None, ALU.add).then_inc(wsum2_done, 1)
                dve.wait_ge(index_f, b + 1)
                for k in range(TOP):
                    ins = dve.tensor_scalar(onehot[:, bass.ds(b, 1), k, :].rearrange("s o e -> s (o e)"),
                                            iota_e[0:S, :], top_f[:, k:k + 1], None, ALU.is_equal)
                ins.then_inc(onehot_done, 1)
                dve.wait_ge(wsum2_done, b + 1)
                dve.reciprocal(winv[:, :], wsum2[:, :]).then_inc(winv_done, 1)
                dve.wait_ge(onehot_done, b + 1)
                dve.tensor_tensor(chosen[:, :], onehot[:, bass.ds(b, 1), 0, :].rearrange("s o e -> s (o e)"),
                                  onehot[:, bass.ds(b, 1), 1, :].rearrange("s o e -> s (o e)"), ALU.add) \
                    .then_inc(chosen_done, 1)
                dve.wait_ge(winv_done, b + 1)
                dve.tensor_scalar(winv2[:, :], winv[:, :], tg_moe[0:S, :], None, ALU.mult).then_inc(winv2_done, 1)
                dve.wait_ge(winv2_done, b + 1)
                dve.tensor_scalar(weight[:, bass.ds(b, 1), :].rearrange("s o k -> s (o k)"), top_p[:, 0:TOP],
                                  winv2[:, :], None, ALU.mult).then_inc(weight_done, 1)

            def places(b, p):
                dve.wait_ge(rank_read, b + 1)
                dve.tensor_tensor(row_of[:, :], rank_sb[:, 0:E], run[0:S, :], ALU.add).then_inc(row_done, 1)
                dve.wait_ge(row_done, b + 1)
                dve.tensor_tensor(row_of[:, :], row_of[:, :], list_row[0:S, :], ALU.add).then_inc(row2_done, 1)
                dve.tensor_tensor(run[0:S, :], run[0:S, :], rank_sb[:, E:2 * E], ALU.add).then_inc(run_done, 1)
                dve.wait_ge(row2_done, b + 1)
                dve.tensor_tensor(picked[:, :, :], onehot[:, bass.ds(b, 1), :, :].rearrange("s o k e -> s (o k) e"),
                                  row_of[:, :].rearrange("s (o e) -> s o e", o=1).to_broadcast([S, TOP, E]),
                                  ALU.mult).then_inc(picked_done, 1)
                apart(dve, pool_const)
                dve.wait_ge(picked_done, b + 1)
                dve.tensor_reduce(x_row[:, bass.ds(b, 1), :].rearrange("s o k -> s (o k)"), picked[:, :, :],
                                  axis=AX.X, op=ALU.add).then_inc(x_row_done, 1)
                apart(dve, pool_const)
                dve.wait_ge(x_row_done, b + 1)
                for k in range(TOP):
                    dve.tensor_copy(x_row_i[TOP * p + k][:, :], x_row[:, bass.ds(b, 1), k]).then_inc(x_index_done, 1)

            dve.tensor_scalar(tg_moe[:, :], tg[:, 1:2], 0.3, None, ALU.mult).then_inc(dve_step, 1)
            n += 1
            dve.wait_ge(dve_step, n)
            over_attend_steps(dve, attend)

            def per(a, shape):
                return a.rearrange("p (e o) -> p e o", o=1).to_broadcast(shape)

            def each(a, shape):
                return a.rearrange("p (o e) -> p o e", o=1).to_broadcast(shape)

            tiles_of, start, stop, offset, ends, _spare = plan
            own(dve.tensor_tensor(plan_c[0:S, :, :], per(run[0:S, :], [S, E, NTE]), each(tile_row[0:S, :], [S, E, NTE]),
                                  ALU.is_gt))
            own(dve.tensor_reduce(tiles_of[0:S, :], plan_c[0:S, :, :], axis=AX.X, op=ALU.add))
            own(dve.tensor_tensor(plan_s[0:S, :, :], before_e[0:S, :, :], each(tiles_of[0:S, :], [S, E, E]), ALU.mult))
            own(dve.tensor_reduce(start[0:S, :], plan_s[0:S, :, :], axis=AX.X, op=ALU.add))
            own(dve.tensor_tensor(stop[0:S, :], start[0:S, :], tiles_of[0:S, :], ALU.add))
            tile_expert, tile_first, live, from_list, tile_rows = plan_n
            own(dve.tensor_tensor(plan_t[0:S, :, :], per(tile_no[0:S, :], [S, NT, E]), each(stop[0:S, :], [S, NT, E]),
                                  ALU.is_ge))
            own(dve.tensor_reduce(tile_expert[0:S, :], plan_t[0:S, :, :], axis=AX.X, op=ALU.add))
            own(dve.tensor_tensor(plan_t[0:S, :, :], plan_t[0:S, :, :], each(tiles_of[0:S, :], [S, NT, E]), ALU.mult))
            own(dve.tensor_reduce(tile_first[0:S, :], plan_t[0:S, :, :], axis=AX.X, op=ALU.add))
            own(dve.tensor_scalar(live[0:S, :], tile_expert[0:S, :], float(E) - 0.5, None, ALU.is_lt))
            own(dve.tensor_tensor(tile_expert[0:S, :], tile_expert[0:S, :], live[0:S, :], ALU.mult))
            own(dve.tensor_tensor(tile_rows[0:S, :], tile_no[0:S, :], tile_first[0:S, :], ALU.subtract))
            own(dve.tensor_tensor(tile_rows[0:S, :], tile_rows[0:S, :], live[0:S, :], ALU.mult))
            own(dve.tensor_scalar(tile_rows[0:S, :], tile_rows[0:S, :], float(TR), None, ALU.mult))
            own(dve.tensor_scalar(from_list[0:S, :], tile_expert[0:S, :], float(LIST), None, ALU.mult))
            own(dve.tensor_tensor(tile_rows[0:S, :], tile_rows[0:S, :], from_list[0:S, :], ALU.add))
            dve.tensor_copy(plan_i[0:1, 0:E], run[0:1, :])
            dve.tensor_copy(plan_i[0:1, E:E + NT], tile_expert[0:1, :])
            dve.tensor_copy(plan_i[0:1, E + NT:E + 2 * NT], tile_rows[0:1, :]).then_inc(plan_done, 1)
            own(dve.tensor_scalar(offset[0:S, :], start[0:S, :], float(TR), None, ALU.mult))
            own(dve.tensor_tensor(offset[0:S, :], offset[0:S, :], list_row[0:S, :], ALU.subtract))
            own(dve.tensor_tensor(plan_y[:, :, :], onehot[:, :, :, :].rearrange("s b k e -> s (b k) e"),
                                  each(offset[0:S, :], [S, B * TOP, E]), ALU.mult))
            own(dve.tensor_reduce(y_row[:, :, :].rearrange("s b k -> s (b k)"), plan_y[:, :, :], axis=AX.X, op=ALU.add))
            own(dve.tensor_tensor(y_row[:, :, :], y_row[:, :, :], x_row[:, :, :], ALU.add))
            dve.tensor_copy(y_row_i[:, :, :].rearrange("s n o -> s (n o)"),
                            y_row[:, :, :].rearrange("s b k -> s (b k)")).then_inc(y_index_done, 1)

            dve.sem_inc(h1l_done, 2)
            dve.sem_inc(w2l_done, 1)
            dve.sem_inc(y_sb, 2)

            def low_w1(t, i):
                dve.wait_ge(w1h_done, t * FC + i + 1)
                part = (i // 2, slice((i % 2) * D, (i % 2 + 1) * D))
                dve.tensor_tensor(w1l[:, part[0], part[1]], raw1[:, i, :], w1h[:, part[0], part[1]].bitcast(F32),
                                  ALU.subtract).then_inc(w1l_done, 1)

            def low_rows(t, p):
                for w in range(TW):
                    cols = slice(w * P, (w + 1) * P)
                    dve.wait_ge(mTh_done, TW * t + w + 1)
                    dve.tensor_tensor(mTl[p][:, :, cols], bank[2 + w][:, :].rearrange("p (c n) -> p c n", c=KC),
                                      mTh[p][:, :, cols].bitcast(F32), ALU.subtract).then_inc(mTl_done, 1)

            def output(t, p, w, first):
                dve.wait_ge(o_ps, TW * t + w + 2)
                if first:
                    dve.wait_ge(bias_loaded[p], (t - p) * 16 + 32)
                else:
                    dve.wait_ge(out_tile_stored[w], t * 16)
                dve.tensor_tensor(y_t[w][:, :], bank[4 + w][:, :], b2_t[p][:, :], ALU.add).then_inc(y_sb, 1)

            for i in range(FC):
                low_w1(0, i)
            low_rows(0, 0)

            def tile(t, p, more):
                for f in range(FC):
                    dve.wait_ge(w2h_done, t * FC + f + 1)
                    dve.tensor_tensor(w2l[:, f, :], raw2[:, f, :], w2h[:, f, :].bitcast(F32), ALU.subtract) \
                        .then_inc(w2l_done, 1)
                    dve.wait_ge(gelu_done, t * FC + f + 3)
                    dve.tensor_copy(h1h[:, f, :], h1f[f % 2][:, :]).then_inc(h1h_done, 1)
                    dve.wait_ge(h1h_done, t * FC + f + 1)
                    dve.tensor_tensor(h1l[:, f, :], h1f[f % 2][:, :], h1h[:, f, :].bitcast(F32), ALU.subtract) \
                        .then_inc(h1l_done, 1)
                if more:
                    low_rows(t + 1, 1 - p)
                for w in range(TW):
                    if more:
                        for i in range(w * FC // TW, (w + 1) * FC // TW):
                            low_w1(t + 1, i)
                    output(t, p, w, isinstance(t, int) and t == 0)

            over_tiles(dve, tile)

            for b in range(B):
                for k in range(TOP):
                    n = TOP * b + k
                    dve.wait_ge(gathered[n % NG], (n // NG + 1) * 16)
                    if k == 1:
                        dve.wait_ge(combined, TOP * b + 1)
                    dve.scalar_tensor_tensor(x_all[:, b, :], got[n % NG][:, :], weight[:, b, k:k + 1],
                                             x_all[:, b, :], ALU.mult, ALU.add).then_inc(combined, 1)


_FFN = ["q_w", "q_b", "k_w", "k_b", "v_w", "v_b", "o_w", "o_b", "router_w", "router_b", "w1", "b1", "w2", "b2"]
_INS = ["x", "ctx_1024", "g_xattn", "g_ffn"] + ["L0_xattn_" + n for n in ("w_sim", "b_sim", "W_qv", "b_qv")] \
    + ["L0_ffn_" + n for n in _FFN]
_OUTS = [((B, S, D), "float32")]


def kernel(**inputs):
    import numpy as _np
    import concourse.bacc as _bacc
    from concourse import mybir as _mybir
    from concourse.bass_utils import run_bass_kernel_spmd as _run

    nc = _bacc.Bacc("TRN2", target_bir_lowering=False, num_devices=1)
    arrays, args = {}, []
    for name in _INS:
        a = _np.ascontiguousarray(inputs[name])
        arrays[f"in_{name}_dram"] = a
        args.append(nc.dram_tensor(f"in_{name}_dram", a.shape, _mybir.dt.from_np(a.dtype), kind="ExternalInput").ap())
    for i, (shape, dtype) in enumerate(_OUTS):
        dt = _mybir.dt.from_np(_np.dtype(dtype))
        args.append(nc.dram_tensor(f"out_{i}_dram", shape, dt, kind="ExternalOutput").ap())
    build(nc, *args)
    r = _run(nc, [arrays], core_ids=[0])
    return r.results[0]["out_0_dram"]
```

```python
from collections import namedtuple
from contextlib import ExitStack

import numpy as np

import concourse.bass as bass
from concourse import mybir

F32 = mybir.dt.float32
F32R = mybir.dt.float32r
U32 = mybir.dt.uint32
ALU = mybir.AluOpType
ACT = mybir.ActivationFunctionType
AX = mybir.AxisListType

P = 128
B, S, D = 16, 100, 512
C = 722
KC = D // P
JC = -(-C // P)
JREST = C - (JC - 1) * P
NF = 3 * KC
NS = 2 * KC
H, KPH = 16, 16
LAT = H * KPH
HB = P // KPH
NB = LAT // P
HD = D // H
E, FF = 8, 2 * D
FC = FF // P
EPS = 1e-5
TOP = 2
TR = 256
TW = TR // P
NT = (TOP * B * S + E * (TR - 1)) // TR
NTE = -(-B * S // TR)
W1_ORDER = (*range(0, FC, 2), *range(1, FC, 2))
LIST = B * S + TR + 64
CLEARS = 12
CLEAR_ROWS = E * LIST // P // CLEARS


Stages = namedtuple("Stages", "cur prev route place ahead")


def chunk_rows(j):
    return P if j < JC - 1 else JREST


def apart(eng, done):
    eng.wait_ge(done, 1)


def over_batches(eng, step):
    step(0, 0)
    step(1, 1)
    with eng.Fori(1, B // 2 - 1) as i:
        step(2 * i, 0)
        step(2 * i + 1, 1)
    step(B - 2, 0)
    step(B - 1, 1)


def over_tiles(eng, step):
    step(0, 0, True)
    step(1, 1, True)
    with eng.Fori(1, NT // 2 - 1) as i:
        step(2 * i, 0, True)
        step(2 * i + 1, 1, True)
    step(NT - 2, 0, True)
    step(NT - 1, 1, False)


def over_attend_steps(eng, step):
    def flags(t):
        return Stages(cur=t < B, prev=1 <= t <= B, route=2 <= t <= B + 1, place=t >= 3, ahead=t + 1 < B)

    for t in range(4):
        step(t, t % 2, flags(t))
    with eng.Fori(2, B // 2 - 1) as i:
        step(2 * i, 0, flags(4))
        step(2 * i + 1, 1, flags(4))
    for t in range(B - 2, B + 3):
        step(t, t % 2, flags(t))


def build(nc, x, ctx_1024, g_xattn, g_ffn, w_sim, b_sim, W_qv, b_qv, q_w, q_b, k_w, k_b, v_w, v_b, o_w, o_b,
          router_w, router_b, w1, b1, w2, b2, out):
    stack = ExitStack()
    with stack:
        base = -(-nc.sbuf_base // 32) * 32
        cursor = [base]

        def place(name, shape, dt=F32):
            size = int(np.prod(shape[1:])) * 4
            t = nc.alloc_sbuf_tensor_at(name, shape, dt, offset=cursor[0])
            cursor[0] += -(-size // 32) * 32
            return t

        def sem(name):
            return stack.enter_context(nc.semaphore(name))

        ident = place("ident", [P, P])
        ones = place("ones", [P, P])
        head_mask = place("head_mask", [P, HB])
        iota_e = place("iota_e", [P, E])
        w2T = place("w2T", [P, KC])
        w3T = place("w3T", [P, KC])
        b_sim_b = place("b_sim_b", [P, 1])
        g_b = place("g_b", [P, 2])
        tg = place("tg", [P, 2])
        tg_moe = place("tg_moe", [P, 1])
        minus_half = place("minus_half", [P, B])
        stats = place("stats", [S, B, 6])
        mv = place("mv", [S, B, 2])
        var_eps = place("var_eps", [S, B])
        rstd = place("rstd", [S, B])
        nmax_all = place("nmax_all", [S, B])
        rowsim_all = place("rowsim_all", [S, B])
        rmax = place("rmax", [S, B])
        pool_max = place("pool_max", [B, 1])
        pool_maxb = place("pool_maxb", [B, S])
        pool_e = place("pool_e", [S, B])
        pool_w = place("pool_w", [S, B])
        psum_row = place("psum_row", [S, 1])
        prob_inv = place("prob_inv", [S, 1])
        qbT = place("qbT", [P, NB])
        kbT = place("kbT", [P, NB])
        b1T = place("b1T", [P, E, FC])
        router_wT = place("router_wT", [P, KC, E])
        router_bb = place("router_bb", [S, E])
        before = place("before", [P, P])
        before_e = place("before_e", [P, E, E])
        tile_row = place("tile_row", [P, NTE])
        list_row = place("list_row", [P, E])
        tile_no = place("tile_no", [P, NT])
        onehot = place("onehot", [S, B, TOP, E])
        weight = place("weight", [S, B, TOP])
        x_row = place("x_row", [S, B, TOP])
        run = place("run", [P, E])
        out_row = place("out_row", [S, B])
        pad_row = place("pad_row", [P, 1])
        item = [place(f"item{i}", [S, TOP, 2]) for i in range(2)]
        plan_i = place("plan_i", [1, 2 * NT], U32)
        hcb = [place(f"hcb{i}", [P, KC]) for i in range(2)]
        zeros = place("zeros", [P, D])
        x_all = place("x_all", [S, B, D])

        region_a = cursor[0]
        W_hc = place("W_hc", [P, KC, D])
        W_bar = place("W_bar", [P, KC, D])
        Wh = place("Wh", [P, NS, D], F32R)
        Wl = place("Wl", [P, NS, D], F32R)
        fT = place("fT", [P, B, 2 * KC, S])
        diag = place("diag", [S, S])
        scaled = place("scaled", [P, KC, S])
        region_s = cursor[0]
        wstage = [place(f"wstage{i}", [P, D]) for i in range(2)]
        region_b = cursor[0]
        ctx = [place(f"ctx{i}", [P, JC, D]) for i in range(2)]
        ctxTh = place("ctxTh", [P, KC, C + 2], F32R)
        ctxTl = place("ctxTl", [P, KC, C + 2], F32R)
        hc = place("hc", [S, D])
        aT = place("aT", [P, KC, S])
        aTh = place("aTh", [P, KC, S], F32R)
        aTl = place("aTl", [P, KC, S], F32R)
        prob = place("prob", [S, C])
        probT = place("probT", [P, JC, S])
        w1_b = place("w1_b", [S, D])
        junk = place("junk", [S, D])
        end = cursor[0]
        cursor[0] = region_b
        wqk = place("wqk", [P, KC, 2 * LAT])
        wv = place("wv", [P, KC, LAT])
        fh = [place(f"fh{i}", [P, NF, S], F32R) for i in range(2)]
        fl = [place(f"fl{i}", [P, NF, S], F32R) for i in range(2)]
        prod = place("prod", [P, KC, S])
        We = place("We", [P, KC, D])
        Weh = place("Weh", [P, KC, D], F32R)
        Wel = place("Wel", [P, KC, D], F32R)
        b_qv_b = place("b_qv_b", [S, D])
        y_b = place("y_b", [S, D])
        end = max(end, cursor[0])
        cursor[0] = region_s
        wo = place("wo", [P, NB, D])
        cursor[0] = region_a
        hs = place("hs", [S, D])
        hsT = place("hsT", [P, KC, S])
        qT = place("qT", [P, NB, S])
        KTm = place("KTm", [P, NB, HB, S])
        V = [place(f"V{i}", [S, H, KPH + 1]) for i in range(2)]
        att = [place(f"att{i}", [S, HB, S]) for i in range(2)]
        attT = [place(f"attT{i}", [S, HB, S]) for i in range(2)]
        smax = [place(f"smax{i}", [S, HB]) for i in range(2)]
        den = place("den", [S, H])
        ao = place("ao", [S, H, KPH])
        aoT = place("aoT", [P, NB, S])
        mla = [place(f"mla{i}", [S, D]) for i in range(2)]
        mT = place("mT", [P, KC, S])
        logit = place("logit", [S, E])
        neg_top = place("neg_top", [S, 1])
        esum = place("esum", [S, 1])
        einv = place("einv", [S, 1])
        rp = place("rp", [S, E])
        probs = place("probs", [S, E])
        top_p = place("top_p", [S, E])
        top_i = place("top_i", [S, E], U32)
        top_f = place("top_f", [S, E])
        wsum = place("wsum", [S, 1])
        wsum2 = place("wsum2", [S, 1])
        winv = place("winv", [S, 1])
        winv2 = place("winv2", [S, 1])
        chosen = place("chosen", [S, E])
        rank_sb = place("rank_sb", [S, 2 * E])
        row_of = place("row_of", [S, E])
        picked = place("picked", [S, TOP, E])
        x_row_i = [place(f"x_row_i{i}_{k}", [S, 1], U32) for i in range(2) for k in range(TOP)]
        v_b_b = place("v_b_b", [S, LAT])
        o_b_b = place("o_b_b", [S, D])
        assert cursor[0] <= region_s
        cursor[0] = region_a
        plan = [place(f"plan{i}", [P, E]) for i in range(3)]
        plan_c = place("plan_c", [P, E, NTE])
        plan_s = place("plan_s", [P, E, E])
        plan_t = place("plan_t", [P, NT, E])
        plan_n = [place(f"plan_n{i}", [P, NT]) for i in range(5)]
        w1h = place("w1h", [P, KC, FF], F32R)
        w1l = place("w1l", [P, KC, FF], F32R)
        w2h = place("w2h", [P, FC, D], F32R)
        w2l = place("w2l", [P, FC, D], F32R)
        raw1 = place("raw1", [P, FC, D])
        raw2 = place("raw2", [P, FC, D])
        xs = place("xs", [P, TW, D])
        mTh = [place(f"mTh{i}", [P, KC, TR], F32R) for i in range(2)]
        mTl = [place(f"mTl{i}", [P, KC, TR], F32R) for i in range(2)]
        h1f = [place(f"h1f{i}", [P, TR]) for i in range(2)]
        h1h = place("h1h", [P, FC, TR], F32R)
        h1l = place("h1l", [P, FC, TR], F32R)
        b1_t = [place(f"b1_t{i}", [P, FC]) for i in range(2)]
        b2_t = [place(f"b2_t{i}", [P, D]) for i in range(2)]
        y_t = [place(f"y_t{i}", [P, D]) for i in range(TW)]
        item_t = [place(f"item_t{i}", [P, TW, 2]) for i in range(2)]
        row_f = place("row_f", [P, TW])
        row_i = [place(f"row_i{i}", [P, TW, 1], U32) for i in range(2)]
        end = max(end, cursor[0])
        assert end <= nc.sbuf_usable_end, (end, nc.sbuf_usable_end)

        lists = nc.dram_tensor("lists", [E * LIST, D], F32).ap()
        items = nc.dram_tensor("items", [E * LIST, 2], F32).ap()
        total = nc.dram_tensor("total", [P + B * S, D], F32).ap()
        b1_rows = nc.dram_tensor("b1_rows", [E, P, FC], F32).ap()

        bank = [stack.enter_context(nc.psum_tensor(f"bank{i}", [P, 512], F32)) for i in range(6)]
        pair = stack.enter_context(nc.psum_tensor("pair", [P, 2, 512], F32))

        ao_bank = bank[5][0:S, 0:H * (KPH + 1)]
        aoT_bank = bank[5][:, H * (KPH + 1):H * (KPH + 1) + NB * S]
        logit_bank = bank[1][0:S, 4 * S:4 * S + E]
        rank_bank = bank[1][0:S, 4 * S + E:4 * S + 3 * E]

        x_loaded = [sem(f"x_loaded{g}") for g in range(4)]
        cross_consts_loaded = sem("cross_consts_loaded")
        consts_loaded = sem("consts_loaded")
        ctx_loaded = [sem(f"ctx_loaded{i}") for i in range(2)]
        wstage_loaded = [sem(f"wstage_loaded{i}") for i in range(2)]
        attw_loaded = sem("attw_loaded")
        attb_loaded = sem("attb_loaded")
        bqv_loaded = sem("bqv_loaded")
        out_stored = sem("out_stored")
        pool_const = sem("pool_const")
        w_split = sem("w_split")
        gate_done = sem("gate_done")
        dve_step = sem("dve_step")
        var_done = sem("var_done")
        rstd_done = sem("rstd_done")
        hc_ready = sem("hc_ready")
        rowsim_done = sem("rowsim_done")
        hq_half = sem("hq_half")
        hcT_ps = sem("hcT_ps")
        hcT_sb = sem("hcT_sb")
        aT_ready = sem("aT_ready")
        ctxT_ps = sem("ctxT_ps")
        ctxTh_done = sem("ctxTh_done")
        ctxTl_done = sem("ctxTl_done")
        aTh_done = sem("aTh_done")
        aTl_done = sem("aTl_done")
        sim_done = sem("sim_done")
        max_done = sem("max_done")
        exp_done = sem("exp_done")
        inv_done = sem("inv_done")
        prob_done = sem("prob_done")
        probT_ps = sem("probT_ps")
        probT_sb = sem("probT_sb")
        hq_ps = sem("hq_ps")
        hq_sb = sem("hq_sb")
        pool_a = sem("pool_a")
        pool_b = sem("pool_b")
        pool_c = sem("pool_c")
        pool_exp = sem("pool_exp")
        pool_d = sem("pool_d")
        pool_ps = sem("pool_ps")
        diag_done = sem("diag_done")
        eb_done = sem("eb_done")
        scaled_done = sem("scaled_done")
        hcb_done = sem("hcb_done")
        W_hc_loaded = sem("W_hc_loaded")
        W_scaled = sem("W_scaled")
        We_done = sem("We_done")
        Weh_done = sem("Weh_done")
        Wel_done = sem("Wel_done")
        prod_done = sem("prod_done")
        fh_lowhalf = sem("fh_lowhalf")
        fh_highhalf = sem("fh_highhalf")
        fl_lowhalf = sem("fl_lowhalf")
        fl_highhalf = sem("fl_highhalf")
        y_done = sem("y_done")
        y_biased = sem("y_biased")
        x1_done = sem("x1_done")
        stats2_done = sem("stats2_done")
        hs_ready = sem("hs_ready")
        hsT_ps = sem("hsT_ps")
        hsT_sb = sem("hsT_sb")
        qk_ps = sem("qk_ps")
        q_sb = sem("q_sb")
        k_sb = sem("k_sb")
        v_ps = sem("v_ps")
        v_sb = sem("v_sb")
        sc_ps = sem("sc_ps")
        smax_done = sem("smax_done")
        sub_done = sem("sub_done")
        att_exp = sem("att_exp")
        attT_ps = sem("attT_ps")
        attT_sb = sem("attT_sb")
        av_ps = sem("av_ps")
        den_done = sem("den_done")
        ao_sb = sem("ao_sb")
        aoT_ps = sem("aoT_ps")
        aoT_sb = sem("aoT_sb")
        mla_ps = sem("mla_ps")
        mla_sb = sem("mla_sb")
        mT_ps = sem("mT_ps")
        mT_sb = sem("mT_sb")
        lg_ps = sem("lg_ps")
        rank_ps = sem("rank_ps")
        lg_sb = sem("lg_sb")
        base_done = sem("base_done")
        rank_read = sem("rank_read")
        neg_top_done = sem("neg_top_done")
        router_exp = sem("router_exp")
        einv_done = sem("einv_done")
        probs_done = sem("probs_done")
        top_done = sem("top_done")
        index_done = sem("index_done")
        index_f = sem("index_f")
        onehot_done = sem("onehot_done")
        chosen_done = sem("chosen_done")
        wsum_done = sem("wsum_done")
        wsum2_done = sem("wsum2_done")
        winv_done = sem("winv_done")
        winv2_done = sem("winv2_done")
        weight_done = sem("weight_done")
        row_done = sem("row_done")
        row2_done = sem("row2_done")
        run_done = sem("run_done")
        picked_done = sem("picked_done")
        x_row_done = sem("x_row_done")
        x_index_done = sem("x_index_done")
        scattered = [sem(f"scattered{i}") for i in range(2)]
        lists_cleared = sem("lists_cleared")
        b1_stored = sem("b1_stored")
        plan_done = sem("plan_done")
        xs_loaded = sem("xs_loaded")
        raw1_loaded = [sem(f"raw1_loaded{i}") for i in range(2)]
        raw2_loaded = sem("raw2_loaded")
        bias_loaded = [sem(f"bias_loaded{i}") for i in range(2)]
        items_loaded = [sem(f"items_loaded{i}") for i in range(2)]
        base_stored = sem("base_stored")
        item_done = sem("item_done")
        row_max_done = sem("row_max_done")
        row_ready = sem("row_ready")
        y_weighted = sem("y_weighted")
        added = [sem(f"added{i}") for i in range(TW)]
        xT_ps = sem("xT_ps")
        mTh_done = sem("mTh_done")
        mTl_done = sem("mTl_done")
        w1h_done = sem("w1h_done")
        w1l_done = sem("w1l_done")
        w2h_done = sem("w2h_done")
        w2l_done = sem("w2l_done")
        h_ps = sem("h_ps")
        gelu_done = sem("gelu_done")
        h1h_done = sem("h1h_done")
        h1l_done = sem("h1l_done")
        o_ps = sem("o_ps")
        y_sb = sem("y_sb")

        block = stack.enter_context(nc.Block())

        x_v = x.rearrange("b s d -> s b d")
        out_v = out.rearrange("b s d -> s b d")
        W_v = W_qv.rearrange("(c p) n -> c p n", p=P)
        q_used = q_w.rearrange("(c p) (h t k) -> c t p h k", p=P, t=HD // KPH, k=KPH)
        N_CONSTS = 3 + E + H
        N_CROSS = 6
        NPOOL = 19
        N_ATTW = 3 * KC + 1

        @block.sync
        def _(sp):
            with nc.allow_non_contiguous_dma(reason="short vectors laid over partitions"):
                def load_x(g):
                    sp.dma_start(x_all[:, 4 * g:4 * g + 4, :], x_v[:, 4 * g:4 * g + 4, :]).then_inc(x_loaded[g], 16)

                load_x(0)
                for dst, src in ((w1_b[:, :], w_sim[0:D].partition_broadcast(S)),
                                 (w2T[:, :], w_sim[D:2 * D].rearrange("(c p) -> p c", p=P)),
                                 (w3T[:, :], w_sim[2 * D:3 * D].rearrange("(c p) -> p c", p=P)),
                                 (b_sim_b[:, :], b_sim.partition_broadcast(P)),
                                 (g_b[:, 0:1], g_xattn.partition_broadcast(P)),
                                 (g_b[:, 1:2], g_ffn.partition_broadcast(P))):
                    sp.dma_start(dst, src).then_inc(cross_consts_loaded, 16)
                n = 0

                def const(dst, src):
                    nonlocal n
                    n += 1
                    sp.dma_start(dst, src).then_inc(consts_loaded, 16)


                def load_ctx(b, p):
                    full = (JC - 1) * P
                    even = JREST - JREST % 16
                    for half, done in enumerate((hq_half, hq_ps)):
                        cols = slice(half * D // 2, (half + 1) * D // 2)
                        if not (isinstance(b, int) and b < 2):
                            sp.wait_ge(done, b - 1)
                        sp.dma_start(ctx[p][:, 0:JC - 1, cols],
                                     ctx_1024[b, 0:full, cols].rearrange("(c p) n -> p c n", p=P)) \
                            .then_inc(ctx_loaded[p], 16)
                        sp.dma_start(ctx[p][0:even, JC - 1, cols], ctx_1024[b, full:full + even, cols]) \
                            .then_inc(ctx_loaded[p], 16)
                        sp.dma_start(ctx[p][even:JREST, JC - 1, cols], ctx_1024[b, full + even:C, cols]) \
                            .then_inc(ctx_loaded[p], 16)

                load_ctx(0, 0)
                for g in range(1, 4):
                    load_x(g)
                load_ctx(1, 1)
                for dst, part in ((W_hc, 0), (W_bar, 3)):
                    sp.dma_start(dst[:, :, :], W_qv[part * D:(part + 1) * D, :].rearrange("(c p) n -> p c n", p=P)) \
                        .then_inc(W_hc_loaded, 16)
                const(router_wT[:, :, :], router_w.rearrange("(c p) e -> p c e", p=P))
                const(router_bb[:, :], router_b.partition_broadcast(S))
                const(kbT[:, :], k_b.rearrange("(g p) -> p g", p=P))
                for e in range(E):
                    const(b1T[:, e, :], b1[e].rearrange("(f p) -> p f", p=P))
                for h in range(H):
                    r = (h % HB) * KPH
                    const(qbT[r:r + KPH, h // HB:h // HB + 1], q_b[h * HD:h * HD + KPH].rearrange("(k o) -> k o", o=1))
                assert n == N_CONSTS
                with sp.Fori(1, B // 2 - 1) as i:
                    load_ctx(2 * i, 0)
                    load_ctx(2 * i + 1, 1)
                load_ctx(B - 2, 0)
                load_ctx(B - 1, 1)
                sp.wait_ge(hq_ps, B)
                sp.wait_ge(probT_sb, 2 * B)
                sp.wait_ge(pool_d, 1)
                sp.dma_start(b_qv_b[:, :], b_qv.partition_broadcast(S)).then_inc(bqv_loaded, 16)
                for c in range(KC):
                    sp.dma_start(wqk[:, c, 0:LAT].rearrange("p (h k) -> p h k", k=KPH), q_used[c, 0]) \
                        .then_inc(attw_loaded, 16)
                    sp.dma_start(wqk[:, c, LAT:2 * LAT], k_w[c * P:(c + 1) * P, :]).then_inc(attw_loaded, 16)
                    sp.dma_start(wv[:, c, :], v_w[c * P:(c + 1) * P, :]).then_inc(attw_loaded, 16)
                cleared = lists.rearrange("(p r) n -> p r n", p=P)
                sp.wait_ge(pool_const, NPOOL)
                with sp.Fori(0, CLEARS) as i:
                    sp.dma_start(cleared[:, bass.ds(i * CLEAR_ROWS, CLEAR_ROWS), :],
                                 zeros[:, :].rearrange("p (o n) -> p o n", o=1).to_broadcast([P, CLEAR_ROWS, D])) \
                        .then_inc(lists_cleared, 16)
                sp.dma_start(items.rearrange("(p r) n -> p (r n)", p=P), zeros[:, 0:2 * E * LIST // P]) \
                    .then_inc(lists_cleared, 16)
                sp.wait_ge(w_split, 2 * NS)
                sp.dma_start(wo[:, :, :], o_w[0:LAT, :].rearrange("(g p) n -> p g n", p=P)).then_inc(attw_loaded, 16)
                sp.wait_ge(y_done, B)
                sp.dma_start(v_b_b[:, :], v_b.partition_broadcast(S)).then_inc(attb_loaded, 16)
                sp.dma_start(o_b_b[:, :], o_b.partition_broadcast(S)).then_inc(attb_loaded, 16)
                sp.wait_ge(consts_loaded, N_CONSTS * 16)
                sp.dma_start(b1_rows.rearrange("e p f -> p e f"), b1T[:, :, :]).then_inc(b1_stored, 16)
                sp.wait_ge(b1_stored, 16)
                sp.wait_ge(base_done, B)
                sp.dma_start(total[P:P + B * S, :].rearrange("(b s) d -> s b d", b=B), x_all[:, :, :]) \
                    .then_inc(base_stored, 16)
                sp.dma_start(total[0:P, :], zeros[:, :]).then_inc(base_stored, 16)
                sp.wait_ge(plan_done, 1)

                def tile_expert(t):
                    return sp.value_load(plan_i[0:1, bass.ds(t, 1)], min_val=0, max_val=E - 1)

                def tile_row_of(t):
                    return sp.value_load(plan_i[0:1, bass.ds(NT + t, 1)], min_val=0, max_val=E * LIST - TR)

                def load_rows(row):
                    sp.dma_start(xs[:, :, :], lists[bass.ds(row, TR), :].rearrange("(w p) n -> p w n", p=P)) \
                        .then_inc(xs_loaded, 16)

                def load_items(row, p):
                    sp.dma_start(item_t[p][:, :, :], items[bass.ds(row, TR), :].rearrange("(w p) n -> p w n", p=P)) \
                        .then_inc(items_loaded[p], 16)

                def load_w1(e, halves=(0, 1)):
                    for a in halves:
                        sp.dma_start(raw1[:, :, :].rearrange("p (c a) n -> p c a n", c=KC)[:, :, a, :],
                                     w1[bass.ds(e, 1)].rearrange("o (c p) n -> p (o c) n", p=P)[:, :, a * D:(a + 1) * D]) \
                            .then_inc(raw1_loaded[a], 16)

                def load_biases(e, p):
                    sp.dma_start(b1_t[p][:, :], b1_rows[bass.ds(e, 1)].rearrange("o p f -> (o p) f")) \
                        .then_inc(bias_loaded[p], 16)
                    sp.dma_start(b2_t[p][:, :], b2[bass.ds(e, 1), :].to_broadcast([P, D])).then_inc(bias_loaded[p], 16)

                def load_w2(e):
                    sp.dma_start(raw2[:, :, :], w2[bass.ds(e, 1)].rearrange("o (c p) n -> p (o c) n", p=P)) \
                        .then_inc(raw2_loaded, 16)

                e0 = tile_expert(0)
                load_w1(e0, (0,))
                row0 = tile_row_of(0)
                for i in range(2):
                    sp.wait_ge(scattered[i], TOP * B * 16)
                load_rows(row0)
                load_w1(e0, (1,))
                load_items(row0, 0)
                load_biases(e0, 0)
                load_w2(e0)

                def tile(t, p, more):
                    if more:
                        e = tile_expert(t + 1)
                        sp.wait_ge(xT_ps, TW * (t + 1))
                        row = tile_row_of(t + 1)
                        load_rows(row)
                        sp.wait_ge(w1l_done, (t + 1) * FC)
                        load_w1(e)
                        sp.wait_ge(y_weighted, TW * t + 2)
                        load_items(row, 1 - p)
                        load_biases(e, 1 - p)
                        sp.wait_ge(w2l_done, (t + 1) * FC + 1)
                        load_w2(e)
                over_tiles(sp, tile)
                for w in range(TW):
                    sp.wait_ge(added[w], NT * 16)
                half = B * S // 2
                flat = out.rearrange("b s d -> (b s) d")
                for g in range(2):
                    sp.dma_start(flat[g * half:(g + 1) * half, :], total[P + g * half:P + (g + 1) * half, :]) \
                        .then_inc(out_stored, 16)
                sp.wait_ge(out_stored, 32)

        @block.gpsimd
        def _(pool):
            n = 0

            def own(ins):
                nonlocal n
                n += 1
                ins.then_inc(pool_const, 1)
                pool.wait_ge(pool_const, n)

            own(pool.memset(ident[:, :], 0.0))
            own(pool.affine_select(out=ident[:, :], in_=ident[:, :], compare_op=ALU.not_equal, fill=1.0, base=0,
                                   pattern=[[-1, P]], channel_multiplier=1))
            own(pool.memset(ones[:, :], 1.0))
            own(pool.memset(minus_half[:, :], -0.5))
            own(pool.memset(head_mask[:, :], 1.0))
            own(pool.affine_select(out=head_mask[:, :], in_=head_mask[:, :], compare_op=ALU.is_ge, fill=0.0, base=0,
                                   pattern=[[-KPH, HB]], channel_multiplier=1))
            own(pool.affine_select(out=head_mask[:, :], in_=head_mask[:, :], compare_op=ALU.is_ge, fill=0.0,
                                   base=KPH - 1, pattern=[[KPH, HB]], channel_multiplier=-1))
            own(pool.iota(iota_e[:, :], pattern=[[1, E]], base=0, channel_multiplier=0,
                          allow_small_or_imprecise_dtypes=True))
            own(pool.memset(before[:, :], 1.0))
            own(pool.affine_select(out=before[:, :], in_=before[:, :], compare_op=ALU.is_gt, fill=0.0, base=0,
                                   pattern=[[1, P]], channel_multiplier=-1))
            own(pool.memset(before_e[:, :, :], 1.0))
            own(pool.affine_select(out=before_e[:, :, :], in_=before_e[:, :, :], compare_op=ALU.is_gt, fill=0.0,
                                   base=0, pattern=[[1, E], [-1, E]], channel_multiplier=0))
            for dst, count, step in ((tile_row, NTE, TR), (list_row, E, LIST), (tile_no, NT, 1)):
                own(pool.iota(dst[:, :], pattern=[[step, count]], base=0, channel_multiplier=0,
                              allow_small_or_imprecise_dtypes=True))
            own(pool.iota(out_row[:, :], pattern=[[S, B]], base=P, channel_multiplier=1,
                          allow_small_or_imprecise_dtypes=True))
            own(pool.iota(pad_row[:, :], pattern=[[1, 1]], base=0, channel_multiplier=1,
                          allow_small_or_imprecise_dtypes=True))
            own(pool.memset(run[:, :], 0.0))
            own(pool.memset(zeros[:, :], 0.0))
            for k, (first, end) in enumerate(((0, 4), (4, B))):
                pool.wait_ge(var_done, k + 1)
                pool.tensor_tensor(rstd[:, first:end], var_eps[:, first:end], minus_half[0:S, first:end], ALU.pow) \
                    .then_inc(rstd_done, 1)
            with pool.Fori(0, NS // 2) as m:
                k = 2 * m
                for i in range(2):
                    pool.dma_start(wstage[i][:, :], W_v[k + KC + i]).then_inc(wstage_loaded[i], 16)
                for i in range(2):
                    pool.wait_ge(wstage_loaded[i], k * 8 + 16)
                    pool.tensor_copy(Wh[:, k + i, :], wstage[i][:, :]).then_inc(w_split, 1)
                    pool.wait_ge(w_split, k * 2 + 2 * i + 1)
                    pool.tensor_tensor(Wl[:, k + i, :], wstage[i][:, :], Wh[:, k + i, :].bitcast(F32), ALU.subtract) \
                        .then_inc(w_split, 1)
                pool.wait_ge(w_split, k * 2 + 4)
            pool.wait_ge(W_hc_loaded, 32)

            def effective_w(b, p):
                for c in range(KC):
                    pool.wait_ge(W_scaled, KC * b + c + 1)
                    pool.tensor_tensor(We[:, c, :], We[:, c, :], W_hc[:, c, :], ALU.add).then_inc(We_done, 1)

            over_batches(pool, effective_w)
            for k, (first, end) in enumerate(((0, B // 2), (B // 2, B))):
                pool.wait_ge(var_done, k + 3)
                pool.tensor_tensor(rstd[:, first:end], var_eps[:, first:end], minus_half[0:S, first:end], ALU.pow) \
                    .then_inc(rstd_done, 1)
            pool.wait_ge(lists_cleared, (CLEARS + 1) * 16)
            for b in range(B):
                for k in range(TOP):
                    pool.wait_ge(x_index_done, TOP * b + k + 1)
                    pool.indirect_dma_start(lists[:, :], bass.IndirectOffsetOnAxis(ap=x_row_i[TOP * (b % 2) + k][:, :], axis=0),
                                            mla[b % 2][:, :], None).then_inc(scattered[b % 2], 16)
                pool.wait_ge(item_done, b + 1)
                for k in range(TOP):
                    pool.indirect_dma_start(items[:, :], bass.IndirectOffsetOnAxis(ap=x_row_i[TOP * (b % 2) + k][:, :], axis=0),
                                            item[b % 2][:, k, :], None).then_inc(scattered[b % 2], 16)
            pool.wait_ge(base_stored, 32)
            for t in range(NT):
                for w in range(TW):
                    pool.wait_ge(y_weighted, TW * t + w + 3)
                    if t + w > 0:
                        pool.wait_ge(added[1 - w], (t + w) * 16)
                    pool.indirect_dma_start(total[:, :], bass.IndirectOffsetOnAxis(ap=row_i[t % 2][:, w, :], axis=0),
                                            y_t[w][:, :], None, compute_op=ALU.add).then_inc(added[w], 16)

        @block.scalar
        def _(act):
            act.wait_ge(cross_consts_loaded, N_CROSS * 16)
            act.preload_act_table(ACT.Exp)
            act.activation(tg[:, :], g_b[:, :], ACT.Tanh).then_inc(gate_done, 1)

            def high_ctxT(nb, chunks):
                for j in chunks:
                    act.wait_ge(ctxT_ps, nb * JC + j + 1)
                    r = chunk_rows(j)
                    act.activation(ctxTh[:, :, j * P:j * P + r],
                                   bank[1 + j % 4][:, :].rearrange("p (c n) -> p c n", c=KC)[:, :, 0:r],
                                   ACT.Copy).then_inc(ctxTh_done, 1)

            def high_aT(nb):
                act.wait_ge(aT_ready, nb + 1)
                act.activation(aTh[:, :, :], aT[:, :, :], ACT.Copy).then_inc(aTh_done, 1)

            high_ctxT(0, range(JC))
            high_aT(0)

            def cross(b, p):
                last = isinstance(b, int) and b == B - 1
                if not last:
                    high_ctxT(b + 1, (0,))
                apart(act, pool_const)
                act.wait_ge(max_done, b + 1)
                act.wait_ge(probT_ps, 2 * b)
                act.activation(prob[:, :].rearrange("s (u n) -> s u n", u=2), pair[0:S, :, 0:C // 2], ACT.Exp,
                               bias=nmax_all[:, bass.ds(b, 1)],
                               accum_out=psum_row[:, :]).then_inc(exp_done, 1)
                if not last:
                    high_ctxT(b + 1, (1, 2, 3))
                for u in range(2):
                    act.wait_ge(probT_ps, 2 * b + u + 1)
                    act.wait_ge(hq_ps, b)
                    act.activation(probT[:, 3 * u:3 * u + 2, :],
                                   pair[:, u, 0:2 * S].rearrange("p (c s) -> p c s", c=2), ACT.Copy)
                    r = chunk_rows(3 * u + 2)
                    act.activation(probT[0:r, 3 * u + 2, :], pair[0:r, u, 2 * S:3 * S], ACT.Copy) \
                        .then_inc(probT_sb, 1)
                if not last:
                    high_ctxT(b + 1, (4, 5))
                    high_aT(b + 1)
                else:
                    act.wait_ge(pool_c, 1)
                    act.activation(pool_e[:, :], pool_e[:, :], ACT.Exp).then_inc(pool_exp, 1)
                apart(act, pool_const)
                act.wait_ge(hq_ps, b + 1)
                act.activation(fT[:, b, KC:2 * KC, :], bank[5][:, 0:KC * S].rearrange("p (c s) -> p c s", c=KC),
                               ACT.Copy).then_inc(hq_sb, 1)

            over_batches(act, cross)

            def round_first(nb, q):
                if not (isinstance(nb, int) and nb < 2):
                    act.wait_ge(y_done, nb - 1)
                apart(act, pool_const)
                act.wait_ge(hq_sb, nb + 1)
                act.activation(fh[q][:, 0:2 * KC, :], fT[:, nb, :, :], ACT.Copy).then_inc(fh_lowhalf, 1)

            def scale_w(nb, q):
                act.wait_ge(hcb_done, nb + 1)
                if not (isinstance(nb, int) and nb == 0):
                    act.wait_ge(Wel_done, KC * nb)
                for c in range(KC):
                    act.activation(We[:, c, :], W_bar[:, c, :], ACT.Copy, scale=hcb[q][:, c:c + 1]) \
                        .then_inc(W_scaled, 1)

            def round_second(nb, q):
                act.wait_ge(prod_done, nb + 1)
                act.activation(fh[q][:, 2 * KC:NF, :], prod[:, :, :], ACT.Copy).then_inc(fh_highhalf, 1)

            act.wait_ge(pool_d, 1)
            act.wait_ge(W_hc_loaded, 32)
            scale_w(0, 0)
            round_first(0, 0)
            round_second(0, 0)

            def project(b, p):
                if not (isinstance(b, int) and b == 0):
                    act.wait_ge(y_done, b)
                for c in range(KC):
                    act.wait_ge(We_done, KC * b + c + 1)
                    act.activation(Weh[:, c, :], We[:, c, :], ACT.Copy).then_inc(Weh_done, 1)
                if not (isinstance(b, int) and b == B - 1):
                    round_first(b + 1, 1 - p)
                    round_second(b + 1, 1 - p)
                    scale_w(b + 1, 1 - p)

            over_batches(act, project)

            def attT_to_sbuf(b, u):
                act.wait_ge(attT_ps, 2 * b + u + 1)
                act.activation(attT[u][:, :, :].rearrange("s (u h) n -> s u h n", u=2),
                               pair[0:S, :, 0:4 * S].rearrange("s u (h n) -> s u h n", h=4), ACT.Copy) \
                    .then_inc(attT_sb, 1)

            def exponentials(t, u):
                act.wait_ge(sub_done, 2 * t + u + 1)
                act.activation(att[u][:, :, :], att[u][:, :, :], ACT.Exp, scale=float(KPH) ** -0.5) \
                    .then_inc(att_exp, 1)

            def hsT_to_sbuf(b):
                act.wait_ge(hsT_ps, b + 1)
                act.activation(hsT[:, :, :], bank[4][:, 0:KC * S].rearrange("p (c s) -> p c s", c=KC), ACT.Copy) \
                    .then_inc(hsT_sb, 1)

            hsT_to_sbuf(0)

            def attend(t, p, do):
                if do.route:
                    act.wait_ge(mT_ps, t - 1)
                    act.activation(mT[:, :, :], bank[0][:, 0:KC * S].rearrange("p (c s) -> p c s", c=KC), ACT.Copy) \
                        .then_inc(mT_sb, 1)
                if do.prev:
                    attT_to_sbuf(t - 1, 0)
                if do.route:
                    act.wait_ge(neg_top_done, t - 1)
                    act.activation(rp[:, :], logit[:, :], ACT.Exp, bias=neg_top[:, :], accum_out=esum[:, :]) \
                        .then_inc(router_exp, 1)
                if do.prev:
                    attT_to_sbuf(t - 1, 1)
                if do.cur:
                    exponentials(t, 0)
                if do.prev:
                    act.wait_ge(aoT_ps, t)
                    act.activation(aoT[:, :, :], aoT_bank.rearrange("p (g s) -> p g s", g=NB), ACT.Copy) \
                        .then_inc(aoT_sb, 1)
                if do.ahead:
                    hsT_to_sbuf(t + 1)
                if do.cur:
                    exponentials(t, 1)

            over_attend_steps(act, attend)

            act.sem_inc(gelu_done, 2)
            act.preload_act_table(ACT.Gelu)
            for i in range(2):
                act.wait_ge(scattered[i], TOP * B * 16)

            def high_w1(t):
                act.wait_ge(h_ps, t * FC + 1)
                for i in W1_ORDER:
                    if i < 2:
                        act.wait_ge(raw1_loaded[i], (t + 1) * 16)
                    act.activation(w1h[:, i // 2, (i % 2) * D:(i % 2 + 1) * D], raw1[:, i, :], ACT.Copy) \
                        .then_inc(w1h_done, 1)

            def high_rows(t, p):
                act.wait_ge(xT_ps, TW * (t + 1))
                for w in range(TW):
                    act.activation(mTh[p][:, :, w * P:(w + 1) * P], bank[2 + w][:, :].rearrange("p (c n) -> p c n", c=KC),
                                   ACT.Copy).then_inc(mTh_done, 1)

            high_rows(0, 0)
            high_w1(0)

            def tile(t, p, more):
                act.wait_ge(bias_loaded[p], (t - p) * 16 + 32)
                act.wait_ge(raw2_loaded, (t + 1) * 16)
                act.wait_ge(o_ps, TW * t + 1)
                for f in range(FC):
                    act.activation(w2h[:, f, :], raw2[:, f, :], ACT.Copy).then_inc(w2h_done, 1)
                    act.wait_ge(h_ps, t * FC + f + 2)
                    act.wait_ge(h1l_done, t * FC + f + 1)
                    act.activation(h1f[f % 2][:, :], bank[f % 2][:, 0:TR], ACT.Gelu, bias=b1_t[p][:, f:f + 1]) \
                        .then_inc(gelu_done, 1)
                if more:
                    high_rows(t + 1, 1 - p)
                    high_w1(t + 1)

            over_tiles(act, tile)

        @block.tensor
        def _(pe):
            pe.wait_ge(pool_const, NPOOL)

            def pool_step(n):
                if n == 1:
                    pe.wait_ge(pool_a, 1)
                    nc.tensor.transpose(bank[0][0:B, 0:S], rmax[:, :], ident[0:S, 0:S]).then_inc(pool_ps, 1)
                elif n == 2:
                    pe.wait_ge(pool_b, 1)
                    nc.tensor.transpose(bank[0][0:S, 0:B], pool_maxb[:, :], ident[0:B, 0:B]).then_inc(pool_ps, 1)
                else:
                    pe.wait_ge(pool_exp, 1)
                    nc.tensor.matmul(bank[0][:, 0:B], ones[0:S, :], pool_e[:, :], start=True, stop=True) \
                        .then_inc(pool_ps, 1)

            def hc_transposes(nb):
                pe.wait_ge(hc_ready, nb + 1)
                pe.wait_ge(aT_ready, nb)
                for c in range(KC):
                    t = nc.tensor.transpose(bank[0][:, c * S:(c + 1) * S], hc[:, c * P:(c + 1) * P], ident[0:S, 0:S])
                t.then_inc(hcT_ps, 1)

            def ctx_transposes(nb, p, chunks):
                pe.wait_ge(ctx_loaded[p], (nb - p) * 48 + 96)
                for j in chunks:
                    r = chunk_rows(j)
                    if j >= 4 or not isinstance(nb, int) or nb > 0:
                        pe.wait_ge(ctxTl_done, nb * JC + max(j - 3, 0))
                    for c in range(KC):
                        t = nc.tensor.transpose(bank[1 + j % 4][:, c * P:c * P + r], ctx[p][0:r, j, c * P:(c + 1) * P],
                                                ident[0:r, 0:r])
                    t.then_inc(ctxT_ps, 1)

            ctx_transposes(0, 0, range(JC))
            hc_transposes(0)

            def cross(b, p):
                last = isinstance(b, int) and b == B - 1
                pe.wait_ge(aTl_done, b + 1)
                pe.wait_ge(ctxTl_done, (b + 1) * JC)
                pe.wait_ge(probT_sb, 2 * b)
                for u in range(2):
                    for c in range(KC):
                        dst = pair[0:S, u, 0:C // 2 + 1]
                        high, low = (w[:, c, u * (C // 2):(u + 1) * (C // 2) + 1] for w in (ctxTh, ctxTl))
                        nc.tensor.matmul(dst, aTl[:, c, :], high, start=(c == 0), stop=False)
                        nc.tensor.matmul(dst, aTh[:, c, :], low, start=False, stop=False)
                        t = nc.tensor.matmul(dst, aTh[:, c, :], high, start=False, stop=(c == KC - 1))
                t.then_inc(sim_done, 1)
                if not last:
                    ctx_transposes(b + 1, 1 - p, range(4))
                    hc_transposes(b + 1)
                pe.wait_ge(prob_done, b + 1)
                for u in range(2):
                    for i in range(3):
                        j = 3 * u + i
                        r = chunk_rows(j)
                        t = nc.tensor.transpose(pair[0:r, u, i * S:(i + 1) * S], prob[:, j * P:j * P + r],
                                                ident[0:S, 0:S])
                    t.then_inc(probT_ps, 1)
                if not last:
                    ctx_transposes(b + 1, 1 - p, range(4, JC))
                pe.wait_ge(probT_sb, 2 * b + 2)
                pe.wait_ge(hq_sb, b)
                for c in range(KC):
                    if last and c > 0:
                        pool_step(c)
                    for j in range(JC):
                        r = chunk_rows(j)
                        t = nc.tensor.matmul(bank[5][:, c * S:(c + 1) * S], ctx[p][0:r, j, c * P:(c + 1) * P],
                                             probT[0:r, j, :], start=(j == 0), stop=(j == JC - 1))
                    if c == KC // 2 - 1:
                        t.then_inc(hq_half, 1)
                t.then_inc(hq_ps, 1)

            over_batches(pe, cross)

            def weights_of(nb):
                pe.wait_ge(diag_done, nb + 1)
                nc.tensor.matmul(bank[2][:, 0:S], ones[0:S, :], diag[:, :], start=True, stop=True).then_inc(eb_done, 1)

            weights_of(0)

            def project(b, p):
                pe.wait_ge(w_split, 2 * NS)
                pe.wait_ge(fh_highhalf, b + 1)
                pe.wait_ge(fl_highhalf, b + 1)
                if not (isinstance(b, int) and b < 2):
                    pe.wait_ge(y_biased, b - 1)
                if not (isinstance(b, int) and b == B - 1):
                    weights_of(b + 1)
                for k in (*range(KC, NF), *range(KC)):
                    if k >= KC:
                        wh, wl = Wh[:, k - KC, :], Wl[:, k - KC, :]
                    else:
                        pe.wait_ge(Weh_done, KC * b + k + 1)
                        pe.wait_ge(Wel_done, KC * b + k + 1)
                        wh, wl = Weh[:, k, :], Wel[:, k, :]
                    nc.tensor.matmul(bank[p][0:S, :], fl[p][:, k, :], wh, start=(k == KC), stop=False)
                    nc.tensor.matmul(bank[p][0:S, :], fh[p][:, k, :], wl, start=False, stop=False)
                    t = nc.tensor.matmul(bank[p][0:S, :], fh[p][:, k, :], wh, start=False, stop=(k == KC - 1))
                t.then_inc(y_done, 1)

            over_batches(pe, project)

            def att_transposes(b, u):
                pe.wait_ge(att_exp, 2 * b + u + 1)
                if not (isinstance(b, int) and b == 0 and u == 0):
                    pe.wait_ge(attT_sb, 2 * b + u)
                for h in range(HB):
                    m = nc.tensor.transpose(pair[0:S, h // 4, (h % 4) * S:(h % 4 + 1) * S], att[u][:, h, :],
                                            ident[0:S, 0:S])
                m.then_inc(attT_ps, 1)

            def scores(t, u):
                pe.wait_ge(q_sb, t + 1)
                pe.wait_ge(k_sb, 2 * t + u + 1)
                for i in range(2):
                    m = nc.tensor.matmul(bank[2 * u + i][0:S, 0:4 * S], qT[:, u, :],
                                         KTm[:, u, 4 * i:4 * i + 4, :].rearrange("p h s -> p (h s)"),
                                         start=True, stop=True)
                m.then_inc(sc_ps, 1)

            def mix(b, p, u):
                pe.wait_ge(attT_sb, 2 * b + u + 1)
                for h in range(HB * u, HB * (u + 1)):
                    m = nc.tensor.matmul(ao_bank[:, h * (KPH + 1):(h + 1) * (KPH + 1)], attT[u][:, h % HB, :],
                                         V[p][:, h, :], start=True, stop=True)
                return m

            def hs_transposes(b):
                pe.wait_ge(hs_ready, b + 1)
                if not (isinstance(b, int) and b == 0):
                    pe.wait_ge(q_sb, b)
                    pe.wait_ge(k_sb, 2 * b)
                for c in range(KC):
                    m = nc.tensor.transpose(bank[4][:, c * S:(c + 1) * S], hs[:, c * P:(c + 1) * P], ident[0:S, 0:S])
                m.then_inc(hsT_ps, 1)

            hs_transposes(0)

            def attend(t, p, do):
                if do.cur:
                    pe.wait_ge(attw_loaded, N_ATTW * 16)
                    pe.wait_ge(hsT_sb, t + 1)
                    for g in range(2 * NB):
                        for c in range(KC):
                            m = nc.tensor.matmul(bank[4][:, g * S:(g + 1) * S], wqk[:, c, g * P:(g + 1) * P],
                                                 hsT[:, c, :], start=(c == 0), stop=(c == KC - 1))
                    m.then_inc(qk_ps, 1)
                if do.route:
                    pe.wait_ge(mla_sb, t - 1)
                    for c in range(KC):
                        m = nc.tensor.transpose(bank[0][:, c * S:(c + 1) * S], mla[p][:, c * P:(c + 1) * P],
                                                ident[0:S, 0:S])
                    m.then_inc(mT_ps, 1)
                if do.prev:
                    att_transposes(t - 1, 0)
                if do.cur:
                    if do.prev:
                        pe.wait_ge(sub_done, 2 * t)
                    for c in range(KC):
                        m = nc.tensor.matmul(bank[2][0:S, 0:LAT], hsT[:, c, :], wv[:, c, :], start=(c == 0),
                                             stop=(c == KC - 1))
                    m.then_inc(v_ps, 1)
                if do.route:
                    pe.wait_ge(mT_sb, t - 1)
                    if do.place:
                        pe.wait_ge(lg_sb, t - 2)
                        pe.wait_ge(rank_read, t - 2)
                    for c in range(KC):
                        m = nc.tensor.matmul(logit_bank, mT[:, c, :], router_wT[:, c, :], start=(c == 0),
                                             stop=(c == KC - 1))
                    m.then_inc(lg_ps, 1)
                if do.prev:
                    att_transposes(t - 1, 1)
                    pe.wait_ge(v_sb, t)
                    if do.route:
                        pe.wait_ge(aoT_sb, t - 1)
                    mix(t - 1, 1 - p, 0)
                if do.cur:
                    if do.route:
                        pe.wait_ge(mT_sb, t - 1)
                        pe.wait_ge(lg_sb, t - 1)
                    if do.prev:
                        pe.wait_ge(sub_done, 2 * t)
                    scores(t, 0)
                if do.prev:
                    mix(t - 1, 1 - p, 1).then_inc(av_ps, 1)
                if do.cur:
                    pe.wait_ge(v_sb, t + 1)
                    scores(t, 1)
                if do.prev:
                    pe.wait_ge(ao_sb, t)
                    if do.route:
                        pe.wait_ge(aoT_sb, t - 1)
                    for g in range(NB):
                        m = nc.tensor.transpose(aoT_bank[:, g * S:(g + 1) * S],
                                                ao[:, g * HB:(g + 1) * HB, :].rearrange("s h k -> s (h k)"),
                                                ident[0:S, 0:S])
                    m.then_inc(aoT_ps, 1)
                if do.ahead:
                    hs_transposes(t + 1)
                if do.route:
                    pe.wait_ge(chosen_done, t - 1)
                    pe.wait_ge(lg_sb, t - 1)
                    if do.cur:
                        pe.wait_ge(sub_done, 2 * t + 1)
                    nc.tensor.matmul(rank_bank[:, 0:E], before[0:S, 0:S], chosen[:, :], start=True, stop=True)
                    nc.tensor.matmul(rank_bank[:, E:2 * E], ones[0:S, 0:S], chosen[:, :], start=True, stop=True) \
                        .then_inc(rank_ps, 1)
                if do.prev:
                    pe.wait_ge(aoT_sb, t)
                    if do.cur:
                        pe.wait_ge(sub_done, 2 * t + 1)
                    for g in range(NB):
                        m = nc.tensor.matmul(bank[0][0:S, :], aoT[:, g, :], wo[:, g, :], start=(g == 0),
                                             stop=(g == NB - 1))
                    m.then_inc(mla_ps, 1)

            over_attend_steps(pe, attend)

            pe.sem_inc(h_ps, 1)
            pe.sem_inc(o_ps, 1)

            def rows_of(t):
                pe.wait_ge(xs_loaded, (t + 1) * 16)
                for w in range(TW):
                    for c in range(KC):
                        m = nc.tensor.transpose(bank[2 + w][:, c * P:(c + 1) * P], xs[:, w, c * P:(c + 1) * P],
                                                ident[:, :])
                    m.then_inc(xT_ps, 1)

            rows_of(0)

            def tile(t, p, more):
                pe.wait_ge(mTh_done, TW * (t + 1))
                pe.wait_ge(mTl_done, TW * (t + 1))
                for f in range(FC):
                    if f % (FC // 2) == 0:
                        pe.wait_ge(w1h_done, FC * t + f + FC // 2)
                        pe.wait_ge(w1l_done, FC * t + f + FC // 2)
                    pe.wait_ge(gelu_done, t * FC + f + 1)
                    for c in range(KC):
                        wh, wl = (w[:, c, f * P:(f + 1) * P] for w in (w1h, w1l))
                        nc.tensor.matmul(bank[f % 2][:, 0:TR], wl, mTh[p][:, c, :], start=(c == 0), stop=False)
                        nc.tensor.matmul(bank[f % 2][:, 0:TR], wh, mTl[p][:, c, :], start=False, stop=False)
                        m = nc.tensor.matmul(bank[f % 2][:, 0:TR], wh, mTh[p][:, c, :], start=False,
                                             stop=(c == KC - 1))
                    m.then_inc(h_ps, 1)
                if more:
                    rows_of(t + 1)
                for w in range(TW):
                    pe.wait_ge(y_sb, TW * t + w + 1)
                    for f in range(FC):
                        if w == 0:
                            pe.wait_ge(h1l_done, t * FC + f + 3)
                            pe.wait_ge(w2l_done, t * FC + f + 2)
                        hh, hl = (h[:, f, w * P:(w + 1) * P] for h in (h1h, h1l))
                        nc.tensor.matmul(bank[4 + w][:, :], hl, w2h[:, f, :], start=(f == 0), stop=False)
                        nc.tensor.matmul(bank[4 + w][:, :], hh, w2l[:, f, :], start=False, stop=False)
                        m = nc.tensor.matmul(bank[4 + w][:, :], hh, w2h[:, f, :], start=False, stop=(f == FC - 1))
                    m.then_inc(o_ps, 1)

            over_tiles(pe, tile)

        @block.vector
        def _(dve):
            n = 0

            def own(ins):
                nonlocal n
                n += 1
                ins.then_inc(dve_step, 1)
                dve.wait_ge(dve_step, n)

            def row_stats(first, end):
                for b in range(first, end):
                    ins = dve.bn_aggr(mv[:, b, :], stats[:, b, :])
                own(ins)
                dve.tensor_scalar(var_eps[:, first:end], mv[:, first:end, 1], EPS, None, ALU.add).then_inc(var_done, 1)

            def first_stats(first, end):
                for b in range(first, end):
                    if b % 4 == 0:
                        dve.wait_ge(x_loaded[b // 4], 16)
                    ins = dve.bn_stats(stats[:, b, :], x_all[:, b, :])
                own(ins)
                row_stats(first, end)

            first_stats(0, 4)
            dve.wait_ge(cross_consts_loaded, N_CROSS * 16)
            dve.wait_ge(rstd_done, 1)

            def normalise(dst, b, done):
                dve.tensor_scalar(dst, x_all[:, b, :], mv[:, b, 0:1], rstd[:, bass.ds(b, 1)], ALU.subtract, ALU.mult) \
                    .then_inc(done, 1)

            def next_hc(nb):
                dve.wait_ge(hcT_ps, nb)
                normalise(hc[:, :], nb, hc_ready)
                dve.wait_ge(hc_ready, nb + 1)
                dve.scalar_tensor_tensor(junk[:, :], hc[:, :], 1.0, w1_b[:, :], ALU.mult, ALU.mult,
                                         accum_out=rowsim_all[:, bass.ds(nb, 1)]).then_inc(rowsim_done, 1)

            def next_aT(nb):
                src = bank[0][:, 0:KC * S].rearrange("p (c s) -> p c s", c=KC)
                apart(dve, pool_const)
                dve.wait_ge(hcT_ps, nb + 1)
                dve.tensor_copy(fT[:, nb, 0:KC, :], src).then_inc(hcT_sb, 1)
                dve.wait_ge(sim_done, nb)
                for c in range(KC):
                    ins = dve.tensor_scalar(aT[:, c, :], src[:, c, :], w3T[:, c:c + 1], w2T[:, c:c + 1], ALU.mult,
                                            ALU.add)
                ins.then_inc(aT_ready, 1)

            def low_ctxT(nb, chunks):
                for j in chunks:
                    dve.wait_ge(ctxTh_done, nb * JC + j + 1)
                    r = chunk_rows(j)
                    dve.tensor_tensor(ctxTl[:, :, j * P:j * P + r],
                                      bank[1 + j % 4][:, :].rearrange("p (c n) -> p c n", c=KC)[:, :, 0:r],
                                      ctxTh[:, :, j * P:j * P + r].bitcast(F32), ALU.subtract).then_inc(ctxTl_done, 1)

            def low_aT(nb):
                dve.wait_ge(aTh_done, nb + 1)
                dve.tensor_tensor(aTl[:, :, :], aT[:, :, :], aTh[:, :, :].bitcast(F32), ALU.subtract) \
                    .then_inc(aTl_done, 1)

            for dst in (ctxTh, ctxTl):
                own(dve.tensor_copy(dst[:, :, C:C + 2], zeros[:, 0:2 * KC].rearrange("p (c n) -> p c n", c=KC)))
            next_hc(0)
            low_ctxT(0, range(JC))
            next_aT(0)
            low_aT(0)

            def cross(b, p):
                last = isinstance(b, int) and b == B - 1
                if not last:
                    next_hc(b + 1)
                apart(dve, pool_const)
                dve.wait_ge(sim_done, b + 1)
                dve.tensor_reduce(nmax_all[:, bass.ds(b, 1)], pair[0:S, :, 0:C // 2], axis=AX.XY, op=ALU.max,
                                  negate=True).then_inc(max_done, 1)
                if not last:
                    low_ctxT(b + 1, (0,))
                dve.wait_ge(exp_done, b + 1)
                dve.reciprocal(prob_inv[:, :], psum_row[:, :]).then_inc(inv_done, 1)
                dve.wait_ge(inv_done, b + 1)
                dve.tensor_scalar(prob[:, :], prob[:, :], prob_inv[:, :], None, ALU.mult).then_inc(prob_done, 1)
                if not last:
                    low_ctxT(b + 1, (1,))
                    next_aT(b + 1)
                    low_ctxT(b + 1, range(2, JC))
                    low_aT(b + 1)
                if isinstance(b, int) and b == 0:
                    first_stats(4, B)
                    dve.wait_ge(rstd_done, 2)

            over_batches(dve, cross)

            own(dve.tensor_tensor(rmax[:, :], rowsim_all[:, :], nmax_all[:, :], ALU.subtract))
            dve.tensor_scalar(rmax[:, :], rmax[:, :], b_sim_b[0:S, :], None, ALU.add).then_inc(pool_a, 1)
            dve.wait_ge(pool_ps, 1)
            own(dve.tensor_reduce(pool_max[:, :], bank[0][0:B, 0:S], axis=AX.X, op=ALU.max))
            dve.tensor_copy(pool_maxb[:, :], pool_max[:, :].to_broadcast([B, S])).then_inc(pool_b, 1)
            dve.wait_ge(pool_ps, 2)
            dve.tensor_tensor(pool_e[:, :], rmax[:, :], bank[0][0:S, 0:B], ALU.subtract).then_inc(pool_c, 1)
            dve.wait_ge(pool_ps, 3)
            own(dve.reciprocal(pool_w[:, :], bank[0][0:S, 0:B]))
            dve.tensor_tensor(pool_w[:, :], pool_w[:, :], pool_e[:, :], ALU.mult).then_inc(pool_d, 1)
            dve.wait_ge(pool_d, 1)

            def diag_of(nb):
                dve.wait_ge(eb_done, nb)
                dve.tensor_scalar(diag[:, :], ident[0:S, 0:S], pool_w[:, bass.ds(nb, 1)], None, ALU.mult) \
                    .then_inc(diag_done, 1)

            def mean_row(nb, q):
                dve.wait_ge(eb_done, nb + 1)
                dve.tensor_tensor(scaled[:, :, :], fT[:, nb, 0:KC, :], bank[2][:, 0:S].rearrange("p (o s) -> p o s", o=1)
                                  .to_broadcast([P, KC, S]), ALU.mult).then_inc(scaled_done, 1)
                dve.wait_ge(scaled_done, nb + 1)
                dve.tensor_reduce(hcb[q][:, :], scaled[:, :, :], axis=AX.X, op=ALU.add).then_inc(hcb_done, 1)

            def product(nb):
                dve.wait_ge(fh_highhalf, nb)
                dve.wait_ge(fl_highhalf, nb)
                dve.tensor_tensor(prod[:, :, :], fT[:, nb, 0:KC, :], fT[:, nb, KC:2 * KC, :], ALU.mult) \
                    .then_inc(prod_done, 1)

            def low_features(nb, q):
                dve.wait_ge(fh_lowhalf, nb + 1)
                dve.tensor_tensor(fl[q][:, 0:2 * KC, :], fT[:, nb, :, :], fh[q][:, 0:2 * KC, :].bitcast(F32),
                                  ALU.subtract).then_inc(fl_lowhalf, 1)
                dve.wait_ge(fh_highhalf, nb + 1)
                dve.tensor_tensor(fl[q][:, 2 * KC:NF, :], prod[:, :, :], fh[q][:, 2 * KC:NF, :].bitcast(F32),
                                  ALU.subtract).then_inc(fl_highhalf, 1)

            diag_of(0)
            mean_row(0, 0)
            dve.wait_ge(hq_sb, B)
            product(0)
            diag_of(1)
            low_features(0, 0)
            dve.wait_ge(bqv_loaded, 16)
            dve.wait_ge(gate_done, 1)

            def next_hs(t):
                if not (isinstance(t, int) and t == 0):
                    dve.wait_ge(hsT_ps, t)
                normalise(hs[:, :], t, hs_ready)
                dve.wait_ge(hs_ready, t + 1)
                dve.scalar_tensor_tensor(x_all[:, t, :], hs[:, :], tg[0:S, 1:2], x_all[:, t, :], ALU.mult, ALU.add) \
                    .then_inc(base_done, 1)

            def residual(b, p):
                dve.wait_ge(y_done, b + 1)
                dve.tensor_tensor(y_b[:, :], bank[p][0:S, :], b_qv_b[:, :], ALU.add).then_inc(y_biased, 1)
                dve.wait_ge(y_biased, b + 1)
                dve.scalar_tensor_tensor(x_all[:, b, :], y_b[:, :], tg[0:S, 0:1], x_all[:, b, :], ALU.mult, ALU.add) \
                    .then_inc(x1_done, 1)
                apart(dve, pool_const)
                dve.wait_ge(x1_done, b + 1)
                dve.bn_stats(stats[:, b, :], x_all[:, b, :]).then_inc(stats2_done, 1)

            def project(b, p):
                if not (isinstance(b, int) and b == B - 1):
                    product(b + 1)
                    mean_row(b + 1, 1 - p)
                for c in range(KC):
                    dve.wait_ge(Weh_done, KC * b + c + 1)
                    dve.tensor_tensor(Wel[:, c, :], We[:, c, :], Weh[:, c, :].bitcast(F32), ALU.subtract) \
                        .then_inc(Wel_done, 1)
                if not (isinstance(b, int) and b == B - 1):
                    low_features(b + 1, 1 - p)
                if not (isinstance(b, int) and b >= B - 2):
                    diag_of(b + 2)
                if not (isinstance(b, int) and b == 0):
                    residual(b - 1, 1 - p)
                if isinstance(b, int) and b == B - 2:
                    dve.wait_ge(stats2_done, B // 2)
                    row_stats(0, B // 2)

            over_batches(dve, project)
            dve.wait_ge(y_done, B)
            dve.wait_ge(rstd_done, 3)
            next_hs(0)
            residual(B - 1, 1)
            dve.wait_ge(stats2_done, B)
            dve.wait_ge(consts_loaded, N_CONSTS * 16)
            row_stats(B // 2, B)
            for i in range(2):
                ins = dve.memset(V[i][:, :, KPH:KPH + 1], 1.0)
            ins.then_inc(dve_step, 1)
            n += 1
            dve.wait_ge(attb_loaded, 32)
            dve.wait_ge(rstd_done, 4)

            def softmax_shift(t, u):
                view = [bank[2 * u + i][0:S, 0:4 * S].rearrange("s (h n) -> s h n", h=4) for i in range(2)]
                dve.wait_ge(sc_ps, 2 * t + u + 1)
                for i in range(2):
                    ins = dve.tensor_reduce(smax[u][:, 4 * i:4 * i + 4], view[i], axis=AX.X, op=ALU.max)
                ins.then_inc(smax_done, 1)
                dve.wait_ge(smax_done, 2 * t + u + 1)
                if not (isinstance(t, int) and t == 0):
                    dve.wait_ge(attT_ps, 2 * t - 1 + u)
                for i in range(2):
                    ins = dve.tensor_tensor(att[u][:, 4 * i:4 * i + 4, :], view[i],
                                            smax[u][:, 4 * i:4 * i + 4].rearrange("s (h o) -> s h o", o=1)
                                            .to_broadcast([S, 4, S]), ALU.subtract)
                ins.then_inc(sub_done, 1)

            def attend(t, p, do):
                if do.route:
                    dve.wait_ge(mla_ps, t - 1)
                    if not (isinstance(t, int) and t < 4):
                        dve.wait_ge(scattered[p], TOP * 16 * (t - 2 - p))
                    dve.tensor_tensor(mla[p][:, :], bank[0][0:S, :], o_b_b[:, :], ALU.add).then_inc(mla_sb, 1)
                if do.place:
                    dve.wait_ge(rank_ps, t - 2)
                    dve.tensor_copy(rank_sb[:, :], rank_bank).then_inc(rank_read, 1)
                    places(t - 3, 1 - p)
                if do.ahead:
                    next_hs(t + 1)
                if do.cur:
                    dve.wait_ge(qk_ps, t + 1)
                    for g in range(NB):
                        ins = dve.tensor_scalar(qT[:, g, :], bank[4][:, g * S:(g + 1) * S], qbT[:, g:g + 1], None,
                                                ALU.add)
                    ins.then_inc(q_sb, 1)
                    for g in range(NB):
                        dve.scalar_tensor_tensor(KTm[:, g, :, :],
                                                 bank[4][:, (NB + g) * S:(NB + g + 1) * S]
                                                 .rearrange("p (o s) -> p o s", o=1)
                                                 .to_broadcast([P, HB, S]), kbT[:, g:g + 1],
                                                 head_mask[:, :].rearrange("p (h o) -> p h o", o=1)
                                                 .to_broadcast([P, HB, S]), ALU.add, ALU.mult).then_inc(k_sb, 1)
                    dve.wait_ge(v_ps, t + 1)
                    dve.tensor_tensor(V[p][:, :, 0:KPH], bank[2][0:S, 0:LAT].rearrange("s (h k) -> s h k", h=H),
                                      v_b_b[:, :].rearrange("s (h k) -> s h k", h=H), ALU.add).then_inc(v_sb, 1)
                if do.route:
                    dve.wait_ge(lg_ps, t - 1)
                    dve.tensor_tensor(logit[:, :], logit_bank, router_bb[:, :], ALU.add).then_inc(lg_sb, 1)
                    route(t - 2)
                if do.cur:
                    softmax_shift(t, 0)
                if do.prev:
                    o = ao_bank.rearrange("s (h k) -> s h k", h=H)
                    dve.wait_ge(av_ps, t)
                    dve.reciprocal(den[:, :], o[:, :, KPH]).then_inc(den_done, 1)
                    dve.wait_ge(den_done, t)
                    dve.tensor_tensor(ao[:, :, :], o[:, :, 0:KPH], den[:, :].rearrange("s (h o) -> s h o", o=1)
                                      .to_broadcast([S, H, KPH]), ALU.mult).then_inc(ao_sb, 1)
                if do.cur:
                    softmax_shift(t, 1)

            def route(b):
                dve.wait_ge(lg_sb, b + 1)
                dve.tensor_reduce(neg_top[:, :], logit[:, :], axis=AX.X, op=ALU.max, negate=True) \
                    .then_inc(neg_top_done, 1)
                dve.wait_ge(router_exp, b + 1)
                dve.reciprocal(einv[:, :], esum[:, :]).then_inc(einv_done, 1)
                dve.wait_ge(einv_done, b + 1)
                dve.tensor_scalar(probs[:, :], rp[:, :], einv[:, :], None, ALU.mult).then_inc(probs_done, 1)
                apart(dve, pool_const)
                dve.wait_ge(probs_done, b + 1)
                dve.max(top_p[:, :], probs[:, :]).then_inc(top_done, 1)
                apart(dve, pool_const)
                dve.wait_ge(top_done, b + 1)
                dve.max_index(top_i[:, :], top_p[:, :], probs[:, :]).then_inc(index_done, 1)
                dve.tensor_tensor(wsum[:, :], top_p[:, 0:1], top_p[:, 1:2], ALU.add).then_inc(wsum_done, 1)
                dve.wait_ge(index_done, b + 1)
                dve.tensor_copy(top_f[:, :], top_i[:, :]).then_inc(index_f, 1)
                dve.wait_ge(wsum_done, b + 1)
                dve.tensor_scalar(wsum2[:, :], wsum[:, :], 1e-8, None, ALU.add).then_inc(wsum2_done, 1)
                dve.wait_ge(index_f, b + 1)
                for k in range(TOP):
                    ins = dve.tensor_scalar(onehot[:, bass.ds(b, 1), k, :].rearrange("s o e -> s (o e)"),
                                            iota_e[0:S, :], top_f[:, k:k + 1], None, ALU.is_equal)
                ins.then_inc(onehot_done, 1)
                dve.wait_ge(wsum2_done, b + 1)
                dve.reciprocal(winv[:, :], wsum2[:, :]).then_inc(winv_done, 1)
                dve.wait_ge(onehot_done, b + 1)
                dve.tensor_tensor(chosen[:, :], onehot[:, bass.ds(b, 1), 0, :].rearrange("s o e -> s (o e)"),
                                  onehot[:, bass.ds(b, 1), 1, :].rearrange("s o e -> s (o e)"), ALU.add) \
                    .then_inc(chosen_done, 1)
                dve.wait_ge(winv_done, b + 1)
                dve.tensor_scalar(winv2[:, :], winv[:, :], tg_moe[0:S, :], None, ALU.mult).then_inc(winv2_done, 1)
                dve.wait_ge(winv2_done, b + 1)
                dve.tensor_scalar(weight[:, bass.ds(b, 1), :].rearrange("s o k -> s (o k)"), top_p[:, 0:TOP],
                                  winv2[:, :], None, ALU.mult).then_inc(weight_done, 1)

            def places(b, p):
                dve.wait_ge(rank_read, b + 1)
                dve.tensor_tensor(row_of[:, :], rank_sb[:, 0:E], run[0:S, :], ALU.add).then_inc(row_done, 1)
                dve.wait_ge(row_done, b + 1)
                dve.tensor_tensor(row_of[:, :], row_of[:, :], list_row[0:S, :], ALU.add).then_inc(row2_done, 1)
                dve.tensor_tensor(run[0:S, :], run[0:S, :], rank_sb[:, E:2 * E], ALU.add).then_inc(run_done, 1)
                dve.wait_ge(row2_done, b + 1)
                dve.tensor_tensor(picked[:, :, :], onehot[:, bass.ds(b, 1), :, :].rearrange("s o k e -> s (o k) e"),
                                  row_of[:, :].rearrange("s (o e) -> s o e", o=1).to_broadcast([S, TOP, E]),
                                  ALU.mult).then_inc(picked_done, 1)
                apart(dve, pool_const)
                dve.wait_ge(picked_done, b + 1)
                dve.tensor_reduce(x_row[:, bass.ds(b, 1), :].rearrange("s o k -> s (o k)"), picked[:, :, :],
                                  axis=AX.X, op=ALU.add).then_inc(x_row_done, 1)
                apart(dve, pool_const)
                dve.wait_ge(x_row_done, b + 1)
                for k in range(TOP):
                    dve.tensor_copy(x_row_i[TOP * p + k][:, :], x_row[:, bass.ds(b, 1), k]).then_inc(x_index_done, 1)
                apart(dve, pool_const)
                dve.wait_ge(weight_done, b + 1)
                dve.tensor_copy(item[p][:, :, 0], weight[:, bass.ds(b, 1), :].rearrange("s o k -> s (o k)"))
                dve.tensor_copy(item[p][:, :, 1], out_row[:, bass.ds(b, 1)].to_broadcast([S, TOP])).then_inc(item_done, 1)

            dve.tensor_scalar(tg_moe[:, :], tg[:, 1:2], 0.3, None, ALU.mult).then_inc(dve_step, 1)
            n += 1
            dve.wait_ge(dve_step, n)
            over_attend_steps(dve, attend)

            def per(a, shape):
                return a.rearrange("p (e o) -> p e o", o=1).to_broadcast(shape)

            def each(a, shape):
                return a.rearrange("p (o e) -> p o e", o=1).to_broadcast(shape)

            tiles_of, start, stop = plan
            own(dve.tensor_tensor(plan_c[0:S, :, :], per(run[0:S, :], [S, E, NTE]), each(tile_row[0:S, :], [S, E, NTE]),
                                  ALU.is_gt))
            own(dve.tensor_reduce(tiles_of[0:S, :], plan_c[0:S, :, :], axis=AX.X, op=ALU.add))
            own(dve.tensor_tensor(plan_s[0:S, :, :], before_e[0:S, :, :], each(tiles_of[0:S, :], [S, E, E]), ALU.mult))
            own(dve.tensor_reduce(start[0:S, :], plan_s[0:S, :, :], axis=AX.X, op=ALU.add))
            own(dve.tensor_tensor(stop[0:S, :], start[0:S, :], tiles_of[0:S, :], ALU.add))
            tile_expert, tile_first, live, from_list, tile_rows = plan_n
            own(dve.tensor_tensor(plan_t[0:S, :, :], per(tile_no[0:S, :], [S, NT, E]), each(stop[0:S, :], [S, NT, E]),
                                  ALU.is_ge))
            own(dve.tensor_reduce(tile_expert[0:S, :], plan_t[0:S, :, :], axis=AX.X, op=ALU.add))
            own(dve.tensor_tensor(plan_t[0:S, :, :], plan_t[0:S, :, :], each(tiles_of[0:S, :], [S, NT, E]), ALU.mult))
            own(dve.tensor_reduce(tile_first[0:S, :], plan_t[0:S, :, :], axis=AX.X, op=ALU.add))
            own(dve.tensor_scalar(live[0:S, :], tile_expert[0:S, :], float(E) - 0.5, None, ALU.is_lt))
            own(dve.tensor_tensor(tile_expert[0:S, :], tile_expert[0:S, :], live[0:S, :], ALU.mult))
            own(dve.tensor_tensor(tile_rows[0:S, :], tile_no[0:S, :], tile_first[0:S, :], ALU.subtract))
            own(dve.tensor_tensor(tile_rows[0:S, :], tile_rows[0:S, :], live[0:S, :], ALU.mult))
            own(dve.tensor_scalar(tile_rows[0:S, :], tile_rows[0:S, :], float(TR), None, ALU.mult))
            own(dve.tensor_scalar(from_list[0:S, :], tile_expert[0:S, :], float(LIST), None, ALU.mult))
            own(dve.tensor_tensor(tile_rows[0:S, :], tile_rows[0:S, :], from_list[0:S, :], ALU.add))
            own(dve.tensor_scalar(from_list[0:S, :], live[0:S, :], -float(B * S), float(B * S), ALU.mult, ALU.add))
            own(dve.tensor_tensor(tile_rows[0:S, :], tile_rows[0:S, :], from_list[0:S, :], ALU.add))
            dve.tensor_copy(plan_i[0:1, 0:NT], tile_expert[0:1, :])
            dve.tensor_copy(plan_i[0:1, NT:2 * NT], tile_rows[0:1, :]).then_inc(plan_done, 1)
            dve.sem_inc(h1l_done, 2)
            for i in range(2):
                dve.wait_ge(scattered[i], TOP * B * 16)
            dve.sem_inc(w2l_done, 1)
            dve.sem_inc(y_sb, 2)
            dve.sem_inc(y_weighted, 2)

            def low_w1(t, n):
                i = W1_ORDER[n]
                dve.wait_ge(w1h_done, t * FC + n + 1)
                part = (i // 2, slice((i % 2) * D, (i % 2 + 1) * D))
                dve.tensor_tensor(w1l[:, part[0], part[1]], raw1[:, i, :], w1h[:, part[0], part[1]].bitcast(F32),
                                  ALU.subtract).then_inc(w1l_done, 1)

            def low_rows(t, p):
                for w in range(TW):
                    cols = slice(w * P, (w + 1) * P)
                    dve.wait_ge(mTh_done, TW * t + w + 1)
                    dve.tensor_tensor(mTl[p][:, :, cols], bank[2 + w][:, :].rearrange("p (c n) -> p c n", c=KC),
                                      mTh[p][:, :, cols].bitcast(F32), ALU.subtract).then_inc(mTl_done, 1)

            def rows_of_sum(t, p):
                dve.wait_ge(items_loaded[p], (t - p) * 8 + 16)
                dve.tensor_tensor(row_f[:, :], item_t[p][:, :, 1], pad_row[:, :].to_broadcast([P, TW]), ALU.max) \
                    .then_inc(row_max_done, 1)
                dve.wait_ge(row_max_done, t + 1)
                dve.tensor_copy(row_i[p][:, :, :].rearrange("p w o -> p (w o)"), row_f[:, :]).then_inc(row_ready, 1)

            def output(t, p, w):
                dve.wait_ge(o_ps, TW * t + w + 2)
                dve.wait_ge(bias_loaded[p], (t - p) * 16 + 32)
                if not (isinstance(t, int) and t == 0):
                    dve.wait_ge(added[w], t * 16)
                dve.tensor_tensor(y_t[w][:, :], bank[4 + w][:, :], b2_t[p][:, :], ALU.add).then_inc(y_sb, 1)
                dve.wait_ge(row_ready, t + 1)
                dve.wait_ge(y_sb, TW * t + w + 3)
                dve.tensor_scalar(y_t[w][:, :], y_t[w][:, :], item_t[p][:, w, 0:1], None, ALU.mult) \
                    .then_inc(y_weighted, 1)

            low_rows(0, 0)
            for i in range(FC):
                low_w1(0, i)

            def tile(t, p, more):
                for f in range(FC):
                    dve.wait_ge(w2h_done, t * FC + f + 1)
                    dve.tensor_tensor(w2l[:, f, :], raw2[:, f, :], w2h[:, f, :].bitcast(F32), ALU.subtract) \
                        .then_inc(w2l_done, 1)
                    dve.wait_ge(gelu_done, t * FC + f + 3)
                    dve.tensor_copy(h1h[:, f, :], h1f[f % 2][:, :]).then_inc(h1h_done, 1)
                    dve.wait_ge(h1h_done, t * FC + f + 1)
                    dve.tensor_tensor(h1l[:, f, :], h1f[f % 2][:, :], h1h[:, f, :].bitcast(F32), ALU.subtract) \
                        .then_inc(h1l_done, 1)
                if more:
                    low_rows(t + 1, 1 - p)
                rows_of_sum(t, p)
                for w in range(TW):
                    if more:
                        for i in range(w * FC // TW, (w + 1) * FC // TW):
                            low_w1(t + 1, i)
                    output(t, p, w)

            over_tiles(dve, tile)


_FFN = ["q_w", "q_b", "k_w", "k_b", "v_w", "v_b", "o_w", "o_b", "router_w", "router_b", "w1", "b1", "w2", "b2"]
_INS = ["x", "ctx_1024", "g_xattn", "g_ffn"] + ["L0_xattn_" + n for n in ("w_sim", "b_sim", "W_qv", "b_qv")] \
    + ["L0_ffn_" + n for n in _FFN]
_OUTS = [((B, S, D), "float32")]


def kernel(**inputs):
    import numpy as _np
    import concourse.bacc as _bacc
    from concourse import mybir as _mybir
    from concourse.bass_utils import run_bass_kernel_spmd as _run

    nc = _bacc.Bacc("TRN2", target_bir_lowering=False, num_devices=1)
    arrays, args = {}, []
    for name in _INS:
        a = _np.ascontiguousarray(inputs[name])
        arrays[f"in_{name}_dram"] = a
        args.append(nc.dram_tensor(f"in_{name}_dram", a.shape, _mybir.dt.from_np(a.dtype), kind="ExternalInput").ap())
    for i, (shape, dtype) in enumerate(_OUTS):
        dt = _mybir.dt.from_np(_np.dtype(dtype))
        args.append(nc.dram_tensor(f"out_{i}_dram", shape, dt, kind="ExternalOutput").ap())
    build(nc, *args)
    r = _run(nc, [arrays], core_ids=[0])
    return r.results[0]["out_0_dram"]
```
